# Optimizing a Trainium2 kernel written in Bass

```python
import numpy as np
import jax
import jax.numpy as jnp

def _softmax(x, axis=-1):
    return jax.nn.softmax(x, axis=axis)

def _gelu(x):
    return jax.nn.gelu(x, approximate=True)

def _silu(x):
    return jax.nn.silu(x)

def _sigmoid(x):
    return jax.nn.sigmoid(x)

def _layernorm(x, axis=-1, eps=1e-05):
    m = jnp.mean(x, axis=axis, keepdims=True)
    v = jnp.var(x, axis=axis, keepdims=True)
    return (x - m) / jnp.sqrt(v + eps)

def _scatter_add(tgt, idx, src, axis=0):
    return tgt.at[idx].add(src)

def _segment_sum(src, seg, n):
    return jax.ops.segment_sum(src, seg, n)
kernel_name = 'mk_gnn_resnorm_d4_gnn_r32_df67eb'

def setup_inputs(seed: int=0):
    np.random.seed(seed)
    _w = jnp.asarray

    def _rec_inputs():
        import jax
        import jax.numpy as jnp
        _gk = jax.random.key(seed)
        x = -0.0003713 + 1 * jax.random.normal(jax.random.fold_in(_gk, 1), (3125, 256), jnp.float32)
        src = jax.random.randint(jax.random.fold_in(_gk, 2), (50000,), 0, 3125, jnp.int32)
        dst = jax.random.randint(jax.random.fold_in(_gk, 3), (50000,), 0, 3125, jnp.int32)
        _o = jnp.argsort(dst, stable=True)
        src = src[_o]
        dst = dst[_o]
        return (x, src, dst)
    x, src, dst = _rec_inputs()

    def _L0_gnn_setup():
        import jax, jax.numpy as jnp
        import numpy as np
        N_NODES = 50000
        N_EDGES = 25000
        D_IN = 256
        D_OUT = 256
        key = jax.random.key(seed)
        k1, k2, k3 = jax.random.split(key, 3)
        x = jax.random.normal(k1, (N_NODES, D_IN), dtype=jnp.float32)
        edge_index = jax.random.randint(k2, (2, N_EDGES), 0, N_NODES, dtype=jnp.int64)
        W = jax.random.normal(k3, (D_IN, D_OUT), dtype=jnp.float32) * (1.0 / np.sqrt(D_IN))
        b = jnp.zeros((D_OUT,), dtype=jnp.float32)
        return {'x': x, 'edge_index': edge_index, 'W': W, 'b': b}
    _L0_gnn_all = _L0_gnn_setup()
    _L0_gnn_in = {k: v for k, v in _L0_gnn_all.items() if k in ('W', 'b')}
    del _L0_gnn_all

    def _L1_gnn_setup():
        import jax, jax.numpy as jnp
        import numpy as np
        N = 50000
        E = 25000
        F = 256
        H = 4
        D = 64
        key = jax.random.key(seed)
        ks = jax.random.split(key, 10)
        s = 0.02
        HD = H * D
        return {'feat': jax.random.normal(ks[0], (N, F), jnp.float32), 'src': jax.random.randint(ks[1], (E,), 0, N), 'dst': jax.random.randint(ks[2], (E,), 0, N), 'Wq': jax.random.normal(ks[3], (HD, F), jnp.float32) * s, 'bq': jnp.zeros((HD,), jnp.float32), 'Wk': jax.random.normal(ks[4], (HD, F), jnp.float32) * s, 'bk': jnp.zeros((HD,), jnp.float32), 'Wv': jax.random.normal(ks[5], (HD, F), jnp.float32) * s, 'bv': jnp.zeros((HD,), jnp.float32), 'Wskip': jax.random.normal(ks[6], (HD, F), jnp.float32) * s, 'bskip': jnp.zeros((HD,), jnp.float32), 'Wgate': jax.random.normal(ks[7], (1, 3 * HD), jnp.float32) * s, 'bgate': jnp.zeros((1,), jnp.float32), 'ln_w': jnp.ones((HD,), jnp.float32), 'ln_b': jnp.zeros((HD,), jnp.float32), 'prelu_a': jnp.float32(0.25)}
    _L1_gnn_all = _L1_gnn_setup()
    _L1_gnn_in = {k: v for k, v in _L1_gnn_all.items() if k in ('Wq', 'bq', 'Wk', 'bk', 'Wv', 'bv', 'Wskip', 'bskip', 'Wgate', 'bgate', 'ln_w', 'ln_b', 'prelu_a')}
    del _L1_gnn_all

    def _L2_gnn_setup():
        import jax, jax.numpy as jnp
        import numpy as np
        N, IN_CH, HEADS, OUT_CH, E = (50000, 256, 4, 64, 25000)
        key = jax.random.key(seed)
        k1, k2, k3, k4, k5 = jax.random.split(key, 5)
        x = jax.random.normal(k1, (N, IN_CH), dtype=jnp.float32)
        edge_index = jax.random.randint(k2, (2, E), 0, N, dtype=jnp.int64)
        bw = float(np.sqrt(6.0 / (IN_CH + HEADS * OUT_CH)))
        ba = float(np.sqrt(6.0 / (HEADS + OUT_CH)))
        weight = jax.random.uniform(k3, (IN_CH, HEADS * OUT_CH), jnp.float32, -bw, bw)
        attn_l = jax.random.uniform(k4, (HEADS, OUT_CH), jnp.float32, -ba, ba)
        attn_r = jax.random.uniform(k5, (HEADS, OUT_CH), jnp.float32, -ba, ba)
        return {'x': x, 'edge_index': edge_index, 'weight': weight, 'attn_l': attn_l, 'attn_r': attn_r}
    _L2_gnn_all = _L2_gnn_setup()
    _L2_gnn_in = {k: v for k, v in _L2_gnn_all.items() if k in ('weight', 'attn_l', 'attn_r')}
    del _L2_gnn_all

    def _L3_gnn_setup():
        import jax, jax.numpy as jnp
        import numpy as np
        N, E, D_IN, D_OUT = (50000, 50000, 256, 256)
        key = jax.random.key(seed)
        k1, k2, k3, k4, k5, k6 = jax.random.split(key, 6)
        x = jax.random.normal(k1, (N, D_IN), dtype=jnp.float32)
        edge_index = jax.random.randint(k2, (2, E), 0, N, dtype=jnp.int64)
        s = 1.0 / np.sqrt(D_IN)
        W1 = jax.random.uniform(k3, (D_OUT, D_IN), minval=-s, maxval=s, dtype=jnp.float32)
        b1 = jax.random.uniform(k4, (D_OUT,), minval=-s, maxval=s, dtype=jnp.float32)
        W2 = jax.random.uniform(k5, (D_OUT, D_IN), minval=-s, maxval=s, dtype=jnp.float32)
        b2 = jax.random.uniform(k6, (D_OUT,), minval=-s, maxval=s, dtype=jnp.float32)
        return {'x': x, 'W1': W1, 'b1': b1, 'W2': W2, 'b2': b2, 'edge_index': edge_index}
    _L3_gnn_all = _L3_gnn_setup()
    _L3_gnn_in = {k: v for k, v in _L3_gnn_all.items() if k in ('W1', 'b1', 'W2', 'b2')}
    del _L3_gnn_all
    return {'x': x, 'src': src, 'dst': dst, 'L0_gnn_W': _L0_gnn_in['W'], 'L0_gnn_b': _L0_gnn_in['b'], 'L1_gnn_Wq': _L1_gnn_in['Wq'], 'L1_gnn_bq': _L1_gnn_in['bq'], 'L1_gnn_Wk': _L1_gnn_in['Wk'], 'L1_gnn_bk': _L1_gnn_in['bk'], 'L1_gnn_Wv': _L1_gnn_in['Wv'], 'L1_gnn_bv': _L1_gnn_in['bv'], 'L1_gnn_Wskip': _L1_gnn_in['Wskip'], 'L1_gnn_bskip': _L1_gnn_in['bskip'], 'L1_gnn_Wgate': _L1_gnn_in['Wgate'], 'L1_gnn_bgate': _L1_gnn_in['bgate'], 'L1_gnn_ln_w': _L1_gnn_in['ln_w'], 'L1_gnn_ln_b': _L1_gnn_in['ln_b'], 'L1_gnn_prelu_a': _L1_gnn_in['prelu_a'], 'L2_gnn_weight': _L2_gnn_in['weight'], 'L2_gnn_attn_l': _L2_gnn_in['attn_l'], 'L2_gnn_attn_r': _L2_gnn_in['attn_r'], 'L3_gnn_W1': _L3_gnn_in['W1'], 'L3_gnn_b1': _L3_gnn_in['b1'], 'L3_gnn_W2': _L3_gnn_in['W2'], 'L3_gnn_b2': _L3_gnn_in['b2']}

def reference(x, src, dst, L0_gnn_W, L0_gnn_b, L1_gnn_Wq, L1_gnn_bq, L1_gnn_Wk, L1_gnn_bk, L1_gnn_Wv, L1_gnn_bv, L1_gnn_Wskip, L1_gnn_bskip, L1_gnn_Wgate, L1_gnn_bgate, L1_gnn_ln_w, L1_gnn_ln_b, L1_gnn_prelu_a, L2_gnn_weight, L2_gnn_attn_l, L2_gnn_attn_r, L3_gnn_W1, L3_gnn_b1, L3_gnn_W2, L3_gnn_b2):
    import jax
    import jax.numpy as jnp

    def _L0_gnn_ref(x, edge_index, W, b):
        import jax, jax.numpy as jnp
        import numpy as np
        N_NODES = 50000
        N_EDGES = 25000
        D_IN = 256
        D_OUT = 256
        N = x.shape[0]
        loops = jnp.arange(N, dtype=edge_index.dtype)
        src = jnp.concatenate([edge_index[0], loops])
        dst = jnp.concatenate([edge_index[1], loops])
        deg = jax.ops.segment_sum(jnp.ones_like(dst, dtype=x.dtype), dst, num_segments=N)
        dinv = jax.lax.rsqrt(deg)
        norm = dinv[src] * dinv[dst]
        xw = jnp.matmul(x, W)
        msg = xw[src] * norm[:, None]
        agg = jax.ops.segment_sum(msg, dst, num_segments=N)
        return jax.nn.relu(agg + b)

    def _L1_gnn_ref(feat, src, dst, Wq, bq, Wk, bk, Wv, bv, Wskip, bskip, Wgate, bgate, ln_w, ln_b, prelu_a):
        import jax, jax.numpy as jnp
        import numpy as np
        N = 50000
        E = 25000
        F = 256
        H = 4
        D = 64
        n = feat.shape[0]
        scale = 1.0 / np.sqrt(D).astype(np.float32)
        q = (feat @ Wq.T + bq).reshape(n, H, D)
        k = (feat @ Wk.T + bk).reshape(n, H, D)
        v = (feat @ Wv.T + bv).reshape(n, H, D)
        e = jnp.einsum('ehd,ehd->eh', q[src], k[dst]) * scale
        m = jax.ops.segment_max(e, dst, num_segments=n)
        ex = jnp.exp(e - m[dst])
        denom = jax.ops.segment_sum(ex, dst, num_segments=n)
        sa = ex / denom[dst]
        agg = jax.ops.segment_sum(sa[:, :, None] * v[src], dst, num_segments=n)
        rst = agg.reshape(n, H * D)
        skip = feat @ Wskip.T + bskip
        g = jax.nn.sigmoid(jnp.concatenate([skip, rst, skip - rst], axis=-1) @ Wgate.T + bgate)
        rst = g * skip + (1.0 - g) * rst
        mu = rst.mean(-1, keepdims=True)
        var = rst.var(-1, keepdims=True)
        rst = (rst - mu) * jax.lax.rsqrt(var + 1e-05) * ln_w + ln_b
        return jnp.where(rst >= 0, rst, prelu_a * rst)

    def _L2_gnn_ref(x, edge_index, weight, attn_l, attn_r):
        import jax, jax.numpy as jnp
        import numpy as np
        N, IN_CH, HEADS, OUT_CH, E = (50000, 256, 4, 64, 25000)
        heads, out_ch = attn_l.shape
        n = x.shape[0]
        xt = jnp.matmul(x, weight).reshape(-1, heads, out_ch)
        row, col = (edge_index[0], edge_index[1])
        alpha_l = jnp.einsum('ehd,hd->eh', xt[row], attn_l)
        alpha_r = jnp.einsum('ehd,hd->eh', xt[col], attn_r)
        alpha = jax.nn.softmax(jax.nn.leaky_relu(alpha_l + alpha_r, 0.01), axis=1)
        tmp = jnp.einsum('nh,nhd->nd', alpha[:n], xt[col[:n]])
        out = jnp.broadcast_to(tmp[:, None, :], (n, heads, out_ch))
        return out.reshape(n, heads * out_ch)

    def _L3_gnn_ref(x, W1, b1, W2, b2, edge_index):
        import jax, jax.numpy as jnp
        import numpy as np
        N, E, D_IN, D_OUT = (50000, 50000, 256, 256)
        dst = edge_index[0]
        nbr = edge_index[1]
        n = x.shape[0]
        agg = jax.ops.segment_sum(x[nbr], dst, num_segments=n)
        cnt = jax.ops.segment_sum(jnp.ones((nbr.shape[0],), x.dtype), dst, num_segments=n)
        mean = agg / jnp.maximum(cnt, 1.0)[:, None]
        return x @ W1.T + b1 + mean @ W2.T + b2
    edge_index = jnp.stack([src, dst])
    x = _layernorm(x + _L0_gnn_ref(x, edge_index, L0_gnn_W, L0_gnn_b), axis=-1)
    x = _layernorm(x + _L1_gnn_ref(x, src, dst, L1_gnn_Wq, L1_gnn_bq, L1_gnn_Wk, L1_gnn_bk, L1_gnn_Wv, L1_gnn_bv, L1_gnn_Wskip, L1_gnn_bskip, L1_gnn_Wgate, L1_gnn_bgate, L1_gnn_ln_w, L1_gnn_ln_b, L1_gnn_prelu_a), axis=-1)
    x = _layernorm(x + _L2_gnn_ref(x, edge_index, L2_gnn_weight, L2_gnn_attn_l, L2_gnn_attn_r), axis=-1)
    x = _layernorm(x + _L3_gnn_ref(x, L3_gnn_W1, L3_gnn_b1, L3_gnn_W2, L3_gnn_b2, edge_index), axis=-1)
    return x

_drawn_inputs = setup_inputs


def setup_inputs(seed=0):
    import zlib

    import numpy as np

    out = dict(_drawn_inputs(seed))
    spreads = {'L0_gnn_b': (0.0, 0.1),
     'L1_gnn_bq': (0.0, 0.8),
     'L1_gnn_bk': (0.0, 0.8),
     'L1_gnn_bv': (0.0, 0.1),
     'L1_gnn_bskip': (0.0, 0.1),
     'L1_gnn_ln_w': (1.0, 0.2),
     'L1_gnn_ln_b': (0.0, 0.1)}
    factors = {'L1_gnn_Wq': 3.071, 'L1_gnn_Wk': 3.263}
    for name, (base, spread) in spreads.items():
        noise = np.random.default_rng([zlib.crc32(name.encode()), seed]).standard_normal(out[name].shape)
        drawn = base * np.exp(spread * noise) if base else spread * noise
        out[name] = jnp.asarray(drawn.astype(out[name].dtype))
    for name, factor in factors.items():
        out[name] = (out[name] * factor).astype(out[name].dtype)
    return out
```

```python
from contextlib import ExitStack

import concourse.bass as bass
from concourse import mybir

F32 = mybir.dt.float32
I32 = mybir.dt.int32
ALU = mybir.AluOpType
ACT = mybir.ActivationFunctionType
X_AXIS = mybir.AxisListType.X

P = 128
N = 3125
E = 50000
D = 256
H = 4
HD = D // H
NT = 26
USED = -(-N // P)
TAIL = N - (USED - 1) * P
ROWS = 392
PAD_ROW = ROWS - 1
PAD_DST = 1 << 20
NW = 416
WG = 104
GRP = 8
RING = 2 * GRP
ITER = NW // RING
AW = D + 2 * H
BIG = 1.0e30
EPS = 1e-5
NPAIR = NT // 2
TABLES = 4
SW = D + 1


def gnn_kernel(nc, x, edges, w_all, w_l2, bias, attn, wgate, scalars, out):
    ctx = ExitStack()
    with ctx:
        def sb(name, shape, dt=F32):
            return ctx.enter_context(nc.sbuf_tensor(name, shape, dt))

        def sem(name):
            return ctx.enter_context(nc.semaphore(name))

        def table(name, width):
            return nc.dram_tensor(name, [NT * P, width], F32).ap()

        y0_table = table("y0_table", D)
        q_table = table("q_table", D)
        v_table = table("v_table", D)
        l2_table = table("l2_table", AW)
        al_table = table("al_table", H)
        sums = [nc.dram_tensor(f"sums{n}", [NT * P + P, SW], F32).ap() for n in range(TABLES)]
        src_rows = nc.dram_tensor("src_rows", [NW, P], F32).ap()

        feat = sb("feat", [P, NT, D])
        acc = [sb(f"acc{n}", [P, NT, AW]) for n in range(2)]
        aux = sb("aux", [P, NT, D])
        ring = sb("ring", [P, RING, SW])
        mask = sb("mask", [P, 2, GRP, P])
        maskT = sb("maskT", [P, GRP, P])
        ev = sb("ev", [P, GRP, D + H])
        w_sb = sb("w_sb", [P, 2, 7 * D])
        w2_sb = sb("w2_sb", [P, 2, AW])
        bias_bc = sb("bias_bc", [P, 9 * D])
        wgate_bc = sb("wgate_bc", [P, 3 * D])
        scal_bc = sb("scal_bc", [P, 2])
        stage = sb("stage", [P, 2, D])
        xT = sb("xT", [P, 2, 2, P])
        cnt = sb("cnt", [P, NT])
        ident = sb("ident", [P, P])
        ones = sb("ones", [P, P])
        iota_d = sb("iota_d", [P, P])
        wcol = sb("wcol", [WG, 4])
        cum = sb("cum", [P, NT])
        cum_i = sb("cum_i", [P, 2, NT], I32)
        first_row = sb("first_row", [P, NT])
        last_row = sb("last_row", [P, NT])
        items = sb("items", [P, NT])
        start = sb("start", [P, NT])
        off = sb("off", [P, NT])
        doff = sb("doff", [P, NT])
        ge = sb("ge", [WG, 4, USED - 1])
        geo = sb("geo", [WG, 4, USED - 1])
        tcol = sb("tcol", [WG, 4])
        t128 = sb("t128", [WG, 4])
        jcol = sb("jcol", [WG, 4])
        jcol2 = sb("jcol2", [WG, 4])
        jidx = sb("jidx", [WG, 4], I32)
        tile_i = sb("tile_i", [1, NW], I32)
        srcT = sb("srcT", [P, NW], I32)
        dstl = sb("dstl", [P, NW + GRP])
        idx_stage = sb("idx_stage", [P, 2, GRP], I32)
        l2_idx = sb("l2_idx", [P, 2, USED], I32)
        deg = sb("deg", [P, NT])
        dsq = sb("dsq", [P, NT])
        dinv = sb("dinv", [P, NT])
        rcnt = sb("rcnt", [P, NT])
        reset = sb("reset", [P, NW // 32, P])
        score = sb("score", [P, NW, H])
        mfull = sb("mfull", [P, NW, H])
        ex_in = sb("ex_in", [P, GRP, H])
        stats = sb("stats", [P, NT, 6])
        mv = sb("mv", [P, NT, 2])
        sd = sb("sd", [P, NT])
        rstd = sb("rstd", [P, NT])
        small = sb("small", [P, 4, NT])
        ral = sb("ral", [P, NT, H])
        alpha = sb("alpha", [P, NT, H])
        den4 = sb("den4", [P, NT, H])
        eps_col = sb("eps_col", [P, 1])
        small_idx = sb("small_idx", [P, 2, GRP])
        to_spare = small_idx[:, 0, :]
        to_spare2 = small_idx[:, 1, :]
        tile_row = sb("tile_row", [P, NW])
        spare_row = sb("spare_row", [P, 1])

        def within(tensor, at, shape, dt=F32):
            words = 1
            for n in shape[1:]:
                words *= n
            flat = tensor[:].rearrange("p t f -> p (t f)")[0:shape[0], at:at + words]
            flat = flat if dt == F32 else flat.bitcast(dt)
            names = "xyz"[:len(shape) - 1]
            sizes = dict(zip(names, shape[1:]))
            sizes.pop(names[0])
            return flat.rearrange(f"p ({' '.join(names)}) -> p {' '.join(names)}", **sizes) if len(names) > 1 else flat

        NB = NW // 32
        rows_i = within(acc[0], 0, [ROWS // 4, 4, 2 * P], I32)
        rows_f = within(acc[0], 1024, [WG, 4, 2 * P])
        work_i = within(acc[0], 2048, [WG, 4, 2 * P], I32)
        dst_f = within(acc[0], 3072, [ROWS // 4, 4, P])
        tile_w = within(acc[0], 3584, [P, 2, NW])
        iota_w = within(acc[0], 4416, [P, NW])
        degs = within(acc[0], 4832, [P, 2, NW])
        attn_bc = within(acc[1], 0, [P, 2, D])
        sel = within(acc[0], 0, [P, NW, H + 1])
        treset = within(acc[0], 2080, [P, 2, NW])
        cand = within(acc[0], 2912, [P, H, NW])
        mfwd = within(acc[0], 4576, [P, H, NW])
        turnedT = within(acc[1], 0, [P, NB, P])
        runT = within(acc[1], 1664, [P, NB, P])
        last = within(acc[1], 3328, [P, NB, P])
        key4 = within(acc[1], 4992, [P, NW, H])
        tmp64 = within(acc[0], 0, [P, NT, HD])
        prod = within(ev, 0, [P, 2, 2 * D])
        same = within(ev, 0, [P, GRP, P])
        earlier = within(ev, GRP * P, [P, GRP, P])
        src_row = within(w_sb, 0, [P, 2, GRP, P])
        srcf = within(w_sb, 2 * GRP * P, [P, NW + GRP])
        before_tri = within(w_sb, 2 * GRP * P + NW + GRP, [P, P])
        zeros = within(maskT, 0, [P, SW])
        ps = ctx.enter_context(nc.psum_tensor("ps", [P, 8, 512], F32))
        ps_flat = ps[:].rearrange("p b c -> p (b c)")

        in_edges, in_x, in_w, in_l2i = sem("in_edges"), sem("in_x"), sem("in_w"), sem("in_l2i")
        rows_got, l2_got, out_stored = sem("rows_got"), sem("l2_got"), sem("out_stored")
        y0_stored, qv_stored, l2_stored, rows_stored = (sem("y0_stored"), sem("qv_stored"),
                                                      sem("l2_stored"), sem("rows_stored"))
        zeros_ready, cleared = sem("zeros_ready"), sem("cleared")
        row_in = [sem(f"row_in{n}") for n in range(2)]
        summed_in = [sem(f"summed_in{n}") for n in range(TABLES)]
        read_back = [sem(f"read_back{n}") for n in range(2)]
        got = [sem(f"got{n}") for n in range(RING)]
        const_ready, x_tail, ones_ready = sem("const_ready"), sem("x_tail"), sem("ones_ready")
        cnt_ready, cum_ready, jidx_ready = sem("cnt_ready"), sem("cum_ready"), sem("jidx_ready")
        rowsf_ready, rowsT_ready, meta_ready = sem("rowsf_ready"), sem("rowsT_ready"), sem("meta_ready")
        deg_ready, deg_rooted = sem("deg_ready"), sem("deg_rooted")
        var_ready, rooted, feat_ready = sem("var_ready"), sem("rooted"), sem("feat_ready")
        logit_ready, gate_ready = sem("logit_ready"), sem("gate_ready")
        l2_logits, l2_exps = sem("l2_logits"), sem("l2_exps")
        y0_ready, qv_ready, ks_ready = sem("y0_ready"), sem("qv_ready"), sem("ks_ready")
        l2_ready, y3_ready, out_ready = sem("l2_ready"), sem("y3_ready"), sem("out_ready")
        keys_ready, last_ready, seg_ready, m_ready = (sem("keys_ready"), sem("last_ready"),
                                                      sem("seg_ready"), sem("m_ready"))
        sums_out = sem("sums_out")
        dve_seq = sem("dve_seq")
        pool_steps = sem("pool_steps")
        idx_staged = sem("idx_staged")
        staged = sem("staged")
        turned = sem("turned")
        xT_ready = sem("xT_ready")
        projected = sem("projected")
        evacuated = sem("evacuated")
        block_turned, block_out = sem("block_turned"), sem("block_out")
        DEG, AGG0, SCORE, SEG, ATT, SPREAD = range(6)
        mask_ready = [sem(f"mask_ready{n}") for n in range(6)]
        summed = {n: sem(f"summed{n}") for n in (DEG, AGG0, SEG, ATT)}
        added = {n: sem(f"added{n}") for n in (AGG0, ATT)}
        maskT_full = {n: sem(f"maskT_full{n}") for n in (SCORE, ATT, SPREAD)}
        maskT_ready = {n: sem(f"maskT_ready{n}") for n in (SCORE, ATT, SPREAD)}
        prod_ready = sem("prod_ready")
        k_ready, scored = sem("k_ready"), sem("scored")
        m_full, less_m, ex_ready, ev_ready = sem("m_full"), sem("less_m"), sem("ex_ready"), sem("ev_ready")

        same_made, idx_steps = sem("same_made"), sem("idx_steps")
        same_ready, dup_full, idx_ready = sem("same_ready"), sem("dup_full"), sem("idx_ready")
        row_full, row_out, group_in = sem("row_full"), sem("row_out"), sem("group_in")
        chunk_used, tri_ready, srcf_ready = sem("chunk_used"), sem("tri_ready"), sem("srcf_ready")

        XW, QV, K, SKIP, L2P, L3P = range(6)
        NGRP = NW // GRP
        GATHERS = [AGG0, SCORE, ATT]

        HALF = NT // 2

        def part(n):
            return acc[n // 2][:, (n % 2) * HALF:(n % 2 + 1) * HALF, :]

        block = ctx.enter_context(nc.Block())

        @block.sync
        def _(sp):
            sp.dma_start(rows_i, edges.rearrange("(p r) e -> p r e", r=4)).then_inc(in_edges, 16)
            sp.dma_start(feat[:, 0:USED - 1, :],
                         x[0:(USED - 1) * P, :].rearrange("(t p) f -> p t f", p=P)).then_inc(in_x, 16)
            sp.wait_ge(x_tail, 1)
            sp.dma_start(feat[0:TAIL, USED - 1, :], x[(USED - 1) * P:N, :]).then_inc(in_x, 16)
            sp.dma_start(w_sb[:], w_all.rearrange("(k p) n -> p k n", p=P)).then_inc(in_w, 16)
            sp.dma_start(w2_sb[:, :, 0:D], w_l2.rearrange("(k p) n -> p k n", p=P)).then_inc(in_w, 16)
            sp.dma_start(bias_bc[:], bias.partition_broadcast(P)).then_inc(in_w, 16)
            sp.dma_start(attn_bc.rearrange("p a b -> p (a b)"), attn.partition_broadcast(P)).then_inc(in_w, 16)
            sp.dma_start(wgate_bc[:], wgate.partition_broadcast(P)).then_inc(in_w, 16)
            sp.dma_start(scal_bc[:], scalars.partition_broadcast(P)).then_inc(in_w, 16)
            with nc.allow_non_contiguous_dma(reason="3200 indices, once"):
                sp.dma_start(l2_idx[:, 0, :], edges[0:USED, 0:P].rearrange("r e -> e r")).then_inc(in_l2i, 16)
                sp.dma_start(l2_idx[:, 1, :], edges[0:USED, P:2 * P].rearrange("r e -> e r")).then_inc(in_l2i, 16)

            def store(table_ap, src, done):
                sp.dma_start(table_ap.rearrange("(t p) f -> p t f", p=P), src).then_inc(done, 16)

            sp.wait_ge(zeros_ready, 1)
            for t in sums:
                sp.dma_start(t.rearrange("(t p) f -> p t f", p=P),
                             zeros.unsqueeze(1).to_broadcast([P, NT + 1, SW])).then_inc(cleared, 16)
            sp.wait_ge(rowsf_ready, 1)
            sp.dma_start(src_rows.rearrange("(g p) e -> p g e", p=WG), rows_f[:, :, 0:P]).then_inc(rows_stored, 16)

            sp.wait_ge(y0_ready, 1)
            store(y0_table, aux[:], y0_stored)
            sp.wait_ge(qv_ready, 1)
            store(q_table, acc[0][:, :, 0:D], qv_stored)
            store(v_table, acc[1][:, :, 0:D], qv_stored)
            sp.wait_ge(l2_ready, 1)
            store(l2_table, acc[0][:], l2_stored)
            with nc.allow_non_contiguous_dma(reason="16 bytes of each node, once"):
                store(al_table, acc[0][:, :, D + H:AW], l2_stored)
            def load_sources(start_row, half):
                sp.dma_start(src_row[:, half, :, :].rearrange("p w e -> p (w e)"),
                             src_rows[start_row, :].rearrange("w e -> (w e)").partition_broadcast(P)
                             ).then_inc(row_in[half], 16)

            sp.wait_ge(srcf_ready, 1)
            sp.wait_ge(rows_stored, 16)
            load_sources(slice(0, GRP), 0)
            load_sources(slice(GRP, 2 * GRP), 1)
            with sp.Fori(0, ITER - 1) as i:
                for half in range(2):
                    sp.wait_ge(same_ready, i * 2 + (half + 1))
                    load_sources(bass.ds(i * RING + (2 + half) * GRP, GRP), half)
            sp.wait_ge(same_ready, NGRP - 1)
            load_sources(slice(0, GRP), 0)

            for n in range(TABLES):
                sp.wait_ge(summed_in[n], 16 * (NW // TABLES))
            for c in range(2):
                for n in range(TABLES):
                    if c:
                        sp.wait_ge(chunk_used, 1 if n else 2)
                    sp.dma_start(part(n)[:, :, 0:SW],
                                 sums[n][c * HALF * P:(c + 1) * HALF * P, :].rearrange("(t p) f -> p t f", p=P)
                                 ).then_inc(read_back[c], 16)
            sp.wait_ge(out_ready, 1)
            sp.dma_start(out[0:HALF * P, :].rearrange("(t p) f -> p t f", p=P),
                         feat[:, 0:HALF, :]).then_inc(out_stored, 16)
            sp.wait_ge(out_ready, 2)
            sp.dma_start(out[HALF * P:(USED - 1) * P, :].rearrange("(t p) f -> p t f", p=P),
                         feat[:, HALF:USED - 1, :]).then_inc(out_stored, 16)
            sp.dma_start(out[(USED - 1) * P:N, :], feat[0:TAIL, USED - 1, :]).then_inc(out_stored, 16)
            sp.wait_ge(out_stored, 48)

        @block.gpsimd
        def _(pool):
            pool.memset(ones[:], 1.0).then_inc(ones_ready, 1)
            pool.memset(zeros, 0.0).then_inc(zeros_ready, 1)
            pool.iota(iota_d[:], pattern=[[1, P]], base=0, channel_multiplier=0,
                      allow_small_or_imprecise_dtypes=True).then_inc(const_ready, 1)
            pool.iota(iota_w, pattern=[[1, NW]], base=0, channel_multiplier=0,
                      allow_small_or_imprecise_dtypes=True).then_inc(const_ready, 1)
            pool.iota(wcol[:], pattern=[[WG, 4]], base=0, channel_multiplier=1,
                      allow_small_or_imprecise_dtypes=True).then_inc(const_ready, 1)
            pool.wait_ge(ones_ready, 1)
            pool.affine_select(out=ident[:], in_=ones[:], compare_op=ALU.is_equal, fill=0.0, base=0,
                               pattern=[[-1, P]], channel_multiplier=1).then_inc(const_ready, 1)
            pool.memset(eps_col[:], EPS).then_inc(const_ready, 1)
            pool.iota(spare_row[:], pattern=[[0, 1]], base=NT * P, channel_multiplier=1,
                      allow_small_or_imprecise_dtypes=True).then_inc(const_ready, 1)

            pool.wait_ge(jidx_ready, 1)
            for g in range(4):
                pool.indirect_dma_start(out=work_i[:, g, :], out_offset=None, in_=edges,
                                        in_offset=bass.IndirectOffsetOnAxis(ap=jidx[:, g:g + 1], axis=0),
                                        ).then_inc(rows_got, 16)
            pool.wait_ge(meta_ready, 1)

            def gathers(loop, table_ap, free, per_group, later):
                before = GATHERS.index(loop) * NGRP
                with pool.Fori(0, ITER) as i:
                    for half in range(2):
                        pool.wait_ge(free, i * (2 * per_group) + (half * per_group + later))
                        pool.sem_inc(pool_steps, 1)
                        pool.tensor_copy(idx_stage[:, half, :],
                                         srcT[:, bass.ds(i * RING + half * GRP, GRP)]).then_inc(idx_staged, 1)
                        pool.wait_ge(idx_staged, i * 2 + (before + half + 1))
                        pool.sem_inc(pool_steps, 1)
                        for j in range(GRP):
                            slot = half * GRP + j
                            pool.indirect_dma_start(
                                out=ring[:, slot, 0:D], out_offset=None, in_=table_ap,
                                in_offset=bass.IndirectOffsetOnAxis(ap=idx_stage[:, half, j:j + 1], axis=0),
                            ).then_inc(got[slot], 16)

            pool.wait_ge(y0_stored, 16)
            gathers(AGG0, y0_table, summed[AGG0], GRP, GRP)
            pool.wait_ge(qv_stored, 32)
            gathers(SCORE, q_table, scored, 4, 0)
            pool.wait_ge(scored, 4 + NW // 2)
            gathers(ATT, v_table, ev_ready, 4, 0)
            pool.wait_ge(l2_stored, 32)
            pool.wait_ge(in_l2i, 32)
            for t in range(USED):
                pool.indirect_dma_start(out=acc[1][:, t, :], out_offset=None, in_=l2_table,
                                        in_offset=bass.IndirectOffsetOnAxis(ap=l2_idx[:, 1, t:t + 1], axis=0),
                                        ).then_inc(l2_got, 16)
                pool.indirect_dma_start(out=ral[:, t, :], out_offset=None, in_=al_table,
                                        in_offset=bass.IndirectOffsetOnAxis(ap=l2_idx[:, 0, t:t + 1], axis=0),
                                        ).then_inc(l2_got, 16)
            pool.wait_ge(y3_ready, 1)
            pool.affine_select(out=before_tri, in_=ones[:], compare_op=ALU.is_gt, fill=0.0, base=0,
                               pattern=[[1, P]], channel_multiplier=-1).then_inc(tri_ready, 1)
            pool.wait_ge(cleared, 16 * TABLES)
            with pool.Fori(0, ITER) as i:
                for half in range(2):
                    pool.wait_ge(idx_ready, i * 2 + (half + 1))
                    pool.sem_inc(pool_steps, 1)
                    for j in range(GRP):
                        slot = half * GRP + j
                        n = j % TABLES
                        pool.wait_ge(row_out, i * RING + (4 + slot + 1))
                        pool.sem_inc(pool_steps, 1)
                        pool.wait_ge(summed_in[n], i * (16 * RING // TABLES) + 16 * (slot // TABLES))
                        pool.sem_inc(pool_steps, 1)
                        pool.indirect_dma_start(
                            out=sums[n], in_=ring[:, slot, :], in_offset=None,
                            out_offset=bass.IndirectOffsetOnAxis(ap=idx_stage[:, half, j:j + 1], axis=0),
                            compute_op=ALU.add).then_inc(summed_in[n], 16)
                        if j == TABLES - 1:
                            pool.sem_inc(group_in, 1)

        @block.scalar
        def _(act):
            act.wait_ge(const_ready, 6)

            def turn_nodes(proj, features):
                base = proj * NT
                act.wait_ge(feat_ready, features)
                with act.Fori(0, NPAIR) as i:
                    for a in range(2):
                        nc.scalar.copy(stage[:, a, :], feat[:, bass.ds(i * 2 + a, 1), :]
                                       .rearrange("p a b -> p (a b)")).then_inc(staged, 1)
                    for a in range(2):
                        act.wait_ge(turned, i * 2 + (base + a + 1))
                        act.wait_ge(projected, i * 2 + (base + a + 1))
                        nc.scalar.copy(xT[:, a, :, :].rearrange("p k n -> p (k n)"),
                                       ps[:, a, 0:2 * P]).then_inc(xT_ready, 1)

            def masks_back(loop):
                act.sem_inc(maskT_ready[loop], 2)
                with act.Fori(0, NGRP) as g:
                    for half in range(2):
                        act.wait_ge(maskT_full[loop], g * 2 + (half + 1))
                        if loop == SCORE:
                            act.wait_ge(k_ready, g * 4 + 4)
                        else:
                            act.wait_ge(m_full, g)
                        nc.scalar.copy(maskT[:, half * 4:half * 4 + 4, :].rearrange("p a b -> p (a b)"),
                                       ps[:, half, :]).then_inc(maskT_ready[loop], 1)
                    if loop == ATT:
                        act.wait_ge(summed[ATT], g * GRP)
                        act.wait_ge(less_m, g + 1)
                        nc.scalar.activation(ev[:, :, D:D + H], ex_in[:], ACT.Exp,
                                             scale=HD ** -0.5).then_inc(ex_ready, 1)

            def blocks_out(first, dst, heads=H):
                for g in range(NB):
                    act.wait_ge(block_turned, first + g + 1)
                    src = ps[:, (first + g) % 2, 0:P]
                    if heads == 1:
                        src = src.rearrange("p (w h) -> p w h", h=H)[:, :, 0:1]
                    elif len(dst(g).shape) == 3:
                        src = src.rearrange("p (w h) -> p w h", h=H)
                    nc.scalar.copy(dst(g), src).then_inc(block_out, 1)

            def root(n):
                act.wait_ge(var_ready, n)
                nc.scalar.activation(sd[:], mv[:, :, 1], ACT.Sqrt, bias=eps_col[:, 0:1]).then_inc(rooted, 1)

            turn_nodes(XW, 1)
            act.wait_ge(deg_ready, 1)
            nc.scalar.activation(dsq[:], deg[:], ACT.Sqrt, bias=ones[:, 0:1]).then_inc(deg_rooted, 1)
            blocks_out(0, lambda g: turnedT[:, g, :])
            root(1)
            turn_nodes(QV, 2)
            turn_nodes(K, 2)
            masks_back(SCORE)
            blocks_out(NB, lambda g: turnedT[:, g, :])
            blocks_out(2 * NB, lambda g: sel[:, g * 32:g * 32 + 32, H:H + 1], 1)
            blocks_out(3 * NB, lambda g: sel[:, g * 32:g * 32 + 32, 0:H])
            turn_nodes(SKIP, 2)
            masks_back(ATT)
            act.wait_ge(logit_ready, 1)
            nc.scalar.activation(small[:, 2, :], small[:, 0, :], ACT.Sigmoid,
                                 bias=scal_bc[:, 1:2]).then_inc(gate_ready, 1)
            root(2)
            root(3)
            turn_nodes(L2P, 3)
            act.wait_ge(l2_logits, 1)
            nc.scalar.activation(alpha[:], ral[:], ACT.Exp).then_inc(l2_exps, 1)
            root(4)
            turn_nodes(L3P, 4)
            act.sem_inc(maskT_ready[SPREAD], 2)
            act.sem_inc(row_out, 4)
            with act.Fori(0, ITER) as i:
                for side in range(2):
                    for half in range(2):
                        act.wait_ge(maskT_full[SPREAD], i * 4 + (side * 2 + half + 1))
                        act.wait_ge(row_full, i * RING + side * GRP)
                        nc.scalar.copy(maskT[:, half * 4:half * 4 + 4, :].rearrange("p a b -> p (a b)"),
                                       ps[:, half, :]).then_inc(maskT_ready[SPREAD], 1)
                    act.wait_ge(group_in, i * 2 + side)
                    for j in range(GRP):
                        act.wait_ge(row_full, i * RING + (side * GRP + j + 1))
                        nc.scalar.copy(ring[:, side * GRP + j, :], ps[:, 2 + j % 4, 0:SW]).then_inc(row_out, 1)
            root(5)
            root(6)

        @block.tensor
        def _(pe):
            pe.wait_ge(const_ready, 6)
            pe.wait_ge(ones_ready, 1)
            pe.wait_ge(cnt_ready, 1)
            pe.matmul(ps[:, 7, 0:NT], ones[0:ROWS // 4, :], cnt[0:ROWS // 4, :], start=True,
                      stop=True).then_inc(cum_ready, 1)
            pe.sem_inc(projected, 2)

            def project(proj, w, c0, n):
                base = proj * NT
                with pe.Fori(0, NPAIR) as i:
                    for a in range(2):
                        pe.wait_ge(staged, i * 2 + (base + a + 1))
                        pe.transpose(ps[:, a, 0:P], stage[:, a, 0:P], ident[:])
                        pe.transpose(ps[:, a, P:2 * P], stage[:, a, P:2 * P], ident[:]).then_inc(turned, 1)
                    for a in range(2):
                        pe.wait_ge(xT_ready, i * 2 + (base + a + 1))
                        pe.wait_ge(evacuated, i * 2 + (base + a + 1))
                        pe.matmul(ps[:, 2 + a, 0:n], xT[:, a, 0, :], w[:, 0, c0:c0 + n], start=True, stop=False)
                        pe.matmul(ps[:, 2 + a, 0:n], xT[:, a, 1, :], w[:, 1, c0:c0 + n],
                                  start=False, stop=True).then_inc(projected, 1)

            def turn_blocks(first, src):
                for g in range(NB):
                    if first + g >= 2:
                        pe.wait_ge(block_out, first + g - 1)
                    pe.transpose(ps[:, (first + g) % 2, 0:P], src(g), ident[:]).then_inc(block_turned, 1)

            def aggregate(loop):
                before = GATHERS.index(loop) * ITER * 16
                pe.sem_inc(summed[loop], RING)
                with pe.Fori(0, ITER) as i:
                    for half in range(2):
                        pe.wait_ge(mask_ready[loop], i * 2 + (half + 1))
                        for j in range(GRP):
                            slot = half * GRP + j
                            pe.wait_ge(got[slot], i * 16 + (before + 16))
                            pe.wait_ge(added[loop], i * RING + (slot + 1))
                            pe.matmul(ps[:, j, 0:D], mask[:, half, j, :], ring[:, slot, 0:D],
                                      start=True, stop=True).then_inc(summed[loop], 1)

            def small_sums(loop, dst, rhs):
                with pe.Fori(0, ITER) as i:
                    for half in range(2):
                        pe.wait_ge(mask_ready[loop], i * 2 + (half + 1))
                        for j in range(GRP):
                            mm = pe.matmul(dst(i, half * GRP + j), mask[:, half, j, :],
                                           rhs(i, half * GRP + j), start=True, stop=True)
                        mm.then_inc(summed[loop], 1)

            def turn_masks(loop, i, half):
                pe.wait_ge(mask_ready[loop], i * 2 + (half + 1))
                pe.wait_ge(maskT_ready[loop], i * 4 + (2 * half + 2))
                for j in range(GRP):
                    tr = pe.transpose(ps[:, j // 4, (j % 4) * P:(j % 4 + 1) * P], mask[:, half, j, :], ident[:])
                    if j % 4 == 3:
                        tr.then_inc(maskT_full[loop], 1)
                pe.wait_ge(maskT_ready[loop], i * 4 + (2 * half + 4))

            pe.wait_ge(in_w, 96)
            project(XW, w_sb, 0, D)
            pe.wait_ge(rowsf_ready, 1)
            for g in range(4):
                pe.transpose(ps[:, 4, g * WG:(g + 1) * WG], rows_f[:, g, 0:P], ident[0:WG, 0:WG])
                tr = pe.transpose(ps[:, 5, g * WG:(g + 1) * WG], rows_f[:, g, P:2 * P], ident[0:WG, 0:WG])
            tr.then_inc(rowsT_ready, 1)
            small_sums(DEG, lambda i, n: ps[:, 7, bass.ds(i * RING + n, 1)], lambda i, n: ones[:, 0:1])
            pe.wait_ge(evacuated, 2 + NT)
            pe.wait_ge(keys_ready, 1)
            turn_blocks(0, lambda g: key4[:, g * 32:g * 32 + 32, :].rearrange("p a b -> p (a b)"))
            pe.wait_ge(block_out, NB)
            pe.wait_ge(y0_stored, 16)
            aggregate(AGG0)
            pe.wait_ge(added[AGG0], 8 + NW)
            project(QV, w_sb, D, 2 * D)
            project(K, w_sb, 3 * D, D)

            pe.wait_ge(ks_ready, 1)
            pe.sem_inc(k_ready, 4)
            tile_regs = [pe.alloc_register(f"k_tile{j}") for j in range(GRP)]
            with pe.Fori(0, ITER) as i:
                for half in range(2):
                    pe.load(tile_regs, tile_i[0:1, bass.ds(i * RING + half * GRP, GRP)])
                    tiles = [pe.snap(r, min_val=0, max_val=NT - 1) for r in tile_regs]
                    turn_masks(SCORE, i, half)
                    for j in range(GRP):
                        if j % 2 == 0:
                            pe.wait_ge(scored, i * 8 + (half * 4 + j // 2 + 1))
                        mm = pe.matmul(ps[:, 2 + j // 2, (j % 2) * D:(j % 2 + 1) * D], maskT[:, j, :],
                                       aux[:, bass.ds(tiles[j], 1), :].rearrange("p a b -> p (a b)"),
                                       start=True, stop=True)
                        if j % 2 == 1:
                            mm.then_inc(k_ready, 1)

            pe.wait_ge(scored, 4 + NW // 2)
            turn_blocks(NB, lambda g: score[:, g * 32:g * 32 + 32, :].rearrange("p a b -> p (a b)"))
            pe.wait_ge(last_ready, 1)
            turn_blocks(2 * NB, lambda g: last[:, g, :])
            pe.wait_ge(seg_ready, 1)
            turn_blocks(3 * NB, lambda g: runT[:, g, :])
            pe.wait_ge(block_out, 4 * NB)
            small_sums(SEG, lambda i, n: ps_flat[:, bass.ds(i * (RING * 8) + n * 8, 5)],
                       lambda i, n: sel[:, bass.ds(i * RING + n, 1), 0:5].rearrange("p a b -> p (a b)"))

            pe.wait_ge(sums_out, 1)
            project(SKIP, w_sb, 4 * D, D)
            pe.wait_ge(evacuated, 2 + 4 * NT)
            pe.wait_ge(m_ready, 1)
            with pe.Fori(0, ITER) as i:
                for half in range(2):
                    turn_masks(ATT, i, half)
                    pe.wait_ge(less_m, i * 2 + half)
                    for j in range(GRP):
                        mm = pe.matmul(ps[:, 2, j * H:(j + 1) * H], maskT[:, j, :],
                                       mfull[:, bass.ds(i * RING + half * GRP + j, 1), :]
                                       .rearrange("p a b -> p (a b)"), start=True, stop=True)
                    mm.then_inc(m_full, 1)
                    for j in range(GRP):
                        pe.wait_ge(ev_ready, i * 8 + (4 + half * 4 + j // 2 + 1))
                        pe.wait_ge(added[ATT], i * RING + (half * GRP + j + 1))
                        pe.matmul(ps[:, 3 + j % 4, 0:D + H], mask[:, half, j, :], ev[:, j, :],
                                  start=True, stop=True).then_inc(summed[ATT], 1)

            pe.wait_ge(added[ATT], 4 + NW)
            project(L2P, w2_sb, 0, AW)
            project(L3P, w_sb, 5 * D, 2 * D)
            pe.wait_ge(y3_ready, 1)
            with pe.Fori(0, ITER) as i:
                for half in range(2):
                    pe.load(tile_regs, tile_i[0:1, bass.ds(i * RING + half * GRP, GRP)])
                    tiles = [pe.snap(r, min_val=0, max_val=NT - 1) for r in tile_regs]
                    pe.wait_ge(mask_ready[SPREAD], i * 2 + (half + 1))
                    pe.wait_ge(same_ready, i * 2 + (half + 1))
                    pe.wait_ge(maskT_ready[SPREAD], i * 4 + (2 * half + 2))
                    for j in range(GRP):
                        mm = pe.matmul(ps[:, j // 4, (j % 4) * P:(j % 4 + 1) * P], mask[:, half, j, :],
                                       same[:, j, :], start=True, stop=True)
                        if j % 4 == 3:
                            mm.then_inc(maskT_full[SPREAD], 1)
                    pe.wait_ge(idx_ready, i * 2 + half)
                    for j in range(GRP):
                        mm = pe.matmul(ps[:, 6, j:j + 1], earlier[:, j, :], ones[:, 0:1], start=True, stop=True)
                    mm.then_inc(dup_full, 1)
                    pe.wait_ge(maskT_ready[SPREAD], i * 4 + (2 * half + 4))
                    for j in range(GRP):
                        pe.wait_ge(row_out, i * RING + (half * GRP + j + 1))
                        pe.matmul(ps[:, 2 + j % 4, 0:SW], maskT[:, j, :],
                                  acc[0][:, bass.ds(tiles[j], 1), 0:SW].rearrange("p a b -> p (a b)"),
                                  start=True, stop=True).then_inc(row_full, 1)

        @block.vector
        def _(v):
            chain = [0]

            def link(ins):
                chain[0] += 1
                ins.then_inc(dve_seq, 1)
                v.wait_ge(dve_seq, chain[0])

            def bias(n, count=1):
                return bias_bc[:, n * D:(n + count) * D]

            def over_tiles(row, tiles=NT):
                return row.unsqueeze(1).to_broadcast([P, tiles, row.shape[-1]])

            v.sem_inc(evacuated, 2)
            v.memset(feat[:, USED - 1:NT, :], 0.0).then_inc(x_tail, 1)
            v.memset(cnt[:], 0.0)
            v.wait_ge(const_ready, 6)
            v.wait_ge(in_edges, 16)
            rows_d = rows_i[:, :, P:2 * P]
            n_rows = ROWS // 4
            link(v.tensor_copy(dst_f, rows_d))
            for c in range(1, USED + 1):
                ins = v.tensor_scalar(prod[0:n_rows, c % 2, :], dst_f.rearrange("p a b -> p (a b)"), float(P * c), 0.0, ALU.is_lt, ALU.add,
                                      accum_out=cnt[0:n_rows, c:c + 1])
                link(ins)
            v.sem_inc(cnt_ready, 1)
            v.wait_ge(cum_ready, 1)
            link(v.tensor_copy(cum[:], ps[:, 7, 0:NT]))
            link(v.tensor_copy(cum_i[:, 0, :], cum[:]))
            link(v.tensor_scalar(cum_i[:, 1, :], cum[:], -1.0, None, ALU.add))
            link(v.tensor_single_scalar(cum_i[:], cum_i[:], 7, ALU.arith_shift_right))
            link(v.tensor_copy(first_row[:], cum_i[:, 0, :]))
            link(v.tensor_copy(last_row[:], cum_i[:, 1, :]))
            U1 = USED
            link(v.tensor_tensor(items[:, 0:U1], last_row[:, 1:U1 + 1], first_row[:, 0:U1], ALU.subtract))
            link(v.tensor_scalar(items[:, 0:U1], items[:, 0:U1], 1.0, None, ALU.add))
            link(v.tensor_tensor(off[:, 0:U1], cum[:, 1:U1 + 1], cum[:, 0:U1], ALU.is_gt))
            link(v.tensor_tensor(items[:, 0:U1], items[:, 0:U1], off[:, 0:U1], ALU.mult))
            link(v.memset(start[:, 0:1], 0.0))
            link(v.tensor_tensor_scan(start[:, 1:U1 + 1], ones[:, 0:U1], items[:, 0:U1], 0.0, ALU.mult, ALU.add))
            link(v.tensor_tensor(off[:, 0:U1], first_row[:, 0:U1], start[:, 0:U1], ALU.subtract))
            link(v.tensor_tensor(doff[:, 1:U1], off[:, 1:U1], off[:, 0:U1 - 1], ALU.subtract))
            shape = [WG, 4, U1 - 1]
            link(v.tensor_tensor(ge[:], wcol[:].unsqueeze(2).to_broadcast(shape),
                                 start[0:WG, 1:U1].unsqueeze(1).to_broadcast(shape), ALU.is_ge))
            link(v.tensor_tensor(geo[:], ge[:], doff[0:WG, 1:U1].unsqueeze(1).to_broadcast(shape), ALU.mult))
            link(v.tensor_reduce(tcol[:], ge[:], X_AXIS, ALU.add))
            link(v.tensor_reduce(jcol[:], geo[:], X_AXIS, ALU.add))
            link(v.tensor_scalar(t128[:], tcol[:], float(P), None, ALU.mult))
            link(v.tensor_tensor(jcol[:], jcol[:], wcol[:], ALU.add))
            link(v.tensor_scalar(jcol[:], jcol[:], off[0:WG, 0:1], -float(PAD_ROW), ALU.add, ALU.add))
            link(v.tensor_scalar(jcol2[:], wcol[:], start[0:WG, U1:U1 + 1], None, ALU.is_lt))
            link(v.tensor_tensor(jcol[:], jcol[:], jcol2[:], ALU.mult))
            v.tensor_scalar(jidx[:], jcol[:], float(PAD_ROW), None, ALU.add).then_inc(jidx_ready, 1)
            link(v.memset(tile_w, 0.0))
            for c in range(1, U1):
                link(v.scalar_tensor_tensor(out=tile_w[:, c % 2, :], in0=iota_w, scalar=start[:, c:c + 1],
                                            in1=tile_w[:, (c - 1) % 2, :], op0=ALU.is_ge, op1=ALU.add))
            tw = tile_row
            link(v.tensor_copy(tw[:], tile_w[:, (U1 - 1) % 2, :]))
            link(v.tensor_copy(tile_i[:], tw[0:1, :]))
            v.wait_ge(rows_got, 64)
            link(v.tensor_copy(rows_f[:, :, 0:P], work_i[:, :, 0:P]))
            link(v.tensor_tensor(rows_f[:, :, P:2 * P], work_i[:, :, P:2 * P],
                                 t128[:].unsqueeze(2).to_broadcast([WG, 4, P]), ALU.subtract))
            v.sem_inc(rowsf_ready, 1)

            def evacuate(proj, write):
                base = proj * NT
                with v.Fori(0, NPAIR) as i:
                    for a in range(2):
                        v.wait_ge(projected, i * 2 + (base + a + 3))
                        write(a, lambda t: t[:, bass.ds(i * 2 + a, 1), :].rearrange("p a b -> p (a b)")
                              ).then_inc(evacuated, 1)
                v.wait_ge(evacuated, 2 + base + NT)

            v.wait_ge(in_w, 96)
            for k in range(2):
                for side in range(2):
                    link(v.tensor_tensor(prod[:, 0, 0:D], w2_sb[:, k, 0:D], attn_bc[:, 1 - side, :], ALU.mult))
                    link(v.tensor_reduce(w2_sb[:, k, D + side * H:D + (side + 1) * H],
                                         prod[:, 0, 0:D].rearrange("p (h d) -> p h d", d=HD), X_AXIS, ALU.add))
            v.wait_ge(in_x, 32)
            v.sem_inc(feat_ready, 1)
            evacuate(XW, lambda a, at: v.tensor_copy(at(aux), ps[:, 2 + a, 0:D]))
            v.wait_ge(rowsT_ready, 1)
            link(v.memset(dstl[:, NW:], -1.0))
            link(v.tensor_copy(dstl[:, 0:NW], ps[:, 5, 0:NW]))
            link(v.tensor_copy(srcT[:], ps[:, 4, 0:NW]))
            v.sem_inc(meta_ready, 1)

            def make_mask(loop, slot, at):
                shape3 = [P, GRP, P]
                return v.tensor_tensor(mask[:, slot, :, :], iota_d[:].unsqueeze(1).to_broadcast(shape3),
                                       dstl[:, at].unsqueeze(2).to_broadcast(shape3),
                                       ALU.is_equal).then_inc(mask_ready[loop], 1)

            def mask_loop(loop, slot_free, per_group, later, group):
                make_mask(loop, 0, slice(0, GRP))
                with v.Fori(0, ITER) as i:
                    for half in range(2):
                        v.wait_ge(slot_free, i * (2 * per_group) + (half * per_group + later))
                        make_mask(loop, 1 - half, bass.ds(i * RING + (half + 1) * GRP, GRP))
                        if group:
                            group(i, half)

            mask_loop(DEG, summed[DEG], 1, 0, None)
            v.wait_ge(summed[DEG], NGRP)
            link(v.tensor_copy(degs[:, 0, :], ps[:, 7, 0:NW]))
            for t in range(NT):
                link(v.scalar_tensor_tensor(out=degs[:, 1, :], in0=tw[:], scalar=float(t), in1=degs[:, 0, :],
                                            op0=ALU.is_equal, op1=ALU.mult, accum_out=deg[:, t:t + 1]))
            v.sem_inc(deg_ready, 1)
            v.wait_ge(deg_rooted, 1)
            link(v.reciprocal(dinv[:], dsq[:]))

            def per_node(col, width=D):
                return col.unsqueeze(2).to_broadcast([P, NT, width])

            link(v.tensor_tensor(aux[:], aux[:], per_node(dinv[:]), ALU.mult))
            v.sem_inc(y0_ready, 1)
            v.wait_ge(rows_stored, 16)
            link(v.tensor_copy(acc[0][:, :, 0:D], aux[:]))
            link(v.tensor_copy(key4,
                               dstl[:, 0:NW].unsqueeze(2).to_broadcast([P, NW, H])))
            v.sem_inc(keys_ready, 1)
            v.wait_ge(block_out, NB)
            link(v.memset(reset[:], -BIG))
            link(v.tensor_tensor(reset[:, :, 1:P], turnedT[:, :, 0:P - 1], turnedT[:, :, 1:P], ALU.not_equal))
            link(v.tensor_scalar(reset[:, :, 1:P], reset[:, :, 1:P], -BIG, None, ALU.mult))
            link(v.memset(acc[1][:], 0.0))

            tile_regs = [v.alloc_register(f"add_tile{j}") for j in range(GRP)]

            def add_group(loop, i, half, width, full, free, bank):
                v.load(tile_regs, tile_i[0:1, bass.ds(i * RING + half * GRP, GRP)])
                for j in range(GRP):
                    t = v.snap(tile_regs[j], min_val=0, max_val=NT - 1)
                    n = half * GRP + j
                    v.wait_ge(summed[loop], i * RING + (full + n + 1))
                    v.wait_ge(added[loop], i * RING + (free + n - 1))
                    into = acc[j % 2][:, bass.ds(t, 1), 0:width].rearrange("p a b -> p (a b)")
                    v.tensor_tensor(into, into, ps[:, bank(j), 0:width], ALU.add).then_inc(added[loop], 1)

            def aggregate(loop):
                v.sem_inc(added[loop], 8)
                mask_loop(loop, summed[loop], GRP, 2 * GRP,
                          lambda i, half: add_group(loop, i, half, D, RING, 8, lambda j: j))
                v.wait_ge(added[loop], 8 + NW)

            norms = [0]

            def layernorm(src, dst, tiles=NT):
                norms[0] += 1
                for t in range(tiles):
                    ins = v.bn_stats(stats[:, t, :], src[:, t, :])
                link(ins)
                for t in range(tiles):
                    ins = v.bn_aggr(mv[:, t, :], stats[:, t, :])
                link(ins)
                v.sem_inc(var_ready, 1)
                v.wait_ge(rooted, norms[0])
                link(v.reciprocal(rstd[:], sd[:]))
                for t in range(tiles):
                    ins = v.tensor_scalar(dst[:, t, :], src[:, t, :], mv[:, t, 0:1], rstd[:, t:t + 1],
                                          ALU.subtract, ALU.mult)
                link(ins)

            a0, a1 = acc[0][:, :, 0:D], acc[1][:, :, 0:D]
            v.wait_ge(y0_stored, 16)
            aggregate(AGG0)
            link(v.tensor_tensor(a0, a0, a1, ALU.add))
            link(v.tensor_tensor(a0, a0, per_node(dinv[:]), ALU.mult))
            link(v.tensor_tensor(a0, a0, over_tiles(bias(0)), ALU.add))
            link(v.scalar_tensor_tensor(out=a0, in0=a0, scalar=0.0, in1=feat[:], op0=ALU.max, op1=ALU.add))
            layernorm(a0, feat[:])
            v.sem_inc(feat_ready, 1)

            def pair_out(first, second, n):
                def write(a, at):
                    v.tensor_tensor(at(first), ps[:, 2 + a, 0:D], bias(n), ALU.add)
                    return v.tensor_tensor(at(second), ps[:, 2 + a, D:2 * D], bias(n + 1), ALU.add)
                return write

            evacuate(QV, pair_out(a0, a1, 1))
            v.sem_inc(qv_ready, 1)
            evacuate(K, lambda a, at: v.tensor_tensor(at(aux), ps[:, 2 + a, 0:D], bias(3), ALU.add))
            v.sem_inc(ks_ready, 1)

            def scores(i, half):
                for q in range(4):
                    slot = half * GRP + 2 * q
                    for n in range(2):
                        v.wait_ge(got[slot + n], i * 16 + (ITER * 16 + 16))
                    v.wait_ge(k_ready, i * 8 + (4 + half * 4 + q + 1))
                    v.wait_ge(scored, i * 8 + (half * 4 + q + 3))
                    chain_at = i * 8 + (half * 4 + q + 1)
                    v.tensor_tensor(prod[:, q % 2, :].rearrange("p (a b) -> p a b", a=2),
                                    ps[:, 2 + q, :].rearrange("p (a b) -> p a b", a=2),
                                    ring[:, slot:slot + 2, 0:D],
                                    ALU.mult).then_inc(prod_ready, 1)
                    v.wait_ge(prod_ready, chain_at)
                    v.tensor_reduce(score[:, bass.ds(i * RING + slot, 2), :].rearrange("p a h -> p (a h)"),
                                    prod[:, q % 2, :].rearrange("p (g d) -> p g d", d=HD), X_AXIS,
                                    ALU.add).then_inc(scored, 1)

            v.sem_inc(scored, 4)
            mask_loop(SCORE, maskT_full[SCORE], 2, 0, scores)
            v.wait_ge(scored, 4 + NW // 2)
            v.wait_ge(qv_stored, 32)
            link(v.memset(last, 1.0))
            link(v.tensor_scalar(last[:, :, 0:P - 1], reset[:, :, 1:P], 0.0, None, ALU.is_lt))
            v.sem_inc(last_ready, 1)
            link(v.memset(treset, -BIG))
            link(v.tensor_tensor(treset[:, 0, 1:NW], tw[:, 1:NW], tw[:, 0:NW - 1], ALU.not_equal))
            link(v.tensor_scalar(treset[:, 0, 1:NW], treset[:, 0, 1:NW], -BIG, None, ALU.mult))
            link(v.tensor_copy(treset[:, 1, 0:NW - 1], treset[:, 0, 1:NW]))
            v.wait_ge(block_out, 2 * NB)
            flat = lambda t: t.rearrange("p g e -> p (g e)")
            link(v.tensor_tensor_scan(flat(runT), flat(reset[:]), flat(turnedT), -BIG, ALU.add, ALU.max))
            link(v.tensor_tensor(runT, runT, last, ALU.mult))
            v.sem_inc(seg_ready, 1)
            mask_loop(SEG, summed[SEG], 1, 0, None)
            v.wait_ge(summed[SEG], NGRP)
            at_dst = ps_flat[:, 0:NW * 8].rearrange("p (w c) -> p w c", c=8)
            v.tensor_copy(sel, at_dst[:, :, 0:H + 1]).then_inc(sums_out, 1)
            v.wait_ge(sums_out, 1)
            for h in range(H):
                link(v.tensor_scalar(cand[:, h, :], sel[:, :, H], BIG, -BIG, ALU.mult, ALU.add))
                link(v.tensor_tensor(cand[:, h, :], cand[:, h, :], sel[:, :, h], ALU.add))
                link(v.tensor_tensor_scan(mfwd[:, h, :], treset[:, 0, :], cand[:, h, :], -BIG, ALU.add, ALU.max))
                link(v.tensor_tensor_scan(cand[:, h, ::-1], treset[:, 1, ::-1], mfwd[:, h, ::-1], -BIG,
                                          ALU.add, ALU.max))
                link(v.tensor_copy(mfull[:, :, h], cand[:, h, :]))
            evacuate(SKIP, lambda a, at: v.tensor_tensor(at(aux), ps[:, 2 + a, 0:D], bias(4), ALU.add))
            v.sem_inc(m_ready, 1)
            link(v.memset(acc[0][:], 0.0))
            link(v.memset(acc[1][:], 0.0))

            def attend(i, half):
                g = lambda k, c: i * (2 * k) + (half * k + c)
                v.wait_ge(m_full, g(1, 1))
                v.wait_ge(ex_ready, g(1, 0))
                v.tensor_tensor(ex_in[:], score[:, bass.ds(i * RING + half * GRP, GRP), :],
                                ps[:, 2, 0:GRP * H].rearrange("p (w h) -> p w h", h=H),
                                ALU.subtract).then_inc(less_m, 1)
                v.wait_ge(ex_ready, g(1, 1))
                for q in range(4):
                    slot = half * GRP + 2 * q
                    for n in range(2):
                        v.wait_ge(got[slot + n], i * 16 + (2 * ITER * 16 + 16))
                    for n in range(2):
                        ins = v.tensor_tensor(ev[:, 2 * q + n, 0:D].rearrange("p (h d) -> p h d", d=HD),
                                        ring[:, slot + n, 0:D].rearrange("p (h d) -> p h d", d=HD),
                                        ev[:, 2 * q + n, D:D + H].unsqueeze(2).to_broadcast([P, H, HD]),
                                        ALU.mult)
                    ins.then_inc(ev_ready, 1)
                add_group(ATT, i, half, D + H, 0, 4, lambda j: 3 + j % 4)

            v.sem_inc(added[ATT], 4)
            v.sem_inc(ev_ready, 4)
            mask_loop(ATT, summed[ATT], GRP, 0, attend)
            v.wait_ge(added[ATT], 4 + NW)
            heads = lambda t: t.rearrange("p t (h d) -> p t h d", d=HD)
            link(v.tensor_tensor(acc[0][:, :, 0:D + H], acc[0][:, :, 0:D + H], acc[1][:, :, 0:D + H], ALU.add))
            link(v.tensor_scalar(den4[:], acc[0][:, :, D:D + H], 1e-30, None, ALU.max))
            link(v.reciprocal(den4[:], den4[:]))
            for h in range(H):
                ins = v.tensor_tensor(a0[:, :, h * HD:(h + 1) * HD], a0[:, :, h * HD:(h + 1) * HD],
                                      per_node(den4[:, :, h], HD), ALU.mult)
            link(ins)
            link(v.tensor_tensor(wgate_bc[:, 0:D], wgate_bc[:, 0:D], wgate_bc[:, 2 * D:3 * D], ALU.add))
            link(v.tensor_tensor(wgate_bc[:, D:2 * D], wgate_bc[:, D:2 * D], wgate_bc[:, 2 * D:3 * D],
                                 ALU.subtract))
            link(v.tensor_tensor(a1, aux[:], over_tiles(wgate_bc[:, 0:D]), ALU.mult))
            link(v.tensor_reduce(small[:, 0, :], a1, X_AXIS, ALU.add))
            link(v.tensor_tensor(a1, a0, over_tiles(wgate_bc[:, D:2 * D]), ALU.mult))
            link(v.tensor_reduce(small[:, 1, :], a1, X_AXIS, ALU.add))
            link(v.tensor_tensor(small[:, 0, :], small[:, 0, :], small[:, 1, :], ALU.add))
            v.sem_inc(logit_ready, 1)
            link(v.tensor_tensor(aux[:], aux[:], a0, ALU.subtract))
            v.wait_ge(gate_ready, 1)
            link(v.tensor_tensor(aux[:], aux[:], per_node(small[:, 2, :]), ALU.mult))
            link(v.tensor_tensor(a0, a0, aux[:], ALU.add))
            layernorm(a0, a0)
            link(v.tensor_tensor(a0, a0, over_tiles(bias(5)), ALU.mult))
            link(v.tensor_tensor(a0, a0, over_tiles(bias(6)), ALU.add))
            link(v.tensor_scalar(aux[:], a0, 0.0, scal_bc[:, 0:1], ALU.min, ALU.mult))
            link(v.scalar_tensor_tensor(out=a0, in0=a0, scalar=0.0, in1=aux[:], op0=ALU.max, op1=ALU.add))
            link(v.tensor_tensor(a0, a0, feat[:], ALU.add))
            layernorm(a0, feat[:])
            v.sem_inc(feat_ready, 1)
            evacuate(L2P, lambda a, at: v.tensor_copy(at(acc[0]), ps[:, 2 + a, 0:AW]))
            v.sem_inc(l2_ready, 1)
            v.wait_ge(l2_got, 2 * USED * 16)
            link(v.memset(acc[1][:, USED:, :], 0.0))
            link(v.memset(ral[:, USED:, :], 0.0))
            link(v.tensor_tensor(ral[:], ral[:], acc[1][:, :, D:D + H], ALU.add))
            link(v.tensor_scalar(alpha[:], ral[:], 0.0, 0.01, ALU.min, ALU.mult))
            link(v.scalar_tensor_tensor(out=ral[:], in0=ral[:], scalar=0.0, in1=alpha[:], op0=ALU.max, op1=ALU.add))
            link(v.tensor_reduce(small[:, 3, :], ral[:], X_AXIS, ALU.max))
            link(v.tensor_tensor(ral[:], ral[:], per_node(small[:, 3, :], H), ALU.subtract))
            v.sem_inc(l2_logits, 1)
            v.wait_ge(l2_exps, 1)
            link(v.tensor_reduce(small[:, 3, :], alpha[:], X_AXIS, ALU.add))
            link(v.reciprocal(small[:, 3, :], small[:, 3, :]))
            link(v.tensor_tensor(alpha[:], alpha[:], per_node(small[:, 3, :], H), ALU.mult))
            for h in range(H):
                ins = v.tensor_tensor(a1[:, :, h * HD:(h + 1) * HD], a1[:, :, h * HD:(h + 1) * HD],
                                      per_node(alpha[:, :, h], HD), ALU.mult)
            link(ins)
            link(v.tensor_reduce(tmp64, a1.rearrange("p t (h d) -> p t d h", d=HD), X_AXIS, ALU.add))
            for h in range(H):
                ins = v.tensor_tensor(aux[:, :, h * HD:(h + 1) * HD], feat[:, :, h * HD:(h + 1) * HD],
                                      tmp64, ALU.add)
            link(ins)
            layernorm(aux[:], feat[:])
            v.sem_inc(feat_ready, 1)
            link(v.tensor_tensor(bias(7), bias(7), bias(8), ALU.add))
            v.wait_ge(l2_stored, 32)

            acc0_features = acc[0][:, :, 0:D]

            def l3_out(a, at):
                v.tensor_copy(at(acc0_features), ps[:, 2 + a, 0:D])
                return v.tensor_tensor(at(aux), ps[:, 2 + a, D:2 * D], bias(7), ALU.add)

            evacuate(L3P, l3_out)
            link(v.memset(acc[0][:, :, D:SW], 1.0))
            link(v.memset(srcf[:, NW:], 0.0))
            link(v.tensor_copy(srcf[:, 0:NW], srcT[:]))
            v.sem_inc(y3_ready, 1)
            v.sem_inc(srcf_ready, 1)
            v.wait_ge(tri_ready, 1)
            shape3 = [P, GRP, P]

            def make_same(side, at):
                v.tensor_tensor(same, src_row[:, side, :, :], srcf[:, at].unsqueeze(2).to_broadcast(shape3),
                                ALU.is_equal).then_inc(same_made, 1)

            v.wait_ge(row_in[0], 16)
            make_same(0, slice(0, GRP))
            v.wait_ge(same_made, 1)
            v.tensor_tensor(earlier, same, before_tri.unsqueeze(1).to_broadcast(shape3),
                            ALU.mult).then_inc(same_ready, 1)

            def spread(i, half):
                v.wait_ge(dup_full, i * 2 + (half + 1))
                v.wait_ge(row_in[1 - half], i * 16 + 16 * (half + 1))
                make_same(1 - half, bass.ds(i * RING + (half + 1) * GRP, GRP))
                at = bass.ds(i * RING + half * GRP, GRP)
                v.tensor_scalar(to_spare, srcf[:, at], -1.0, spare_row[:, 0:1], ALU.mult,
                                ALU.add).then_inc(idx_steps, 1)
                v.wait_ge(idx_steps, i * 4 + (half * 2 + 1))
                v.scalar_tensor_tensor(out=to_spare2, in0=ps[:, 6, 0:GRP], scalar=0.5, in1=to_spare,
                                       op0=ALU.is_gt, op1=ALU.mult).then_inc(idx_steps, 1)
                v.wait_ge(same_made, i * 2 + (half + 2))
                v.tensor_tensor(earlier, same, before_tri.unsqueeze(1).to_broadcast(shape3),
                                ALU.mult).then_inc(same_ready, 1)
                v.wait_ge(idx_steps, i * 4 + (half * 2 + 2))
                v.wait_ge(group_in, i * 2 + half)
                v.tensor_tensor(idx_stage[:, half, :], srcf[:, at], to_spare2, ALU.add).then_inc(idx_ready, 1)

            mask_loop(SPREAD, dup_full, 1, 0, spread)
            for c in range(2):
                nodes = slice(c * HALF, (c + 1) * HALF)
                v.wait_ge(read_back[c], 16 * TABLES)
                total = part(0)[:, :, 0:SW]
                for n in range(1, TABLES):
                    link(v.tensor_tensor(total, total, part(n)[:, :, 0:SW], ALU.add))
                v.sem_inc(chunk_used, 1)
                link(v.tensor_scalar(rcnt[:, nodes], total[:, :, D], 1.0, None, ALU.max))
                link(v.reciprocal(rcnt[:, nodes], rcnt[:, nodes]))
                mean = total[:, :, 0:D]
                link(v.tensor_tensor(mean, mean, rcnt[:, nodes].unsqueeze(2).to_broadcast([P, HALF, D]), ALU.mult))
                link(v.tensor_tensor(mean, mean, aux[:, nodes, :], ALU.add))
                link(v.tensor_tensor(mean, mean, feat[:, nodes, :], ALU.add))
                layernorm(mean, feat[:, nodes, :], HALF)
                v.sem_inc(out_ready, 1)
                v.sem_inc(chunk_used, 1)


def kernel(**inputs):
    import numpy as np
    import concourse.bacc as bacc
    from concourse.bass_utils import run_bass_kernel_spmd

    f = {k: np.asarray(v) for k, v in inputs.items()}
    rows = np.zeros((ROWS, 2, P), np.int32)
    rows[:, 1, :] = PAD_DST
    for side, name in enumerate(("src", "dst")):
        whole = E // P
        rows[:whole, side, :] = f[name][:whole * P].reshape(whole, P)
        rows[whole, side, :E - whole * P] = f[name][whole * P:]
    w_all = np.concatenate([f["L0_gnn_W"], f["L1_gnn_Wq"].T, f["L1_gnn_Wv"].T, f["L1_gnn_Wk"].T,
                            f["L1_gnn_Wskip"].T, f["L3_gnn_W2"].T, f["L3_gnn_W1"].T], axis=1)
    bias = np.concatenate([f[n] for n in ("L0_gnn_b", "L1_gnn_bq", "L1_gnn_bv", "L1_gnn_bk", "L1_gnn_bskip",
                                          "L1_gnn_ln_w", "L1_gnn_ln_b", "L3_gnn_b1", "L3_gnn_b2")])
    arrays = {
        "x": f["x"], "edges": rows.reshape(ROWS, 2 * P), "w_all": w_all, "w_l2": f["L2_gnn_weight"],
        "bias": bias,
        "attn": np.concatenate([f["L2_gnn_attn_l"].reshape(-1), f["L2_gnn_attn_r"].reshape(-1)]),
        "wgate": f["L1_gnn_Wgate"].reshape(-1),
        "scalars": np.concatenate([f["L1_gnn_prelu_a"].reshape(1), f["L1_gnn_bgate"].reshape(1)]),
    }
    arrays = {k: np.ascontiguousarray(a) for k, a in arrays.items()}
    nc = bacc.Bacc("TRN2", target_bir_lowering=False, num_devices=1)
    aps = [nc.dram_tensor(k, a.shape, mybir.dt.from_np(a.dtype), kind="ExternalInput").ap()
           for k, a in arrays.items()]
    out = nc.dram_tensor("out", (N, D), F32, kind="ExternalOutput").ap()
    gnn_kernel(nc, *aps, out)
    return run_bass_kernel_spmd(nc, [arrays], core_ids=[0]).results[0]["out"]
```

```python
from contextlib import ExitStack

import concourse.bass as bass
from concourse import mybir

F32 = mybir.dt.float32
BF16 = mybir.dt.bfloat16
I32 = mybir.dt.int32
ALU = mybir.AluOpType
ACT = mybir.ActivationFunctionType
X_AXIS = mybir.AxisListType.X

P = 128
N = 3125
E = 50000
D = 256
H = 4
HD = D // H
NT = 26
USED = -(-N // P)
TAIL = N - (USED - 1) * P
ROWS = 392
PAD_ROW = ROWS - 1
PAD_DST = 1 << 20
NW = 416
WG = 104
GRP = 8
RING = 2 * GRP
ITER = NW // RING
AW = D + 2 * H
BIG = 1.0e30
EPS = 1e-5
NPAIR = NT // 2
TABLES = 4
SW = D + 1


def gnn_kernel(nc, x, edges, edges_t, w_all, w_l2, bias, attn, wgate, scalars, out):
    ctx = ExitStack()
    with ctx:
        def sb(name, shape, dt=F32):
            return ctx.enter_context(nc.sbuf_tensor(name, shape, dt))

        def sem(name):
            return ctx.enter_context(nc.semaphore(name))

        def table(name, width):
            return nc.dram_tensor(name, [NT * P, width], F32).ap()

        y0_table = table("y0_table", D)
        q_table = table("q_table", D)
        v_table = table("v_table", D)
        l2_table = table("l2_table", AW)
        al_table = table("al_table", H)
        sums = [nc.dram_tensor(f"sums{n}", [NT * P + P, SW], F32).ap() for n in range(TABLES)]
        src_rows = nc.dram_tensor("src_rows", [NW, P], F32).ap()

        feat = sb("feat", [P, NT, D])
        acc = [sb(f"acc{n}", [P, NT, AW]) for n in range(2)]
        aux = sb("aux", [P, NT, D])
        ring = sb("ring", [P, RING, D + H])
        mask = sb("mask", [P, 2, GRP, P])
        maskT = sb("maskT", [P, GRP, P])
        pairs = sb("pairs", [P, 2 * GRP * P])
        w_sb = sb("w_sb", [P, 2, 7 * D])
        w2_sb = sb("w2_sb", [P, 2, AW])
        bias_bc = sb("bias_bc", [P, 9 * D])
        wgate_bc = sb("wgate_bc", [P, 3 * D])
        scal_bc = sb("scal_bc", [P, 2])
        stage = sb("stage", [P, 2, D])
        xT = sb("xT", [P, 2, 2, P])
        ident = sb("ident", [P, P])
        ones = sb("ones", [P, P])
        iota_d = sb("iota_d", [P, P])
        wcol = sb("wcol", [WG, 4])
        cum = sb("cum", [P, NT])
        cum_i = sb("cum_i", [P, 2, NT], I32)
        first_row = sb("first_row", [P, NT])
        last_row = sb("last_row", [P, NT])
        items = sb("items", [P, NT])
        start = sb("start", [P, NT])
        off = sb("off", [P, NT])
        doff = sb("doff", [P, NT])
        ge = sb("ge", [WG, 4, USED - 1])
        geo = sb("geo", [WG, 4, USED - 1])
        tcol = sb("tcol", [WG, 4])
        t128 = sb("t128", [WG, 4])
        jcol = sb("jcol", [WG, 4])
        jcol2 = sb("jcol2", [WG, 4])
        jidx = sb("jidx", [WG, 4], I32)
        tile_i = sb("tile_i", [1, NW], I32)
        srcT = sb("srcT", [P, NW], I32)
        dstl = sb("dstl", [P, NW + GRP])
        idx_stage = sb("idx_stage", [P, 2, GRP], I32)
        l2_idx = sb("l2_idx", [P, 2, USED], I32)
        deg = sb("deg", [P, NT])
        dsq = sb("dsq", [P, NT])
        dinv = sb("dinv", [P, NT])
        rcnt = sb("rcnt", [P, NT])
        starts = sb("starts", [P, NW * P // 32 + 1])
        joined = sb("joined", [P, NW + 1])
        one_seg = sb("one_seg", [P, NW])
        lane = sb("lane", [P, 32])
        same_head = sb("same_head", [P, P])
        score = sb("score", [P, NW, H])
        stats = sb("stats", [P, NT, 6])
        mv = sb("mv", [P, NT, 2])
        sd = sb("sd", [P, NT])
        rstd = sb("rstd", [P, NT])
        small = sb("small", [P, 4, NT])
        ral = sb("ral", [P, NT, H])
        alpha = sb("alpha", [P, NT, H])
        den4 = sb("den4", [P, NT, H])
        eps_col = sb("eps_col", [P, 1])
        small_idx = sb("small_idx", [P, 2, GRP])
        to_spare = small_idx[:, 0, :]
        to_spare2 = small_idx[:, 1, :]
        tile_row = sb("tile_row", [P, NW])
        spare_row = sb("spare_row", [P, 1])

        def within(tensor, at, shape, dt=F32):
            words = 1
            for n in shape[1:]:
                words *= n
            flat = tensor[:] if len(tensor.shape) == 2 else tensor[:].rearrange("p t f -> p (t f)")
            flat = flat[0:shape[0], at:at + words]
            flat = flat if dt == F32 else flat.bitcast(dt)
            names = "xyz"[:len(shape) - 1]
            sizes = dict(zip(names, shape[1:]))
            sizes.pop(names[0])
            return flat.rearrange(f"p ({' '.join(names)}) -> p {' '.join(names)}", **sizes) if len(names) > 1 else flat

        NB = NW // 32
        rows_f = within(acc[0], 1024, [WG, 4, 2 * P])
        work_i = within(acc[0], 2048, [WG, 4, 2 * P], I32)
        attn_bc = within(acc[0], 3072, [P, 2, D])
        dst_parts_i = within(acc[0], 3584, [P, 2, NW], I32)
        dst_parts = within(acc[0], 4416, [P, 2, NW])
        tile_diag = within(acc[0], 5248, [WG, 4, WG])
        lane_of = within(acc[0], 5664, [P, 4], I32)
        lane_of_f = within(acc[0], 5668, [P, 4])
        lane_row = within(acc[0], 5672, [P, P])
        in_tile = acc[1][:].rearrange("p t f -> p (t f)")[:, 0:NW * NT // 2].bitcast(BF16).rearrange(
            "p (j c) -> p j c", c=NT)
        edge_cols = within(ring, 0, [P, 2, NW], I32)
        iota_b = within(ring, 2 * NW, [P, P // 2]).bitcast(BF16)
        zero_b = within(ring, 2 * NW + P // 2, [P, P // 2]).bitcast(BF16)
        at_place = mask[:].rearrange("p s g d -> p (s g d)").bitcast(BF16).rearrange(
            "p (s g d) -> p s g d", s=4, g=GRP)
        turnedT = within(acc[1], 0, [P, NB, P])
        runT = within(acc[1], 1664, [P, NB, P])
        ends = within(acc[1], 3328, [P, 2, NB, 32])
        carry_w = within(acc[1], 4160, [P, NW - 1])
        key4 = within(acc[1], 4992, [P, NW, H])
        carry = within(acc[0], 0, [P, 2, NW])
        carried = within(acc[0], 2 * NW, [P, 2, NW])
        placed = within(acc[0], 4 * NW, [P, 2, NB, 32])
        carry_in = within(acc[0], 6 * NW, [P, 2, NB])
        tmp64 = within(acc[0], 0, [P, NT, HD])
        prod = within(pairs, 0, [P, 2, 2 * D])
        same = within(pairs, 0, [P, GRP, P])
        earlier = within(pairs, GRP * P, [P, GRP, P])
        src_row = within(w_sb, 0, [P, 2, GRP, P])
        srcf = within(w_sb, 2 * GRP * P, [P, NW + GRP])
        before_tri = within(w_sb, 2 * GRP * P + NW + GRP, [P, P])
        zeros = within(maskT, 0, [P, SW])
        ps = ctx.enter_context(nc.psum_tensor("ps", [P, 8, 512], F32))
        ps_flat = ps[:].rearrange("p b c -> p (b c)")

        in_edges, in_x, in_w = sem("in_edges"), sem("in_x"), sem("in_w")
        rows_got, l2_got, out_stored = sem("rows_got"), sem("l2_got"), sem("out_stored")
        y0_stored, qv_stored, l2_stored, rows_stored = (sem("y0_stored"), sem("qv_stored"),
                                                      sem("l2_stored"), sem("rows_stored"))
        zeros_ready, cleared = sem("zeros_ready"), sem("cleared")
        row_in = [sem(f"row_in{n}") for n in range(2)]
        summed_in = [sem(f"summed_in{n}") for n in range(TABLES)]
        read_back = [sem(f"read_back{n}") for n in range(2)]
        got = [sem(f"got{n}") for n in range(RING)]
        const_ready, x_tail, ones_ready = sem("const_ready"), sem("x_tail"), sem("ones_ready")
        cum_ready, jidx_ready = sem("cum_ready"), sem("jidx_ready")
        rowsf_ready, rowsT_ready, meta_ready = sem("rowsf_ready"), sem("rowsT_ready"), sem("meta_ready")
        deg_ready, deg_rooted = sem("deg_ready"), sem("deg_rooted")
        var_ready, rooted, feat_ready = sem("var_ready"), sem("rooted"), sem("feat_ready")
        logit_ready, gate_ready = sem("logit_ready"), sem("gate_ready")
        l2_logits, l2_exps = sem("l2_logits"), sem("l2_exps")
        y0_ready, qv_ready, ks_ready = sem("y0_ready"), sem("qv_ready"), sem("ks_ready")
        l2_ready, y3_ready, out_ready = sem("l2_ready"), sem("y3_ready"), sem("out_ready")
        dinv_ready = sem("dinv_ready")
        place_ready, counted, deg_full = sem("place_ready"), sem("counted"), sem("deg_full")
        diag_ready, tiles_full = sem("diag_ready"), sem("tiles_full")
        keys_ready, ends_ready, ends_spread = sem("keys_ready"), sem("ends_ready"), sem("ends_spread")
        starts_ready = sem("starts_ready")
        less_m, exps_ready = sem("less_m"), sem("exps_ready")
        dve_seq = sem("dve_seq")
        pool_steps = sem("pool_steps")
        idx_staged = sem("idx_staged")
        staged = sem("staged")
        turned = sem("turned")
        xT_ready = sem("xT_ready")
        projected = sem("projected")
        evacuated = sem("evacuated")
        block_turned, block_out = sem("block_turned"), sem("block_out")
        AGG0, SCORE, ATT, SPREAD = range(4)
        mask_ready = [sem(f"mask_ready{n}") for n in range(4)]
        summed = {n: sem(f"summed{n}") for n in (AGG0, ATT)}
        added = {n: sem(f"added{n}") for n in (AGG0, ATT)}
        maskT_full = {n: sem(f"maskT_full{n}") for n in (SCORE, SPREAD)}
        maskT_ready = {n: sem(f"maskT_ready{n}") for n in (SCORE, SPREAD)}
        prod_ready = sem("prod_ready")
        k_ready, scored = sem("k_ready"), sem("scored")
        ev_ready = sem("ev_ready")

        same_made, idx_steps = sem("same_made"), sem("idx_steps")
        same_ready, dup_full, idx_ready = sem("same_ready"), sem("dup_full"), sem("idx_ready")
        row_full, row_out, group_in = sem("row_full"), sem("row_out"), sem("group_in")
        chunk_used, tri_ready, srcf_ready = sem("chunk_used"), sem("tri_ready"), sem("srcf_ready")

        XW, QV, K, SKIP, L2P, L3P = range(6)
        NGRP = NW // GRP
        GATHERS = [AGG0, SCORE, ATT]

        HALF = NT // 2

        def part(n):
            return acc[n // 2][:, (n % 2) * HALF:(n % 2 + 1) * HALF, :]

        block = ctx.enter_context(nc.Block())

        @block.sync
        def _(sp):
            sp.dma_start(edge_cols, edges_t).then_inc(in_edges, 16)
            sp.dma_start(feat[:, 0:USED - 1, :],
                         x[0:(USED - 1) * P, :].rearrange("(t p) f -> p t f", p=P)).then_inc(in_x, 16)
            sp.wait_ge(x_tail, 1)
            sp.dma_start(feat[0:TAIL, USED - 1, :], x[(USED - 1) * P:N, :]).then_inc(in_x, 16)
            sp.dma_start(w_sb[:], w_all.rearrange("(k p) n -> p k n", p=P)).then_inc(in_w, 16)
            sp.dma_start(w2_sb[:, :, 0:D], w_l2.rearrange("(k p) n -> p k n", p=P)).then_inc(in_w, 16)
            sp.dma_start(bias_bc[:], bias.partition_broadcast(P)).then_inc(in_w, 16)
            sp.dma_start(attn_bc.rearrange("p a b -> p (a b)"), attn.partition_broadcast(P)).then_inc(in_w, 16)
            sp.dma_start(wgate_bc[:], wgate.partition_broadcast(P)).then_inc(in_w, 16)
            sp.dma_start(scal_bc[:], scalars.partition_broadcast(P)).then_inc(in_w, 16)
            def store(table_ap, src, done):
                sp.dma_start(table_ap.rearrange("(t p) f -> p t f", p=P), src).then_inc(done, 16)

            sp.wait_ge(zeros_ready, 1)
            for t in sums:
                sp.dma_start(t.rearrange("(t p) f -> p t f", p=P),
                             zeros.unsqueeze(1).to_broadcast([P, NT + 1, SW])).then_inc(cleared, 16)
            sp.wait_ge(rowsf_ready, 1)
            sp.dma_start(src_rows.rearrange("(g p) e -> p g e", p=WG), rows_f[:, :, 0:P]).then_inc(rows_stored, 16)

            sp.wait_ge(y0_ready, HALF + 1)
            store(y0_table, aux[:], y0_stored)
            sp.wait_ge(qv_ready, 1)
            store(q_table, acc[0][:, :, 0:D], qv_stored)
            store(v_table, acc[1][:, :, 0:D], qv_stored)
            sp.wait_ge(l2_ready, 1)
            store(l2_table, acc[0][:], l2_stored)
            with nc.allow_non_contiguous_dma(reason="16 bytes of each node, once"):
                store(al_table, acc[0][:, :, D + H:AW], l2_stored)
            def load_sources(start_row, half):
                sp.dma_start(src_row[:, half, :, :].rearrange("p w e -> p (w e)"),
                             src_rows[start_row, :].rearrange("w e -> (w e)").partition_broadcast(P)
                             ).then_inc(row_in[half], 16)

            sp.wait_ge(srcf_ready, 1)
            sp.wait_ge(rows_stored, 16)
            load_sources(slice(0, GRP), 0)
            load_sources(slice(GRP, 2 * GRP), 1)
            with sp.Fori(0, ITER - 1) as i:
                for half in range(2):
                    sp.wait_ge(same_ready, i * 2 + (half + 1))
                    load_sources(bass.ds(i * RING + (2 + half) * GRP, GRP), half)
            sp.wait_ge(same_ready, NGRP - 1)
            load_sources(slice(0, GRP), 0)

            for n in range(TABLES):
                sp.wait_ge(summed_in[n], 16 * (NW // TABLES))
            for c in range(2):
                for n in range(TABLES):
                    if c:
                        sp.wait_ge(chunk_used, 1 if n else 2)
                    sp.dma_start(part(n)[:, :, 0:SW],
                                 sums[n][c * HALF * P:(c + 1) * HALF * P, :].rearrange("(t p) f -> p t f", p=P)
                                 ).then_inc(read_back[c], 16)
            sp.wait_ge(out_ready, 1)
            sp.dma_start(out[0:HALF * P, :].rearrange("(t p) f -> p t f", p=P),
                         feat[:, 0:HALF, :]).then_inc(out_stored, 16)
            sp.wait_ge(out_ready, 2)
            sp.dma_start(out[HALF * P:(USED - 1) * P, :].rearrange("(t p) f -> p t f", p=P),
                         feat[:, HALF:USED - 1, :]).then_inc(out_stored, 16)
            sp.dma_start(out[(USED - 1) * P:N, :], feat[0:TAIL, USED - 1, :]).then_inc(out_stored, 16)
            sp.wait_ge(out_stored, 48)

        @block.gpsimd
        def _(pool):
            pool.memset(ones[:], 1.0).then_inc(ones_ready, 1)
            pool.memset(zeros, 0.0).then_inc(zeros_ready, 1)
            pool.iota(iota_d[:], pattern=[[1, P]], base=0, channel_multiplier=0,
                      allow_small_or_imprecise_dtypes=True).then_inc(const_ready, 1)
            pool.iota(iota_b, pattern=[[1, P]], base=0, channel_multiplier=0,
                      allow_small_or_imprecise_dtypes=True).then_inc(const_ready, 1)
            pool.memset(zero_b, 0.0).then_inc(const_ready, 1)
            pool.iota(wcol[:], pattern=[[WG, 4]], base=0, channel_multiplier=1,
                      allow_small_or_imprecise_dtypes=True).then_inc(const_ready, 1)
            pool.wait_ge(ones_ready, 1)
            pool.affine_select(out=ident[:], in_=ones[:], compare_op=ALU.is_equal, fill=0.0, base=0,
                               pattern=[[-1, P]], channel_multiplier=1).then_inc(const_ready, 1)
            pool.memset(eps_col[:], EPS).then_inc(const_ready, 1)
            pool.iota(spare_row[:], pattern=[[0, 1]], base=NT * P, channel_multiplier=1,
                      allow_small_or_imprecise_dtypes=True).then_inc(const_ready, 1)

            pool.iota(lane_of[:, 0:1], pattern=[[0, 1]], base=0, channel_multiplier=1).then_inc(const_ready, 1)
            pool.iota(lane_row, pattern=[[0, 32], [1, H]], base=0, channel_multiplier=0,
                      allow_small_or_imprecise_dtypes=True).then_inc(const_ready, 1)

            pool.wait_ge(jidx_ready, 1)
            for g in range(4):
                pool.indirect_dma_start(out=work_i[:, g, :], out_offset=None, in_=edges,
                                        in_offset=bass.IndirectOffsetOnAxis(ap=jidx[:, g:g + 1], axis=0),
                                        ).then_inc(rows_got, 16)
            pool.wait_ge(meta_ready, 1)

            def gathers(loop, table_ap, free, per_group, later):
                before = GATHERS.index(loop) * NGRP
                with pool.Fori(0, ITER) as i:
                    for half in range(2):
                        pool.wait_ge(free, i * (2 * per_group) + (half * per_group + later))
                        pool.sem_inc(pool_steps, 1)
                        pool.tensor_copy(idx_stage[:, half, :],
                                         srcT[:, bass.ds(i * RING + half * GRP, GRP)]).then_inc(idx_staged, 1)
                        pool.wait_ge(idx_staged, i * 2 + (before + half + 1))
                        pool.sem_inc(pool_steps, 1)
                        for j in range(GRP):
                            slot = half * GRP + j
                            pool.indirect_dma_start(
                                out=ring[:, slot, 0:D], out_offset=None, in_=table_ap,
                                in_offset=bass.IndirectOffsetOnAxis(ap=idx_stage[:, half, j:j + 1], axis=0),
                            ).then_inc(got[slot], 16)

            pool.wait_ge(y0_stored, 16)
            gathers(AGG0, y0_table, summed[AGG0], GRP, GRP)
            pool.wait_ge(qv_stored, 32)
            gathers(SCORE, q_table, scored, 4, 0)
            pool.wait_ge(scored, 4 + NW // 2)
            gathers(ATT, v_table, summed[ATT], GRP, GRP)
            pool.wait_ge(l2_stored, 32)
            for t in range(USED):
                pool.indirect_dma_start(out=acc[1][:, t, :], out_offset=None, in_=l2_table,
                                        in_offset=bass.IndirectOffsetOnAxis(ap=l2_idx[:, 1, t:t + 1], axis=0),
                                        ).then_inc(l2_got, 16)
                pool.indirect_dma_start(out=ral[:, t, :], out_offset=None, in_=al_table,
                                        in_offset=bass.IndirectOffsetOnAxis(ap=l2_idx[:, 0, t:t + 1], axis=0),
                                        ).then_inc(l2_got, 16)
            pool.wait_ge(y3_ready, 1)
            pool.affine_select(out=before_tri, in_=ones[:], compare_op=ALU.is_gt, fill=0.0, base=0,
                               pattern=[[1, P]], channel_multiplier=-1).then_inc(tri_ready, 1)
            pool.wait_ge(cleared, 16 * TABLES)
            with pool.Fori(0, ITER) as i:
                for half in range(2):
                    pool.wait_ge(idx_ready, i * 2 + (half + 1))
                    pool.sem_inc(pool_steps, 1)
                    for j in range(GRP):
                        slot = half * GRP + j
                        n = j % TABLES
                        pool.wait_ge(row_out, i * RING + (4 + slot + 1))
                        pool.sem_inc(pool_steps, 1)
                        pool.wait_ge(summed_in[n], i * (16 * RING // TABLES) + 16 * (slot // TABLES))
                        pool.sem_inc(pool_steps, 1)
                        pool.indirect_dma_start(
                            out=sums[n], in_=ring[:, slot, 0:SW], in_offset=None,
                            out_offset=bass.IndirectOffsetOnAxis(ap=idx_stage[:, half, j:j + 1], axis=0),
                            compute_op=ALU.add).then_inc(summed_in[n], 16)
                        if j == TABLES - 1:
                            pool.sem_inc(group_in, 1)

        @block.scalar
        def _(act):
            act.wait_ge(const_ready, 9)

            def turn_nodes(proj, features):
                base = proj * NT
                act.wait_ge(feat_ready, features)
                with act.Fori(0, NPAIR) as i:
                    for a in range(2):
                        nc.scalar.copy(stage[:, a, :], feat[:, bass.ds(i * 2 + a, 1), :]
                                       .rearrange("p a b -> p (a b)")).then_inc(staged, 1)
                    for a in range(2):
                        act.wait_ge(turned, i * 2 + (base + a + 1))
                        act.wait_ge(projected, i * 2 + (base + a + 1))
                        nc.scalar.copy(xT[:, a, :, :].rearrange("p k n -> p (k n)"),
                                       ps[:, a, 0:2 * P]).then_inc(xT_ready, 1)

            def blocks_out(first, dst):
                for g in range(NB):
                    act.wait_ge(block_turned, first + g + 1)
                    src = ps[:, (first + g) % 2, 0:P]
                    if len(dst(g).shape) == 3:
                        src = src.rearrange("p (w h) -> p w h", h=H)
                    nc.scalar.copy(dst(g), src).then_inc(block_out, 1)

            def root(n):
                act.wait_ge(var_ready, n)
                nc.scalar.activation(sd[:], mv[:, :, 1], ACT.Sqrt, bias=eps_col[:, 0:1]).then_inc(rooted, 1)

            act.sem_inc(evacuated, 2)
            act.wait_ge(in_x, 32)
            with act.Fori(0, NPAIR) as i:
                for a in range(2):
                    nc.scalar.copy(stage[:, a, :], feat[:, bass.ds(i * 2 + a, 1), :]
                                   .rearrange("p a b -> p (a b)")).then_inc(staged, 1)
                for a in range(2):
                    act.wait_ge(turned, i * 2 + (a + 1))
                    act.wait_ge(projected, i * 2 + (a + 1))
                    nc.scalar.copy(xT[:, a, :, :].rearrange("p k n -> p (k n)"),
                                   ps[:, a, 0:2 * P]).then_inc(xT_ready, 1)
                for a in range(2):
                    act.wait_ge(projected, i * 2 + (a + 3))
                    nc.scalar.copy(aux[:, bass.ds(i * 2 + a, 1), :].rearrange("p a b -> p (a b)"),
                                   ps[:, 2 + a, 0:D]).then_inc(evacuated, 1)
            act.wait_ge(deg_ready, 1)
            nc.scalar.activation(dsq[:], deg[:], ACT.Sqrt, bias=ones[:, 0:1]).then_inc(deg_rooted, 1)
            act.wait_ge(dinv_ready, 1)
            act.wait_ge(evacuated, 2 + NT)
            for t in range(HALF, NT):
                nc.scalar.mul(aux[:, t, :], aux[:, t, :], dinv[:, t:t + 1]).then_inc(y0_ready, 1)
            blocks_out(0, lambda g: turnedT[:, g, :])
            root(1)
            turn_nodes(QV, 1)
            turn_nodes(K, 1)
            act.sem_inc(maskT_ready[SCORE], 2)
            with act.Fori(0, NGRP) as g:
                for half in range(2):
                    act.wait_ge(maskT_full[SCORE], g * 2 + (half + 1))
                    act.wait_ge(k_ready, g * 4 + 4)
                    nc.scalar.copy(maskT[:, half * 4:half * 4 + 4, :].rearrange("p a b -> p (a b)"),
                                   ps[:, half, :]).then_inc(maskT_ready[SCORE], 1)
            blocks_out(NB, lambda g: turnedT[:, g, :])
            act.wait_ge(less_m, 1)
            nc.scalar.activation(turnedT, turnedT, ACT.Exp, scale=HD ** -0.5).then_inc(exps_ready, 1)
            blocks_out(2 * NB, lambda g: score[:, g * 32:g * 32 + 32, :])
            with act.Fori(0, NT) as t:
                nc.scalar.copy(stage[:, 0, :], feat[:, bass.ds(t, 1), :]
                               .rearrange("p a b -> p (a b)")).then_inc(staged, 1)
                act.wait_ge(turned, t + (SKIP * NT + 1))
                nc.scalar.copy(xT[:, 0, :, :].rearrange("p k n -> p (k n)"),
                               ps[:, 0, 0:2 * P]).then_inc(xT_ready, 1)
                act.wait_ge(projected, t + (SKIP * NT + 3))
                nc.scalar.copy(aux[:, bass.ds(t, 1), :].rearrange("p a b -> p (a b)"),
                               ps[:, 1, 0:D]).then_inc(evacuated, 1)
            act.wait_ge(logit_ready, 1)
            nc.scalar.activation(small[:, 2, :], small[:, 0, :], ACT.Sigmoid,
                                 bias=scal_bc[:, 1:2]).then_inc(gate_ready, 1)
            root(2)
            root(3)
            turn_nodes(L2P, 2)
            act.wait_ge(l2_logits, 1)
            nc.scalar.activation(alpha[:], ral[:], ACT.Exp).then_inc(l2_exps, 1)
            root(4)
            turn_nodes(L3P, 3)
            act.sem_inc(maskT_ready[SPREAD], 2)
            act.sem_inc(row_out, 4)
            with act.Fori(0, ITER) as i:
                for side in range(2):
                    for half in range(2):
                        act.wait_ge(maskT_full[SPREAD], i * 4 + (side * 2 + half + 1))
                        act.wait_ge(row_full, i * RING + side * GRP)
                        nc.scalar.copy(maskT[:, half * 4:half * 4 + 4, :].rearrange("p a b -> p (a b)"),
                                       ps[:, half, :]).then_inc(maskT_ready[SPREAD], 1)
                    act.wait_ge(group_in, i * 2 + side)
                    for j in range(GRP):
                        act.wait_ge(row_full, i * RING + (side * GRP + j + 1))
                        nc.scalar.copy(ring[:, side * GRP + j, 0:SW], ps[:, 2 + j % 4, 0:SW]).then_inc(row_out, 1)
            root(5)
            root(6)

        @block.tensor
        def _(pe):
            pe.wait_ge(const_ready, 9)
            pe.wait_ge(ones_ready, 1)
            pe.sem_inc(projected, 2)

            def project(proj, w, c0, n):
                base = proj * NT
                with pe.Fori(0, NPAIR) as i:
                    for a in range(2):
                        pe.wait_ge(staged, i * 2 + (base + a + 1))
                        pe.transpose(ps[:, a, 0:P], stage[:, a, 0:P], ident[:])
                        pe.transpose(ps[:, a, P:2 * P], stage[:, a, P:2 * P], ident[:]).then_inc(turned, 1)
                    for a in range(2):
                        pe.wait_ge(xT_ready, i * 2 + (base + a + 1))
                        pe.wait_ge(evacuated, i * 2 + (base + a + 1))
                        pe.matmul(ps[:, 2 + a, 0:n], xT[:, a, 0, :], w[:, 0, c0:c0 + n], start=True, stop=False)
                        pe.matmul(ps[:, 2 + a, 0:n], xT[:, a, 1, :], w[:, 1, c0:c0 + n],
                                  start=False, stop=True).then_inc(projected, 1)

            def turn_blocks(first, src):
                for g in range(NB):
                    if first + g >= 2:
                        pe.wait_ge(block_out, first + g - 1)
                    pe.transpose(ps[:, (first + g) % 2, 0:P], src(g), ident[:]).then_inc(block_turned, 1)

            def spread_ends(n):
                pe.wait_ge(ends_ready, n)
                for side in range(2):
                    mm = pe.matmul(ps[:, 2 + side, 0:NW], same_head[:],
                                   ends[:, side, :, :].rearrange("p b n -> p (b n)"), start=True, stop=True)
                mm.then_inc(ends_spread, 1)

            def aggregate(loop, banks, width, beside=None):
                before = GATHERS.index(loop) * ITER * 16
                pe.sem_inc(summed[loop], RING)
                with pe.Fori(0, ITER) as i:
                    for half in range(2):
                        pe.wait_ge(mask_ready[loop], i * 2 + (half + 1))
                        for j in range(GRP):
                            slot = half * GRP + j
                            if loop == ATT:
                                pe.wait_ge(ev_ready, i * GRP + (half * 4 + j // 2 + 1))
                            else:
                                pe.wait_ge(got[slot], i * 16 + (before + 16))
                            pe.wait_ge(added[loop], i * RING + (slot + 1))
                            pe.matmul(ps[:, 8 - banks + j % banks, 0:width], mask[:, half, j, :],
                                      ring[:, slot, 0:width],
                                      start=True, stop=True).then_inc(summed[loop], 1)
                            if beside and j % 2 == 1:
                                beside(i, half * 4 + j // 2)

            def turn_masks(loop, i, half):
                pe.wait_ge(mask_ready[loop], i * 2 + (half + 1))
                pe.wait_ge(maskT_ready[loop], i * 4 + (2 * half + 2))
                for j in range(GRP):
                    tr = pe.transpose(ps[:, j // 4, (j % 4) * P:(j % 4 + 1) * P], mask[:, half, j, :], ident[:])
                    if j % 4 == 3:
                        tr.then_inc(maskT_full[loop], 1)
                pe.wait_ge(maskT_ready[loop], i * 4 + (2 * half + 4))

            pe.matmul(ps[:, 7, 0:NT], zero_b, zero_b[:, 0:NT], start=True, stop=False, skip_group_check=True)

            def count(i, group):
                pe.wait_ge(place_ready, i * 4 + (group + 1))
                for j in range(GRP):
                    mm = pe.matmul(ps[:, 7, 0:NT], at_place[:, group, j, :],
                                   in_tile[:, bass.ds(i * (4 * GRP) + group * GRP + j, 1), :]
                                   .rearrange("p a b -> p (a b)"),
                                   start=False, stop=False, skip_group_check=True)
                mm.then_inc(counted, 1)

            pe.wait_ge(in_w, 96)
            with pe.Fori(0, NPAIR) as i:
                for a in range(2):
                    pe.wait_ge(staged, i * 2 + (a + 1))
                    pe.transpose(ps[:, a, 0:P], stage[:, a, 0:P], ident[:])
                    pe.transpose(ps[:, a, P:2 * P], stage[:, a, P:2 * P], ident[:]).then_inc(turned, 1)
                count(i, 0)
                count(i, 1)
                for a in range(2):
                    pe.wait_ge(xT_ready, i * 2 + (a + 1))
                    pe.wait_ge(evacuated, i * 2 + (a + 1))
                    pe.matmul(ps[:, 2 + a, 0:D], xT[:, a, 0, :], w_sb[:, 0, 0:D], start=True, stop=False)
                    pe.matmul(ps[:, 2 + a, 0:D], xT[:, a, 1, :], w_sb[:, 1, 0:D],
                              start=False, stop=True).then_inc(projected, 1)
                count(i, 2)
                count(i, 3)
            pe.matmul(ps[:, 7, 0:NT], zero_b, zero_b[:, 0:NT], start=False, stop=True,
                      skip_group_check=True).then_inc(deg_full, 1)
            pe.wait_ge(deg_ready, 1)
            pe.matmul(ps[:, 6, 0:NT], ones[:], deg[:], start=True, stop=True).then_inc(cum_ready, 1)
            pe.wait_ge(diag_ready, 1)
            for g in range(4):
                mm = pe.matmul(ps[:, 6, g * WG:(g + 1) * WG], ones[0:WG, :], tile_diag[:, g, :],
                               start=True, stop=True)
            mm.then_inc(tiles_full, 1)
            pe.wait_ge(rowsf_ready, 1)
            for g in range(4):
                pe.transpose(ps[:, 4, g * WG:(g + 1) * WG], rows_f[:, g, 0:P], ident[0:WG, 0:WG])
                tr = pe.transpose(ps[:, 5, g * WG:(g + 1) * WG], rows_f[:, g, P:2 * P], ident[0:WG, 0:WG])
            tr.then_inc(rowsT_ready, 1)
            pe.wait_ge(evacuated, 2 + NT)
            pe.wait_ge(keys_ready, 1)
            turn_blocks(0, lambda g: key4[:, g * 32:g * 32 + 32, :].rearrange("p a b -> p (a b)"))
            spread_ends(1)
            pe.wait_ge(y0_stored, 16)
            pe.wait_ge(starts_ready, 1)
            aggregate(AGG0, 8, D)
            pe.wait_ge(added[AGG0], 8 + NW)
            project(QV, w_sb, D, 2 * D)
            project(K, w_sb, 3 * D, D)

            pe.wait_ge(ks_ready, 1)
            pe.sem_inc(k_ready, 4)
            tile_regs = [pe.alloc_register(f"k_tile{j}") for j in range(GRP)]
            with pe.Fori(0, ITER) as i:
                for half in range(2):
                    pe.load(tile_regs, tile_i[0:1, bass.ds(i * RING + half * GRP, GRP)])
                    tiles = [pe.snap(r, min_val=0, max_val=NT - 1) for r in tile_regs]
                    turn_masks(SCORE, i, half)
                    for j in range(GRP):
                        if j % 2 == 0:
                            pe.wait_ge(scored, i * 8 + (half * 4 + j // 2 + 1))
                        mm = pe.matmul(ps[:, 2 + j // 2, (j % 2) * D:(j % 2 + 1) * D], maskT[:, j, :],
                                       aux[:, bass.ds(tiles[j], 1), :].rearrange("p a b -> p (a b)"),
                                       start=True, stop=True)
                        if j % 2 == 1:
                            mm.then_inc(k_ready, 1)

            pe.wait_ge(scored, 4 + NW // 2)
            turn_blocks(NB, lambda g: score[:, g * 32:g * 32 + 32, :].rearrange("p a b -> p (a b)"))
            spread_ends(2)
            pe.wait_ge(block_out, 2 * NB)
            pe.wait_ge(exps_ready, 1)
            turn_blocks(2 * NB, lambda g: turnedT[:, g, :])

            def skip(t, step):
                if step == 0:
                    pe.wait_ge(staged, t + (SKIP * NT + 1))
                    pe.wait_ge(xT_ready, t + SKIP * NT)
                    pe.transpose(ps[:, 0, 0:P], stage[:, 0, 0:P], ident[:])
                    pe.transpose(ps[:, 0, P:2 * P], stage[:, 0, P:2 * P], ident[:]).then_inc(turned, 1)
                elif step == 4:
                    pe.wait_ge(xT_ready, t + (SKIP * NT + 1))
                    pe.wait_ge(evacuated, t + (SKIP * NT + 2))
                    pe.matmul(ps[:, 1, 0:D], xT[:, 0, 0, :], w_sb[:, 0, 4 * D:5 * D], start=True, stop=False)
                    pe.matmul(ps[:, 1, 0:D], xT[:, 0, 1, :], w_sb[:, 1, 4 * D:5 * D], start=False, stop=False)
                    pe.matmul(ps[:, 1, 0:D], ones[0:1, :], bias_bc[0:1, 4 * D:5 * D], start=False,
                              stop=True).then_inc(projected, 1)

            aggregate(ATT, 4, D + H, skip)
            pe.wait_ge(added[ATT], 4 + NW)
            project(L2P, w2_sb, 0, AW)
            project(L3P, w_sb, 5 * D, 2 * D)
            pe.wait_ge(y3_ready, 1)
            with pe.Fori(0, ITER) as i:
                for half in range(2):
                    pe.load(tile_regs, tile_i[0:1, bass.ds(i * RING + half * GRP, GRP)])
                    tiles = [pe.snap(r, min_val=0, max_val=NT - 1) for r in tile_regs]
                    pe.wait_ge(mask_ready[SPREAD], i * 2 + (half + 1))
                    pe.wait_ge(same_ready, i * 2 + (half + 1))
                    pe.wait_ge(maskT_ready[SPREAD], i * 4 + (2 * half + 2))
                    for j in range(GRP):
                        mm = pe.matmul(ps[:, j // 4, (j % 4) * P:(j % 4 + 1) * P], mask[:, half, j, :],
                                       same[:, j, :], start=True, stop=True)
                        if j % 4 == 3:
                            mm.then_inc(maskT_full[SPREAD], 1)
                    pe.wait_ge(idx_ready, i * 2 + half)
                    for j in range(GRP):
                        mm = pe.matmul(ps[:, 6, j:j + 1], earlier[:, j, :], ones[:, 0:1], start=True, stop=True)
                    mm.then_inc(dup_full, 1)
                    pe.wait_ge(maskT_ready[SPREAD], i * 4 + (2 * half + 4))
                    for j in range(GRP):
                        pe.wait_ge(row_out, i * RING + (half * GRP + j + 1))
                        pe.matmul(ps[:, 2 + j % 4, 0:SW], maskT[:, j, :],
                                  acc[0][:, bass.ds(tiles[j], 1), 0:SW].rearrange("p a b -> p (a b)"),
                                  start=True, stop=True).then_inc(row_full, 1)

        @block.vector
        def _(v):
            chain = [0]

            def link(ins):
                chain[0] += 1
                ins.then_inc(dve_seq, 1)
                v.wait_ge(dve_seq, chain[0])

            def bias(n, count=1):
                return bias_bc[:, n * D:(n + count) * D]

            def over_tiles(row, tiles=NT):
                return row.unsqueeze(1).to_broadcast([P, tiles, row.shape[-1]])

            v.memset(feat[:, USED - 1:NT, :], 0.0).then_inc(x_tail, 1)
            v.wait_ge(const_ready, 9)
            v.wait_ge(in_edges, 16)
            dst_i = edge_cols[:, 1, :]
            v.tensor_copy(l2_idx[:], edge_cols[:, :, 0:USED])
            v.tensor_single_scalar(lane_of[:, 1:2], lane_of[:, 0:1], H - 1, ALU.bitwise_and)
            v.tensor_single_scalar(lane_of[:, 2:3], lane_of[:, 0:1], 2, ALU.arith_shift_right)
            link(v.tensor_copy(lane_of_f[:, 0:1], lane_of[:, 0:1]))
            link(v.tensor_copy(lane_of_f[:, 1:3], lane_of[:, 1:3]))
            v.tensor_scalar(same_head[:], lane_row, lane_of_f[:, 1:2], None, ALU.is_equal)
            link(v.tensor_scalar(lane[:], iota_d[:, 0:32], lane_of_f[:, 2:3], None, ALU.is_equal))
            v.tensor_single_scalar(dst_parts_i[:, 0, :], dst_i, P - 1, ALU.bitwise_and)
            link(v.tensor_single_scalar(dst_parts_i[:, 1, :], dst_i, 7, ALU.arith_shift_right))
            link(v.tensor_copy(dst_parts, dst_parts_i))
            link(v.tensor_tensor(in_tile, dst_parts[:, 1, :].unsqueeze(2).to_broadcast([P, NW, NT]),
                                 iota_d[:, 0:NT].unsqueeze(1).to_broadcast([P, NW, NT]), ALU.is_equal))
            v.sem_inc(counted, 4)
            with v.Fori(0, NPAIR) as i:
                for group in range(4):
                    v.wait_ge(counted, i * 4 + (group + 1))
                    for j in range(GRP):
                        ins = v.tensor_scalar(at_place[:, group, j, :], iota_b,
                                              dst_parts[:, 0, bass.ds(i * (4 * GRP) + group * GRP + j, 1)],
                                              None, ALU.is_equal)
                    ins.then_inc(place_ready, 1)
            v.wait_ge(deg_full, 1)
            link(v.tensor_copy(deg[:], ps[:, 7, 0:NT]))
            v.sem_inc(deg_ready, 1)
            v.wait_ge(cum_ready, 1)
            link(v.memset(cum[:, 0:1], 0.0))
            link(v.tensor_tensor_scan(cum[:, 1:NT], ones[:, 0:NT - 1], ps[:, 6, 0:NT - 1], 0.0, ALU.mult, ALU.add))
            link(v.tensor_copy(cum_i[:, 0, :], cum[:]))
            link(v.tensor_scalar(cum_i[:, 1, :], cum[:], -1.0, None, ALU.add))
            link(v.tensor_single_scalar(cum_i[:], cum_i[:], 7, ALU.arith_shift_right))
            link(v.tensor_copy(first_row[:], cum_i[:, 0, :]))
            link(v.tensor_copy(last_row[:], cum_i[:, 1, :]))
            U1 = USED
            link(v.tensor_tensor(items[:, 0:U1], last_row[:, 1:U1 + 1], first_row[:, 0:U1], ALU.subtract))
            link(v.tensor_scalar(items[:, 0:U1], items[:, 0:U1], 1.0, None, ALU.add))
            link(v.tensor_tensor(off[:, 0:U1], cum[:, 1:U1 + 1], cum[:, 0:U1], ALU.is_gt))
            link(v.tensor_tensor(items[:, 0:U1], items[:, 0:U1], off[:, 0:U1], ALU.mult))
            link(v.memset(start[:, 0:1], 0.0))
            link(v.tensor_tensor_scan(start[:, 1:U1 + 1], ones[:, 0:U1], items[:, 0:U1], 0.0, ALU.mult, ALU.add))
            link(v.tensor_tensor(off[:, 0:U1], first_row[:, 0:U1], start[:, 0:U1], ALU.subtract))
            link(v.tensor_tensor(doff[:, 1:U1], off[:, 1:U1], off[:, 0:U1 - 1], ALU.subtract))
            shape = [WG, 4, U1 - 1]
            link(v.tensor_tensor(ge[:], wcol[:].unsqueeze(2).to_broadcast(shape),
                                 start[0:WG, 1:U1].unsqueeze(1).to_broadcast(shape), ALU.is_ge))
            link(v.tensor_tensor(geo[:], ge[:], doff[0:WG, 1:U1].unsqueeze(1).to_broadcast(shape), ALU.mult))
            link(v.tensor_reduce(tcol[:], ge[:], X_AXIS, ALU.add))
            link(v.tensor_reduce(jcol[:], geo[:], X_AXIS, ALU.add))
            link(v.tensor_scalar(t128[:], tcol[:], float(P), None, ALU.mult))
            link(v.tensor_tensor(jcol[:], jcol[:], wcol[:], ALU.add))
            link(v.tensor_scalar(jcol[:], jcol[:], off[0:WG, 0:1], -float(PAD_ROW), ALU.add, ALU.add))
            link(v.tensor_scalar(jcol2[:], wcol[:], start[0:WG, U1:U1 + 1], None, ALU.is_lt))
            link(v.tensor_tensor(jcol[:], jcol[:], jcol2[:], ALU.mult))
            v.tensor_scalar(jidx[:], jcol[:], float(PAD_ROW), None, ALU.add).then_inc(jidx_ready, 1)
            for g in range(4):
                ins = v.tensor_scalar(tile_diag[:, g, :], ident[0:WG, 0:WG], tcol[:, g:g + 1], None, ALU.mult)
            ins.then_inc(diag_ready, 1)
            v.wait_ge(deg_rooted, 1)
            v.reciprocal(dinv[:], dsq[:]).then_inc(dinv_ready, 1)
            v.wait_ge(tiles_full, 1)
            tw = tile_row
            link(v.tensor_copy(tw[:], ps[:, 6, 0:NW]))
            link(v.tensor_copy(tile_i[:], tw[0:1, :]))
            v.wait_ge(rows_got, 64)
            link(v.tensor_copy(rows_f[:, :, 0:P], work_i[:, :, 0:P]))
            link(v.tensor_tensor(rows_f[:, :, P:2 * P], work_i[:, :, P:2 * P],
                                 t128[:].unsqueeze(2).to_broadcast([WG, 4, P]), ALU.subtract))
            v.sem_inc(rowsf_ready, 1)

            def evacuate(proj, write):
                base = proj * NT
                with v.Fori(0, NPAIR) as i:
                    for a in range(2):
                        v.wait_ge(projected, i * 2 + (base + a + 3))
                        write(a, lambda t: t[:, bass.ds(i * 2 + a, 1), :].rearrange("p a b -> p (a b)")
                              ).then_inc(evacuated, 1)
                v.wait_ge(evacuated, 2 + base + NT)

            v.wait_ge(dinv_ready, 1)
            v.wait_ge(evacuated, 2 + NT)
            v.tensor_tensor(aux[:, 0:HALF, :], aux[:, 0:HALF, :],
                            dinv[:, 0:HALF].unsqueeze(2).to_broadcast([P, HALF, D]), ALU.mult).then_inc(y0_ready, 1)
            v.wait_ge(rowsT_ready, 1)
            link(v.memset(dstl[:, NW:], -1.0))
            link(v.tensor_copy(dstl[:, 0:NW], ps[:, 5, 0:NW]))
            link(v.tensor_copy(srcT[:], ps[:, 4, 0:NW]))
            v.sem_inc(meta_ready, 1)

            def make_mask(loop, slot, at):
                shape3 = [P, GRP, P]
                return v.tensor_tensor(mask[:, slot, :, :], iota_d[:].unsqueeze(1).to_broadcast(shape3),
                                       dstl[:, at].unsqueeze(2).to_broadcast(shape3),
                                       ALU.is_equal).then_inc(mask_ready[loop], 1)

            def mask_loop(loop, slot_free, per_group, later, group):
                make_mask(loop, 0, slice(0, GRP))
                with v.Fori(0, ITER) as i:
                    for half in range(2):
                        v.wait_ge(slot_free, i * (2 * per_group) + (half * per_group + later))
                        make_mask(loop, 1 - half, bass.ds(i * RING + (half + 1) * GRP, GRP))
                        if group:
                            group(i, half)

            def per_node(col, width=D):
                return col.unsqueeze(2).to_broadcast([P, NT, width])

            v.wait_ge(in_w, 96)
            for k in range(2):
                for side in range(2):
                    link(v.tensor_tensor(prod[:, 0, 0:D], w2_sb[:, k, 0:D], attn_bc[:, 1 - side, :], ALU.mult))
                    link(v.tensor_reduce(w2_sb[:, k, D + side * H:D + (side + 1) * H],
                                         prod[:, 0, 0:D].rearrange("p (h d) -> p h d", d=HD), X_AXIS, ALU.add))
            v.wait_ge(y0_ready, HALF + 1)
            v.wait_ge(rows_stored, 16)
            link(v.tensor_copy(acc[0][:, :, 0:D], aux[:]))
            link(v.tensor_copy(key4,
                               dstl[:, 0:NW].unsqueeze(2).to_broadcast([P, NW, H])))
            v.sem_inc(keys_ready, 1)
            v.wait_ge(block_out, NB)
            by_row = starts[:, 0:NB * P].rearrange("p (b e) -> p b e", e=P)
            link(v.memset(starts[:], -BIG))
            link(v.tensor_tensor(by_row[:, :, 1:P], turnedT[:, :, 0:P - 1], turnedT[:, :, 1:P], ALU.not_equal))
            link(v.tensor_scalar(by_row[:, :, 1:P], by_row[:, :, 1:P], -BIG, None, ALU.mult))

            def spread_ends(rows, n):
                for side, e in enumerate((0, P - 1)):
                    ins = v.tensor_tensor(ends[:, side, :, :], lane[:].unsqueeze(1).to_broadcast([P, NB, 32]),
                                          rows[:, :, e].unsqueeze(2).to_broadcast([P, NB, 32]), ALU.mult)
                ins.then_inc(ends_ready, 1)
                v.wait_ge(ends_spread, n)

            first, last = ps[:, 2, 0:NW], ps[:, 3, 0:NW]
            spread_ends(turnedT, 1)
            link(v.memset(joined[:], 1.0))
            link(v.tensor_copy(one_seg[:], first))
            link(v.tensor_tensor(joined[:, 1:NW], one_seg[:, 1:NW], last[:, 0:NW - 1], ALU.not_equal))
            link(v.tensor_tensor(carry_w, tw[:, 1:NW], tw[:, 0:NW - 1], ALU.not_equal))
            link(v.tensor_tensor(joined[:, 1:NW], joined[:, 1:NW], carry_w, ALU.max))
            link(v.tensor_scalar(joined[:], joined[:], -BIG, None, ALU.mult))
            link(v.tensor_tensor(one_seg[:], one_seg[:], last, ALU.not_equal))
            link(v.tensor_scalar(one_seg[:], one_seg[:], -BIG, None, ALU.mult))
            v.sem_inc(starts_ready, 1)
            link(v.memset(acc[1][:], 0.0))

            tile_regs = [v.alloc_register(f"add_tile{j}") for j in range(GRP)]

            def add_group(loop, i, half, width, full, free, bank):
                v.load(tile_regs, tile_i[0:1, bass.ds(i * RING + half * GRP, GRP)])
                for j in range(GRP):
                    t = v.snap(tile_regs[j], min_val=0, max_val=NT - 1)
                    n = half * GRP + j
                    v.wait_ge(summed[loop], i * RING + (full + n + 1))
                    v.wait_ge(added[loop], i * RING + (free + n - 1))
                    into = acc[j % 2][:, bass.ds(t, 1), 0:width].rearrange("p a b -> p (a b)")
                    v.tensor_tensor(into, into, ps[:, bank(j), 0:width], ALU.add).then_inc(added[loop], 1)

            def aggregate(loop):
                v.sem_inc(added[loop], 8)
                mask_loop(loop, summed[loop], GRP, 2 * GRP,
                          lambda i, half: add_group(loop, i, half, D, RING, 8, lambda j: j))
                v.wait_ge(added[loop], 8 + NW)

            norms = [0]

            def layernorm(src, dst, tiles=NT):
                norms[0] += 1
                for t in range(tiles):
                    ins = v.bn_stats(stats[:, t, :], src[:, t, :])
                link(ins)
                for t in range(tiles):
                    ins = v.bn_aggr(mv[:, t, :], stats[:, t, :])
                link(ins)
                v.sem_inc(var_ready, 1)
                v.wait_ge(rooted, norms[0])
                link(v.reciprocal(rstd[:], sd[:]))
                for t in range(tiles):
                    ins = v.tensor_scalar(dst[:, t, :], src[:, t, :], mv[:, t, 0:1], rstd[:, t:t + 1],
                                          ALU.subtract, ALU.mult)
                link(ins)

            a0, a1 = acc[0][:, :, 0:D], acc[1][:, :, 0:D]
            v.wait_ge(y0_stored, 16)
            aggregate(AGG0)
            link(v.tensor_tensor(a0, a0, a1, ALU.add))
            link(v.tensor_tensor(a0, a0, per_node(dinv[:]), ALU.mult))
            link(v.tensor_tensor(a0, a0, over_tiles(bias(0)), ALU.add))
            link(v.scalar_tensor_tensor(out=a0, in0=a0, scalar=0.0, in1=feat[:], op0=ALU.max, op1=ALU.add))
            layernorm(a0, feat[:])
            v.sem_inc(feat_ready, 1)

            def pair_out(first, second, n):
                def write(a, at):
                    v.tensor_tensor(at(first), ps[:, 2 + a, 0:D], bias(n), ALU.add)
                    return v.tensor_tensor(at(second), ps[:, 2 + a, D:2 * D], bias(n + 1), ALU.add)
                return write

            evacuate(QV, pair_out(a0, a1, 1))
            v.sem_inc(qv_ready, 1)
            evacuate(K, lambda a, at: v.tensor_tensor(at(aux), ps[:, 2 + a, 0:D], bias(3), ALU.add))
            v.sem_inc(ks_ready, 1)

            def scores(i, half):
                for q in range(4):
                    slot = half * GRP + 2 * q
                    for n in range(2):
                        v.wait_ge(got[slot + n], i * 16 + (ITER * 16 + 16))
                    v.wait_ge(k_ready, i * 8 + (4 + half * 4 + q + 1))
                    v.wait_ge(scored, i * 8 + (half * 4 + q + 3))
                    chain_at = i * 8 + (half * 4 + q + 1)
                    v.tensor_tensor(prod[:, q % 2, :].rearrange("p (a b) -> p a b", a=2),
                                    ps[:, 2 + q, :].rearrange("p (a b) -> p a b", a=2),
                                    ring[:, slot:slot + 2, 0:D],
                                    ALU.mult).then_inc(prod_ready, 1)
                    v.wait_ge(prod_ready, chain_at)
                    v.tensor_reduce(score[:, bass.ds(i * RING + slot, 2), :].rearrange("p a h -> p (a h)"),
                                    prod[:, q % 2, :].rearrange("p (g d) -> p g d", d=HD), X_AXIS,
                                    ALU.add).then_inc(scored, 1)

            v.sem_inc(scored, 4)
            mask_loop(SCORE, maskT_full[SCORE], 2, 0, scores)
            v.wait_ge(scored, 4 + NW // 2)
            v.wait_ge(qv_stored, 32)
            v.wait_ge(block_out, 2 * NB)
            flat = lambda t: t.rearrange("p g e -> p (g e)")

            def row_maxima(values):
                link(v.tensor_tensor_scan(flat(runT), starts[:, 0:NB * P], flat(values), -BIG, ALU.add, ALU.max))
                link(v.tensor_tensor_scan(flat(runT)[:, ::-1], starts[:, 1:][:, ::-1], flat(runT)[:, ::-1], -BIG,
                                          ALU.add, ALU.max))

            row_maxima(turnedT)
            spread_ends(runT, 2)
            link(v.tensor_tensor(carry[:, 0, :], joined[:, 0:NW], one_seg[:], ALU.add))
            link(v.tensor_tensor(carry[:, 1, :], joined[:, 1:], one_seg[:], ALU.add))
            link(v.tensor_tensor_scan(carried[:, 0, :], carry[:, 0, :], last, -BIG, ALU.add, ALU.max))
            link(v.tensor_copy(carry[:, 0, :], first))
            link(v.tensor_tensor_scan(carried[:, 1, ::-1], carry[:, 1, ::-1], carry[:, 0, ::-1], -BIG,
                                      ALU.add, ALU.max))
            link(v.memset(carry, -BIG))
            link(v.tensor_tensor(carry[:, 0, 1:NW], carried[:, 0, 0:NW - 1], joined[:, 1:NW], ALU.add))
            link(v.tensor_tensor(carry[:, 1, 0:NW - 1], carried[:, 1, 1:NW], joined[:, 1:NW], ALU.add))
            for side in range(2):
                ins = v.tensor_tensor(placed[:, side, :, :], lane[:].unsqueeze(1).to_broadcast([P, NB, 32]),
                                      carry[:, side, :].rearrange("p (b n) -> p b n", n=32), ALU.mult)
            link(ins)
            link(v.tensor_reduce(carry_in.rearrange("p s b -> p (s b)"),
                                 placed.rearrange("p s b n -> p (s b) n"), X_AXIS, ALU.add))
            for side, e in enumerate((0, P - 1)):
                ins = v.tensor_tensor(runT[:, :, e], runT[:, :, e], carry_in[:, side, :], ALU.max)
            link(ins)
            row_maxima(runT)
            link(v.tensor_tensor(turnedT, turnedT, runT, ALU.subtract))
            v.sem_inc(less_m, 1)
            v.wait_ge(block_out, 3 * NB)
            link(v.memset(acc[0][:], 0.0))
            link(v.memset(acc[1][:], 0.0))

            def attend(i, half):
                at = i * RING + half * GRP
                for n in range(GRP):
                    v.wait_ge(got[half * GRP + n], i * 16 + (2 * ITER * 16 + 16))
                    if n == 0:
                        v.tensor_copy(ring[:, half * GRP:(half + 1) * GRP, D:D + H],
                                      score[:, bass.ds(at, GRP), :])
                    if n % 2 == 1:
                        slot = half * GRP + n - 1
                        rows = ring[:, slot:slot + 2, 0:D].rearrange("p w (h d) -> p w h d", d=HD)
                        v.tensor_tensor(rows, rows,
                                        score[:, bass.ds(i * RING + slot, 2), :].unsqueeze(3)
                                        .to_broadcast([P, 2, H, HD]), ALU.mult).then_inc(ev_ready, 1)
                add_group(ATT, i, half, D + H, RING, 4, lambda j: 4 + j % 4)

            v.sem_inc(added[ATT], 4)
            mask_loop(ATT, summed[ATT], GRP, 2 * GRP, attend)
            v.wait_ge(added[ATT], 4 + NW)
            v.wait_ge(evacuated, 2 + (SKIP + 1) * NT)
            heads = lambda t: t.rearrange("p t (h d) -> p t h d", d=HD)
            link(v.tensor_tensor(acc[0][:, :, 0:D + H], acc[0][:, :, 0:D + H], acc[1][:, :, 0:D + H], ALU.add))
            link(v.tensor_scalar(den4[:], acc[0][:, :, D:D + H], 1e-30, None, ALU.max))
            link(v.reciprocal(den4[:], den4[:]))
            for h in range(H):
                ins = v.tensor_tensor(a0[:, :, h * HD:(h + 1) * HD], a0[:, :, h * HD:(h + 1) * HD],
                                      per_node(den4[:, :, h], HD), ALU.mult)
            link(ins)
            link(v.tensor_tensor(wgate_bc[:, 0:D], wgate_bc[:, 0:D], wgate_bc[:, 2 * D:3 * D], ALU.add))
            link(v.tensor_tensor(wgate_bc[:, D:2 * D], wgate_bc[:, D:2 * D], wgate_bc[:, 2 * D:3 * D],
                                 ALU.subtract))
            link(v.tensor_tensor(a1, aux[:], over_tiles(wgate_bc[:, 0:D]), ALU.mult))
            link(v.tensor_reduce(small[:, 0, :], a1, X_AXIS, ALU.add))
            link(v.tensor_tensor(a1, a0, over_tiles(wgate_bc[:, D:2 * D]), ALU.mult))
            link(v.tensor_reduce(small[:, 1, :], a1, X_AXIS, ALU.add))
            link(v.tensor_tensor(small[:, 0, :], small[:, 0, :], small[:, 1, :], ALU.add))
            v.sem_inc(logit_ready, 1)
            link(v.tensor_tensor(aux[:], aux[:], a0, ALU.subtract))
            v.wait_ge(gate_ready, 1)
            link(v.tensor_tensor(aux[:], aux[:], per_node(small[:, 2, :]), ALU.mult))
            link(v.tensor_tensor(a0, a0, aux[:], ALU.add))
            layernorm(a0, a0)
            link(v.tensor_tensor(a0, a0, over_tiles(bias(5)), ALU.mult))
            link(v.tensor_tensor(a0, a0, over_tiles(bias(6)), ALU.add))
            link(v.tensor_scalar(aux[:], a0, 0.0, scal_bc[:, 0:1], ALU.min, ALU.mult))
            link(v.scalar_tensor_tensor(out=a0, in0=a0, scalar=0.0, in1=aux[:], op0=ALU.max, op1=ALU.add))
            link(v.tensor_tensor(a0, a0, feat[:], ALU.add))
            layernorm(a0, feat[:])
            v.sem_inc(feat_ready, 1)
            evacuate(L2P, lambda a, at: v.tensor_copy(at(acc[0]), ps[:, 2 + a, 0:AW]))
            v.sem_inc(l2_ready, 1)
            v.wait_ge(l2_got, 2 * USED * 16)
            link(v.memset(acc[1][:, USED:, :], 0.0))
            link(v.memset(ral[:, USED:, :], 0.0))
            link(v.tensor_tensor(ral[:], ral[:], acc[1][:, :, D:D + H], ALU.add))
            link(v.tensor_scalar(alpha[:], ral[:], 0.0, 0.01, ALU.min, ALU.mult))
            link(v.scalar_tensor_tensor(out=ral[:], in0=ral[:], scalar=0.0, in1=alpha[:], op0=ALU.max, op1=ALU.add))
            link(v.tensor_reduce(small[:, 3, :], ral[:], X_AXIS, ALU.max))
            link(v.tensor_tensor(ral[:], ral[:], per_node(small[:, 3, :], H), ALU.subtract))
            v.sem_inc(l2_logits, 1)
            v.wait_ge(l2_exps, 1)
            link(v.tensor_reduce(small[:, 3, :], alpha[:], X_AXIS, ALU.add))
            link(v.reciprocal(small[:, 3, :], small[:, 3, :]))
            link(v.tensor_tensor(alpha[:], alpha[:], per_node(small[:, 3, :], H), ALU.mult))
            for h in range(H):
                ins = v.tensor_tensor(a1[:, :, h * HD:(h + 1) * HD], a1[:, :, h * HD:(h + 1) * HD],
                                      per_node(alpha[:, :, h], HD), ALU.mult)
            link(ins)
            link(v.tensor_reduce(tmp64, a1.rearrange("p t (h d) -> p t d h", d=HD), X_AXIS, ALU.add))
            for h in range(H):
                ins = v.tensor_tensor(aux[:, :, h * HD:(h + 1) * HD], feat[:, :, h * HD:(h + 1) * HD],
                                      tmp64, ALU.add)
            link(ins)
            layernorm(aux[:], feat[:])
            v.sem_inc(feat_ready, 1)
            link(v.tensor_tensor(bias(7), bias(7), bias(8), ALU.add))
            v.wait_ge(l2_stored, 32)

            acc0_features = acc[0][:, :, 0:D]

            def l3_out(a, at):
                v.tensor_copy(at(acc0_features), ps[:, 2 + a, 0:D])
                return v.tensor_tensor(at(aux), ps[:, 2 + a, D:2 * D], bias(7), ALU.add)

            evacuate(L3P, l3_out)
            link(v.memset(acc[0][:, :, D:SW], 1.0))
            link(v.memset(srcf[:, NW:], 0.0))
            link(v.tensor_copy(srcf[:, 0:NW], srcT[:]))
            v.sem_inc(y3_ready, 1)
            v.sem_inc(srcf_ready, 1)
            v.wait_ge(tri_ready, 1)
            shape3 = [P, GRP, P]

            def make_same(side, at):
                v.tensor_tensor(same, src_row[:, side, :, :], srcf[:, at].unsqueeze(2).to_broadcast(shape3),
                                ALU.is_equal).then_inc(same_made, 1)

            v.wait_ge(row_in[0], 16)
            make_same(0, slice(0, GRP))
            v.wait_ge(same_made, 1)
            v.tensor_tensor(earlier, same, before_tri.unsqueeze(1).to_broadcast(shape3),
                            ALU.mult).then_inc(same_ready, 1)

            def spread(i, half):
                v.wait_ge(dup_full, i * 2 + (half + 1))
                v.wait_ge(row_in[1 - half], i * 16 + 16 * (half + 1))
                make_same(1 - half, bass.ds(i * RING + (half + 1) * GRP, GRP))
                at = bass.ds(i * RING + half * GRP, GRP)
                v.tensor_scalar(to_spare, srcf[:, at], -1.0, spare_row[:, 0:1], ALU.mult,
                                ALU.add).then_inc(idx_steps, 1)
                v.wait_ge(idx_steps, i * 4 + (half * 2 + 1))
                v.scalar_tensor_tensor(out=to_spare2, in0=ps[:, 6, 0:GRP], scalar=0.5, in1=to_spare,
                                       op0=ALU.is_gt, op1=ALU.mult).then_inc(idx_steps, 1)
                v.wait_ge(same_made, i * 2 + (half + 2))
                v.tensor_tensor(earlier, same, before_tri.unsqueeze(1).to_broadcast(shape3),
                                ALU.mult).then_inc(same_ready, 1)
                v.wait_ge(idx_steps, i * 4 + (half * 2 + 2))
                v.wait_ge(group_in, i * 2 + half)
                v.tensor_tensor(idx_stage[:, half, :], srcf[:, at], to_spare2, ALU.add).then_inc(idx_ready, 1)

            mask_loop(SPREAD, dup_full, 1, 0, spread)
            for c in range(2):
                nodes = slice(c * HALF, (c + 1) * HALF)
                v.wait_ge(read_back[c], 16 * TABLES)
                total = part(0)[:, :, 0:SW]
                for n in range(1, TABLES):
                    link(v.tensor_tensor(total, total, part(n)[:, :, 0:SW], ALU.add))
                v.sem_inc(chunk_used, 1)
                link(v.tensor_scalar(rcnt[:, nodes], total[:, :, D], 1.0, None, ALU.max))
                link(v.reciprocal(rcnt[:, nodes], rcnt[:, nodes]))
                mean = total[:, :, 0:D]
                link(v.tensor_tensor(mean, mean, rcnt[:, nodes].unsqueeze(2).to_broadcast([P, HALF, D]), ALU.mult))
                link(v.tensor_tensor(mean, mean, aux[:, nodes, :], ALU.add))
                link(v.tensor_tensor(mean, mean, feat[:, nodes, :], ALU.add))
                layernorm(mean, feat[:, nodes, :], HALF)
                v.sem_inc(out_ready, 1)
                v.sem_inc(chunk_used, 1)


def kernel(**inputs):
    import numpy as np
    import concourse.bacc as bacc
    from concourse.bass_utils import run_bass_kernel_spmd

    f = {k: np.asarray(v) for k, v in inputs.items()}
    rows = np.zeros((ROWS, 2, P), np.int32)
    rows[:, 1, :] = PAD_DST
    for side, name in enumerate(("src", "dst")):
        whole = E // P
        rows[:whole, side, :] = f[name][:whole * P].reshape(whole, P)
        rows[whole, side, :E - whole * P] = f[name][whole * P:]
    cols = np.zeros((P, 2, NW), np.int32)
    cols[:, 1, :] = PAD_DST
    cols[:, :, :ROWS] = rows.transpose(2, 1, 0)
    w_all = np.concatenate([f["L0_gnn_W"], f["L1_gnn_Wq"].T, f["L1_gnn_Wv"].T, f["L1_gnn_Wk"].T,
                            f["L1_gnn_Wskip"].T, f["L3_gnn_W2"].T, f["L3_gnn_W1"].T], axis=1)
    bias = np.concatenate([f[n] for n in ("L0_gnn_b", "L1_gnn_bq", "L1_gnn_bv", "L1_gnn_bk", "L1_gnn_bskip",
                                          "L1_gnn_ln_w", "L1_gnn_ln_b", "L3_gnn_b1", "L3_gnn_b2")])
    arrays = {
        "x": f["x"], "edges": rows.reshape(ROWS, 2 * P), "edges_t": cols, "w_all": w_all, "w_l2": f["L2_gnn_weight"],
        "bias": bias,
        "attn": np.concatenate([f["L2_gnn_attn_l"].reshape(-1), f["L2_gnn_attn_r"].reshape(-1)]),
        "wgate": f["L1_gnn_Wgate"].reshape(-1),
        "scalars": np.concatenate([f["L1_gnn_prelu_a"].reshape(1), f["L1_gnn_bgate"].reshape(1)]),
    }
    arrays = {k: np.ascontiguousarray(a) for k, a in arrays.items()}
    nc = bacc.Bacc("TRN2", target_bir_lowering=False, num_devices=1)
    aps = [nc.dram_tensor(k, a.shape, mybir.dt.from_np(a.dtype), kind="ExternalInput").ap()
           for k, a in arrays.items()]
    out = nc.dram_tensor("out", (N, D), F32, kind="ExternalOutput").ap()
    gnn_kernel(nc, *aps, out)
    return run_bass_kernel_spmd(nc, [arrays], core_ids=[0]).results[0]["out"]
```

```python
from contextlib import ExitStack

import concourse.bass as bass
from concourse import mybir

F32 = mybir.dt.float32
BF16 = mybir.dt.bfloat16
I32 = mybir.dt.int32
ALU = mybir.AluOpType
ACT = mybir.ActivationFunctionType
X_AXIS = mybir.AxisListType.X

P = 128
N = 3125
E = 50000
D = 256
H = 4
HD = D // H
NT = 26
USED = -(-N // P)
TAIL = N - (USED - 1) * P
ROWS = 392
FULL_ROWS = E // P
PAD_ROW = ROWS - 1
PAD_DST = 1 << 20
NW = 416
WG = 104
GRP = 8
RING = 2 * GRP
ITER = NW // RING
AW = D + 2 * H
BIG = 1.0e30
EPS = 1e-5
NPAIR = NT // 2
TABLES = 4
SW = D + 1


def ds(at, count):
    return slice(at, at + count) if isinstance(at, int) else bass.ds(at, count)


def pipeline(engine, steps):
    lead, lag = max(a for a, _ in steps), min(a for a, _ in steps)

    def peeled(rounds):
        for i in rounds:
            for ahead, step in steps:
                if 0 <= i + ahead < NPAIR:
                    step(i + ahead)

    peeled(range(-lead, -lag))
    with engine.Fori(0, NPAIR - lead + lag) as i:
        for ahead, step in steps:
            step(i + (ahead - lag))
    peeled(range(NPAIR - lead, NPAIR - lag))


def gnn_kernel(nc, x, edges, edges_t, w_all, w_l2, bias, attn, wgate, scalars, out):
    ctx = ExitStack()
    with ctx:
        def sb(name, shape, dt=F32):
            return ctx.enter_context(nc.sbuf_tensor(name, shape, dt))

        def sem(name):
            return ctx.enter_context(nc.semaphore(name))

        def table(name, width):
            return nc.dram_tensor(name, [NT * P, width], F32).ap()

        y0_table = table("y0_table", D)
        q_table = table("q_table", D)
        v_table = table("v_table", D)
        l2_table = table("l2_table", AW)
        al_table = table("al_table", H)
        sums = [nc.dram_tensor(f"sums{n}", [NT * P + P, SW], F32).ap() for n in range(TABLES)]
        edge_rows = nc.dram_tensor("edge_rows", [ROWS, 2 * P], I32).ap()
        src_rows = nc.dram_tensor("src_rows", [NW, P], F32).ap()

        feat = sb("feat", [P, NT, D])
        acc = [sb(f"acc{n}", [P, NT, AW]) for n in range(2)]
        aux = sb("aux", [P, NT, D])
        ring = sb("ring", [P, RING, D + H])
        mask = sb("mask", [P, 2, GRP, P])
        maskT = sb("maskT", [P, GRP, P])
        pairs = sb("pairs", [P, 2 * GRP * P])
        w_sb = sb("w_sb", [P, 2, 7 * D])
        w2_sb = sb("w2_sb", [P, 2, AW])
        bias_bc = sb("bias_bc", [P, 9 * D])
        wgate_bc = sb("wgate_bc", [P, 3 * D])
        scal_bc = sb("scal_bc", [P, 2])
        stage = sb("stage", [P, 2, D])
        xT = sb("xT", [P, 2, 2, P])
        ident = sb("ident", [P, P])
        ones = sb("ones", [P, P])
        iota_d = sb("iota_d", [P, P])
        wcol = sb("wcol", [WG, 4])
        cum = sb("cum", [P, NT])
        cum_i = sb("cum_i", [P, 2, NT], I32)
        first_row = sb("first_row", [P, NT])
        last_row = sb("last_row", [P, NT])
        items = sb("items", [P, NT])
        start = sb("start", [P, NT])
        off = sb("off", [P, NT])
        doff = sb("doff", [P, NT])
        falls_of = sb("falls_of", [P, 1])
        unsorted_i = sb("unsorted_i", [1, 2], I32)
        ge = sb("ge", [WG, 4, USED - 1])
        geo = sb("geo", [WG, 4, USED - 1])
        tcol = sb("tcol", [WG, 4])
        t128 = sb("t128", [WG, 4])
        jcol = sb("jcol", [WG, 4])
        jcol2 = sb("jcol2", [WG, 4])
        jidx = sb("jidx", [WG, 4], I32)
        tile_i = sb("tile_i", [1, NW], I32)
        srcT = sb("srcT", [P, NW], I32)
        dstl = sb("dstl", [P, NW + GRP])
        idx_stage = sb("idx_stage", [P, 2, GRP], I32)
        l2_idx = sb("l2_idx", [P, 2, USED], I32)
        deg = sb("deg", [P, NT])
        dsq = sb("dsq", [P, NT])
        dinv = sb("dinv", [P, NT])
        rcnt = sb("rcnt", [P, NT])
        starts = sb("starts", [P, NW * P // 32 + 1])
        joined = sb("joined", [P, NW + 1])
        one_seg = sb("one_seg", [P, NW])
        lane = sb("lane", [P, 32])
        same_head = sb("same_head", [P, P])
        score = sb("score", [P, NW, H])
        stats = sb("stats", [P, NT, 6])
        mv = sb("mv", [P, NT, 2])
        sd = sb("sd", [P, NT])
        rstd = sb("rstd", [P, NT])
        less_mean = sb("less_mean", [P, NT])
        feature_sums = sb("feature_sums", [P, 2])
        square_sums = sb("square_sums", [P, 2])
        skip_logit = sb("skip_logit", [P, NT])
        skip_gate = sb("skip_gate", [P, 3])
        agg_logit = sb("agg_logit", [P, 2])
        gate = sb("gate", [P, NT])
        less_slope = sb("less_slope", [P, 1])
        shift = sb("shift", [P, NT])
        small = sb("small", [P, 4, NT])
        ral = sb("ral", [P, NT, H])
        alpha = sb("alpha", [P, NT, H])
        den4 = sb("den4", [P, NT, H])
        eps_col = sb("eps_col", [P, 1])
        small_idx = sb("small_idx", [P, 2, GRP])
        to_spare = small_idx[:, 0, :]
        to_spare2 = small_idx[:, 1, :]
        tile_row = sb("tile_row", [P, NW])
        spare_row = sb("spare_row", [P, 1])

        def within(tensor, at, shape, dt=F32):
            words = 1
            for n in shape[1:]:
                words *= n
            flat = tensor[:] if len(tensor.shape) == 2 else tensor[:].rearrange("p t f -> p (t f)")
            flat = flat[0:shape[0], at:at + words]
            flat = flat if dt == F32 else flat.bitcast(dt)
            names = "xyz"[:len(shape) - 1]
            sizes = dict(zip(names, shape[1:]))
            sizes.pop(names[0])
            return flat.rearrange(f"p ({' '.join(names)}) -> p {' '.join(names)}", **sizes) if len(names) > 1 else flat

        NB = NW // 32
        runs_i = within(pairs, 0, [ROWS // 4, 8 * P + 2], I32)
        runs_f = within(pairs, 8 * P + 2, [ROWS // 4, 4 * P + 1])
        falls = within(acc[0], 0, [ROWS // 4, 4 * P])
        row_i = within(acc[1], 0, [P, 2 * P], I32)
        row_f = within(acc[1], 2 * P, [P, P])
        place_i = within(acc[1], 3 * P, [P, P], I32)
        place_f = within(acc[1], 4 * P, [P, P])
        place_hotT = within(acc[1], 5 * P, [P, P])
        place_hot = within(acc[1], 6 * P, [P, P])
        tile_hot = within(acc[1], 7 * P, [P, NT])
        is_before = within(acc[1], 8 * P, [P, P])
        is_after = within(acc[1], 9 * P, [P, P])
        early_of = within(acc[1], 10 * P, [P, P])
        next_rank = within(acc[1], 11 * P, [P, NT])
        rank_of = within(acc[1], 12 * P, [P, NT])
        dst_cols = within(acc[1], 13 * P, [P, NW])
        rank_f = within(acc[1], 17 * P, [P, 2])
        rank_i = within(acc[1], 17 * P + 2, [P, 1], I32)
        pair_i = within(acc[1], 17 * P + 4, [P, 2], I32)
        rows_f = within(acc[0], 1024, [WG, 4, 2 * P])
        work_i = within(acc[0], 2048, [WG, 4, 2 * P], I32)
        attn_bc = within(acc[0], 3072, [P, 2, D])
        dst_parts_i = within(acc[0], 3584, [P, 2, NW], I32)
        dst_parts = within(acc[0], 4416, [P, 2, NW])
        tile_diag = within(acc[0], 5248, [WG, 4, WG])
        lane_of = within(acc[0], 5664, [P, 4], I32)
        lane_of_f = within(acc[0], 5668, [P, 4])
        lane_row = within(acc[0], 5672, [P, P])
        in_tile = acc[1][:].rearrange("p t f -> p (t f)")[:, 0:NW * NT // 2].bitcast(BF16).rearrange(
            "p (j c) -> p j c", c=NT)
        edge_cols = within(ring, 0, [P, 2, NW], I32)
        iota_b = within(ring, 2 * NW, [P, P // 2]).bitcast(BF16)
        zero_b = within(ring, 2 * NW + P // 2, [P, P // 2]).bitcast(BF16)
        at_place = mask[:].rearrange("p s g d -> p (s g d)").bitcast(BF16).rearrange(
            "p (s g d) -> p s g d", s=4, g=GRP)
        turnedT = within(acc[1], 0, [P, NB, P])
        runT = within(acc[1], 1664, [P, NB, P])
        ends = within(acc[1], 3328, [P, 2, NB, 32])
        carry_w = within(acc[1], 4160, [P, NW - 1])
        key4 = within(acc[1], 4992, [P, NW, H])
        carry = within(acc[0], 0, [P, 2, NW])
        carried = within(acc[0], 2 * NW, [P, 2, NW])
        placed = within(acc[0], 4 * NW, [P, 2, NB, 32])
        carry_in = within(acc[0], 6 * NW, [P, 2, NB])
        two_heads = within(pairs, 4 * D, [P, 2, 2 * HD])
        head_sum = within(pairs, 5 * D, [P, 2, HD])
        prod = within(pairs, 0, [P, 2, 2 * D])
        same = within(pairs, 0, [P, GRP, P])
        earlier = within(pairs, GRP * P, [P, GRP, P])
        src_row = within(w_sb, 0, [P, 2, GRP, P])
        srcf = within(w_sb, 2 * GRP * P, [P, NW + GRP])
        before_tri = within(w_sb, 2 * GRP * P + NW + GRP, [P, P])
        zeros = within(maskT, 0, [P, SW])
        ps = ctx.enter_context(nc.psum_tensor("ps", [P, 8, 512], F32))
        ps_flat = ps[:].rearrange("p b c -> p (b c)")

        in_edges, in_x, in_w, in_w0 = sem("in_edges"), sem("in_x"), sem("in_w"), sem("in_w0")
        rows_got, l2_got, out_stored = sem("rows_got"), sem("l2_got"), sem("out_stored")
        y0_stored, q_stored, v_stored = sem("y0_stored"), sem("q_stored"), sem("v_stored")
        l2_stored, rows_stored = sem("l2_stored"), sem("rows_stored")
        zeros_ready, cleared = sem("zeros_ready"), sem("cleared")
        row_in = [sem(f"row_in{n}") for n in range(2)]
        summed_in = [sem(f"summed_in{n}") for n in range(TABLES)]
        read_back = [sem(f"read_back{n}") for n in range(4)]
        got = [sem(f"got{n}") for n in range(RING)]
        const_ready, x_tail, ones_ready = sem("const_ready"), sem("x_tail"), sem("ones_ready")
        cum_ready, jidx_ready = sem("cum_ready"), sem("jidx_ready")
        rowsf_ready, rowsT_ready, meta_ready = sem("rowsf_ready"), sem("rowsT_ready"), sem("meta_ready")
        deg_ready, deg_rooted = sem("deg_ready"), sem("deg_rooted")
        var_ready, rooted = sem("var_ready"), sem("rooted")
        l2_logits, l2_exps = sem("l2_logits"), sem("l2_exps")
        y0_ready, y0_first = sem("y0_ready"), sem("y0_first")
        y3_ready, out_ready = sem("y3_ready"), sem("out_ready")
        dinv_ready, loops_in, attn_used = sem("dinv_ready"), sem("loops_in"), sem("attn_used")
        runs_cleared, in_runs, falls_ready = sem("runs_cleared"), sem("in_runs"), sem("falls_ready")
        order_known, rows_copied = sem("order_known"), sem("rows_copied")
        tris_ready, ranks_full, ranks_out = sem("tris_ready"), sem("ranks_full"), sem("ranks_out")
        row_loaded, row_seen, hots_ready = sem("row_loaded"), sem("row_seen"), sem("hots_ready")
        looked_up, rank_ready, edge_put = sem("looked_up"), sem("rank_ready"), sem("edge_put")
        place_ready, counted, deg_full = sem("place_ready"), sem("counted"), sem("deg_full")
        diag_ready, tiles_full = sem("diag_ready"), sem("tiles_full")
        keys_ready, ends_ready, ends_spread = sem("keys_ready"), sem("ends_ready"), sem("ends_spread")
        starts_ready = sem("starts_ready")
        less_m, exps_ready = sem("less_m"), sem("exps_ready")
        dve_seq = sem("dve_seq")
        pool_steps = sem("pool_steps")
        idx_staged = sem("idx_staged")
        staged = sem("staged")
        turned = sem("turned")
        xT_ready = sem("xT_ready")
        projected = sem("projected")
        evacuated = sem("evacuated")
        merged, relued, summed_up = sem("merged"), sem("relued"), sem("summed_up")
        mean_made, squared, sd_made = sem("mean_made"), sem("squared"), sem("sd_made")
        gate_in_made, gate_made, differed = sem("gate_in_made"), sem("gate_made"), sem("differed")
        agg_made, agg_merged, logits_made = sem("agg_made"), sem("agg_merged"), sem("logits_made")
        normed, weighted, biased = sem("normed"), sem("weighted"), sem("biased")
        negated, rectified, dens_ready = sem("negated"), sem("rectified"), sem("dens_ready")
        attended, heads_summed, y3_out = sem("attended"), sem("heads_summed"), sem("y3_out")
        rstd_made, scale_made, kept = sem("rstd_made"), sem("scale_made"), sem("kept")
        block_turned, block_out = sem("block_turned"), sem("block_out")
        AGG0, SCORE, ATT, SPREAD = range(4)
        mask_ready = [sem(f"mask_ready{n}") for n in range(4)]
        summed = {n: sem(f"summed{n}") for n in (AGG0, ATT)}
        added = {n: sem(f"added{n}") for n in (AGG0, ATT)}
        maskT_full = {n: sem(f"maskT_full{n}") for n in (SCORE, SPREAD)}
        maskT_ready = {n: sem(f"maskT_ready{n}") for n in (SCORE, SPREAD)}
        prod_ready = sem("prod_ready")
        skip_gate_ready = sem("skip_gate_ready")
        k_ready, scored = sem("k_ready"), sem("scored")
        ev_ready = sem("ev_ready")

        same_made, idx_steps = sem("same_made"), sem("idx_steps")
        same_ready, dup_full, idx_ready = sem("same_ready"), sem("dup_full"), sem("idx_ready")
        row_full, row_out, group_in = sem("row_full"), sem("row_out"), sem("group_in")
        chunk_used, tri_ready, srcf_ready = sem("chunk_used"), sem("tri_ready"), sem("srcf_ready")

        XW, Q, K, V, SKIP, L2P, L3P = range(7)
        NGRP = NW // GRP
        GATHERS = [AGG0, SCORE, ATT]

        squares = within(pairs, 2 * D, [P, 2, D])
        HALF = NT // 2

        def one(t, tile):
            return t[:, ds(tile, 1), 0:D].rearrange("p a b -> p (a b)")

        def two(t, p, width=D):
            return t[:, ds(p * 2, 2), 0:width]

        edges_of = [0, (HALF + 1) // 2, HALF, HALF + (HALF + 1) // 2, NT]
        CHUNKS = list(zip(edges_of, edges_of[1:]))

        def chunk_of(n, c):
            first, last = CHUNKS[c]
            at = (n % 2) * HALF + CHUNKS[c % 2][0]
            return acc[n // 2][:, at:at + last - first, :]

        block = ctx.enter_context(nc.Block())

        def make_places(engine, i, group):
            shape3 = [P, GRP, P]
            return engine.tensor_tensor(
                at_place[:, group, :, :], iota_b.unsqueeze(1).to_broadcast(shape3),
                dst_parts[:, 0, bass.ds(i * (4 * GRP) + group * GRP, GRP)].unsqueeze(2).to_broadcast(shape3),
                ALU.is_equal)

        @block.sync
        def _(sp):
            sp.dma_start(edge_cols, edges_t).then_inc(in_edges, 16)
            sp.dma_start(feat[:, 0:USED - 1, :],
                         x[0:(USED - 1) * P, :].rearrange("(t p) f -> p t f", p=P)).then_inc(in_x, 16)
            sp.wait_ge(runs_cleared, 1)
            sp.dma_start(runs_i[:, 0:8 * P], edges.rearrange("(p r) e -> p (r e)", r=4)).then_inc(in_runs, 16)
            with nc.allow_non_contiguous_dma(reason="97 edges, once"):
                sp.dma_start(runs_i[0:ROWS // 4 - 1, 8 * P:], edges[4:ROWS, 0:2].rearrange("(p r) e -> p r e", r=4)
                             [:, 0, :]).then_inc(in_runs, 16)
            sp.dma_start(edge_rows, edges).then_inc(rows_copied, 16)
            sp.wait_ge(x_tail, 1)
            sp.dma_start(feat[0:TAIL, USED - 1, :], x[(USED - 1) * P:N, :]).then_inc(in_x, 16)
            sp.dma_start(w_sb[:, :, 0:D], w_all[:, 0:D].rearrange("(k p) n -> p k n", p=P)).then_inc(in_w0, 16)
            sp.dma_start(w_sb[:, :, D:], w_all[:, D:].rearrange("(k p) n -> p k n", p=P)).then_inc(in_w, 16)
            sp.dma_start(w2_sb[:, :, 0:D], w_l2.rearrange("(k p) n -> p k n", p=P)).then_inc(in_w, 16)
            sp.dma_start(bias_bc[:], bias.partition_broadcast(P)).then_inc(in_w, 16)
            sp.dma_start(attn_bc.rearrange("p a b -> p (a b)"), attn.partition_broadcast(P)).then_inc(in_w, 16)
            sp.dma_start(wgate_bc[:], wgate.partition_broadcast(P)).then_inc(in_w, 16)
            sp.dma_start(scal_bc[:], scalars.partition_broadcast(P)).then_inc(in_w, 16)
            def store(table_ap, src, done):
                sp.dma_start(table_ap.rearrange("(t p) f -> p t f", p=P), src).then_inc(done, 16)

            sp.wait_ge(zeros_ready, 1)
            for t in sums:
                sp.dma_start(t.rearrange("(t p) f -> p t f", p=P),
                             zeros.unsqueeze(1).to_broadcast([P, NT + 1, SW])).then_inc(cleared, 16)
            y0_tiles = y0_table.rearrange("(t p) f -> p t f", p=P)
            sp.wait_ge(y0_first, 1)
            sp.dma_start(y0_tiles[:, 0:HALF, :], aux[:, 0:HALF, :]).then_inc(y0_stored, 16)
            sp.wait_ge(y0_ready, HALF)
            sp.dma_start(y0_tiles[:, HALF:, :], aux[:, HALF:, :]).then_inc(y0_stored, 16)
            sp.wait_ge(order_known, 1)
            unsorted = sp.alloc_register("sp_unsorted")
            sp.load(unsorted, unsorted_i[0:1, 0:1])
            with sp.If_ne(unsorted, 0):
                def load_row(row):
                    sp.dma_start(row_i, edges[row, :].rearrange("r e -> (r e)").partition_broadcast(P)
                                 ).then_inc(row_loaded, 16)

                with sp.Fori(0, FULL_ROWS) as j:
                    sp.wait_ge(row_seen, j + 1)
                    load_row(bass.ds(j, 1))
                sp.wait_ge(row_seen, FULL_ROWS + 1)
                load_row(slice(FULL_ROWS, FULL_ROWS + 1))
            sp.wait_ge(rowsf_ready, 1)
            sp.dma_start(src_rows.rearrange("(g p) e -> p g e", p=WG), rows_f[:, :, 0:P]).then_inc(rows_stored, 16)

            with sp.Fori(0, NPAIR) as p:
                sp.wait_ge(evacuated, p * 2 + (Q * NT + 4))
                sp.dma_start(q_table.rearrange("(t p) f -> p t f", p=P)[:, bass.ds(p * 2, 2), :],
                             acc[0][:, bass.ds(p * 2, 2), 0:D]).then_inc(q_stored, 16)
            with sp.Fori(0, NT) as t:
                sp.wait_ge(evacuated, t + (V * NT + 3))
                sp.dma_start(v_table.rearrange("(t p) f -> p t f", p=P)[:, bass.ds(t, 1), :],
                             acc[1][:, bass.ds(t, 1), 0:D]).then_inc(v_stored, 16)
            with sp.Fori(0, NPAIR) as p:
                sp.wait_ge(evacuated, p * 2 + (L2P * NT + 4))
                sp.dma_start(l2_table.rearrange("(t p) f -> p t f", p=P)[:, bass.ds(p * 2, 2), :],
                             acc[0][:, bass.ds(p * 2, 2), :]).then_inc(l2_stored, 16)
            with nc.allow_non_contiguous_dma(reason="16 bytes of each node, once"):
                store(al_table, acc[0][:, :, D + H:AW], l2_stored)
            def load_sources(start_row, half):
                sp.dma_start(src_row[:, half, :, :].rearrange("p w e -> p (w e)"),
                             src_rows[start_row, :].rearrange("w e -> (w e)").partition_broadcast(P)
                             ).then_inc(row_in[half], 16)

            sp.wait_ge(srcf_ready, 1)
            sp.wait_ge(rows_stored, 16)
            load_sources(slice(0, GRP), 0)
            load_sources(slice(GRP, 2 * GRP), 1)
            with sp.Fori(0, ITER - 1) as i:
                for half in range(2):
                    sp.wait_ge(same_ready, i * 2 + (half + 1))
                    load_sources(bass.ds(i * RING + (2 + half) * GRP, GRP), half)
            sp.wait_ge(same_ready, NGRP - 1)
            load_sources(slice(0, GRP), 0)

            for n in range(TABLES):
                sp.wait_ge(summed_in[n], 16 * (NW // TABLES))
            def store_out(c):
                sp.wait_ge(out_ready, c + 1)
                first, last = CHUNKS[c][0], min(CHUNKS[c][1], USED - 1)
                sp.dma_start(out[first * P:last * P, :].rearrange("(t p) f -> p t f", p=P),
                             feat[:, first:last, :]).then_inc(out_stored, 16)

            for c, (first, last) in enumerate(CHUNKS):
                for n in range(TABLES):
                    if c > 1:
                        sp.wait_ge(chunk_used, 2 * c - 3 if n else 2 * c - 2)
                    sp.dma_start(chunk_of(n, c)[:, :, 0:SW],
                                 sums[n][first * P:last * P, :].rearrange("(t p) f -> p t f", p=P)
                                 ).then_inc(read_back[c], 16)
                if c > 1:
                    store_out(c - 2)
            for c in range(2, len(CHUNKS)):
                store_out(c)
            sp.dma_start(out[(USED - 1) * P:N, :], feat[0:TAIL, USED - 1, :]).then_inc(out_stored, 16)
            sp.wait_ge(out_stored, 16 * (len(CHUNKS) + 1))

        @block.gpsimd
        def _(pool):
            pool.memset(ones[:], 1.0).then_inc(ones_ready, 1)
            pool.memset(zeros, 0.0).then_inc(zeros_ready, 1)
            pool.iota(iota_d[:], pattern=[[1, P]], base=0, channel_multiplier=0,
                      allow_small_or_imprecise_dtypes=True).then_inc(const_ready, 1)
            pool.iota(iota_b, pattern=[[1, P]], base=0, channel_multiplier=0,
                      allow_small_or_imprecise_dtypes=True).then_inc(const_ready, 1)
            pool.memset(zero_b, 0.0).then_inc(const_ready, 1)
            pool.iota(wcol[:], pattern=[[WG, 4]], base=0, channel_multiplier=1,
                      allow_small_or_imprecise_dtypes=True).then_inc(const_ready, 1)
            pool.wait_ge(ones_ready, 1)
            pool.affine_select(out=ident[:], in_=ones[:], compare_op=ALU.is_equal, fill=0.0, base=0,
                               pattern=[[-1, P]], channel_multiplier=1).then_inc(const_ready, 1)
            pool.memset(eps_col[:], EPS).then_inc(const_ready, 1)
            pool.iota(spare_row[:], pattern=[[0, 1]], base=NT * P, channel_multiplier=1,
                      allow_small_or_imprecise_dtypes=True).then_inc(const_ready, 1)

            pool.iota(lane_of[:, 0:1], pattern=[[0, 1]], base=0, channel_multiplier=1).then_inc(const_ready, 1)
            pool.iota(lane_row, pattern=[[0, 32], [1, H]], base=0, channel_multiplier=0,
                      allow_small_or_imprecise_dtypes=True).then_inc(const_ready, 1)

            pool.wait_ge(rows_copied, 16)
            pool.wait_ge(order_known, 1)
            unsorted = pool.alloc_register("pool_unsorted")
            pool.load(unsorted, unsorted_i[0:1, 0:1])
            with pool.If_ne(unsorted, 0):
                pool.affine_select(out=is_before, in_=ones[:], compare_op=ALU.is_gt, fill=0.0, base=0,
                                   pattern=[[-1, P]], channel_multiplier=1).then_inc(tris_ready, 1)
                pool.affine_select(out=is_after, in_=ones[:], compare_op=ALU.is_gt, fill=0.0, base=0,
                                   pattern=[[1, P]], channel_multiplier=-1).then_inc(tris_ready, 1)

                def put_edges(n):
                    pool.sem_inc(pool_steps, 1)
                    pool.indirect_dma_start(out=edge_rows.rearrange("r (e s) -> (r e) s", s=2), in_=pair_i[0:n, :],
                                            out_offset=bass.IndirectOffsetOnAxis(ap=rank_i[0:n, :], axis=0),
                                            in_offset=None).then_inc(edge_put, 16)

                with pool.Fori(0, FULL_ROWS) as j:
                    pool.wait_ge(rank_ready, j + 1)
                    put_edges(P)
                pool.wait_ge(rank_ready, FULL_ROWS + 1)
                put_edges(E - FULL_ROWS * P)
                pool.wait_ge(edge_put, 16 * (FULL_ROWS + 1))

            pool.wait_ge(jidx_ready, 1)
            for g in range(4):
                pool.indirect_dma_start(out=work_i[:, g, :], out_offset=None, in_=edge_rows,
                                        in_offset=bass.IndirectOffsetOnAxis(ap=jidx[:, g:g + 1], axis=0),
                                        ).then_inc(rows_got, 16)
            pool.wait_ge(meta_ready, 1)

            def gathers(loop, table_ap, free, per_group, later):
                before = GATHERS.index(loop) * NGRP
                with pool.Fori(0, ITER) as i:
                    for half in range(2):
                        pool.wait_ge(free, i * (2 * per_group) + (half * per_group + later))
                        pool.sem_inc(pool_steps, 1)
                        pool.tensor_copy(idx_stage[:, half, :],
                                         srcT[:, bass.ds(i * RING + half * GRP, GRP)]).then_inc(idx_staged, 1)
                        pool.wait_ge(idx_staged, i * 2 + (before + half + 1))
                        pool.sem_inc(pool_steps, 1)
                        for j in range(GRP):
                            slot = half * GRP + j
                            pool.indirect_dma_start(
                                out=ring[:, slot, 0:D], out_offset=None, in_=table_ap,
                                in_offset=bass.IndirectOffsetOnAxis(ap=idx_stage[:, half, j:j + 1], axis=0),
                            ).then_inc(got[slot], 16)

            pool.wait_ge(y0_stored, 32)
            gathers(AGG0, y0_table, summed[AGG0], GRP, GRP)
            pool.sem_inc(kept, 2)
            with pool.Fori(0, NPAIR) as p:
                for a in range(2):
                    pool.wait_ge(staged, p * 2 + (Q * NT + a + 1))
                    pool.tensor_copy(feat[:, bass.ds(p * 2 + a, 1), :].rearrange("p a b -> p (a b)"),
                                     stage[:, a, :]).then_inc(kept, 1)
            pool.wait_ge(q_stored, 16 * NPAIR)
            gathers(SCORE, q_table, scored, 4, 1)
            pool.wait_ge(scored, 5 + NW // 2)
            pool.wait_ge(v_stored, 16 * NT)
            gathers(ATT, v_table, summed[ATT], GRP, GRP)
            pool.wait_ge(dens_ready, 1)
            with pool.Fori(0, NPAIR) as p:
                pool.tensor_tensor(two(acc[0], p), two(acc[0], p), two(acc[1], p), ALU.add).then_inc(agg_merged, 1)

            def add_bias(p):
                pool.wait_ge(weighted, p + 1)
                pool.tensor_tensor(two(acc[0], p), two(acc[0], p),
                                   bias_bc[:, 6 * D:7 * D].unsqueeze(1).to_broadcast([P, 2, D]),
                                   ALU.add).then_inc(biased, 1)

            def keep(nth, proj):
                def step(p):
                    for a in range(2):
                        pool.wait_ge(staged, p * 2 + (proj * NT + a + 1))
                        pool.tensor_copy(one(feat, p * 2 + a), stage[:, a, :]).then_inc(kept, 1)
                return step

            pipeline(pool, [(5, add_bias), (0, keep(1, L2P))])
            pool.wait_ge(l2_stored, 16 * (NPAIR + 1))
            for t in range(USED):
                pool.indirect_dma_start(out=acc[1][:, t, :], out_offset=None, in_=l2_table,
                                        in_offset=bass.IndirectOffsetOnAxis(ap=l2_idx[:, 1, t:t + 1], axis=0),
                                        ).then_inc(l2_got, 16)
                pool.indirect_dma_start(out=ral[:, t, :], out_offset=None, in_=al_table,
                                        in_offset=bass.IndirectOffsetOnAxis(ap=l2_idx[:, 0, t:t + 1], axis=0),
                                        ).then_inc(l2_got, 16)
            with pool.Fori(0, NPAIR) as p:
                keep(2, L3P)(p)
            pool.wait_ge(y3_ready, 1)
            pool.affine_select(out=before_tri, in_=ones[:], compare_op=ALU.is_gt, fill=0.0, base=0,
                               pattern=[[1, P]], channel_multiplier=-1).then_inc(tri_ready, 1)
            pool.wait_ge(cleared, 16 * TABLES)
            pool.sem_inc(group_in, 1)
            def scatter(i):
                for half in range(2):
                    pool.wait_ge(idx_ready, i * 2 + (half + 2))
                    pool.sem_inc(pool_steps, 1)
                    for j in range(GRP):
                        slot = half * GRP + j
                        n = j % TABLES
                        pool.wait_ge(row_out, i * RING + (4 + slot + 1))
                        pool.sem_inc(pool_steps, 1)
                        if not (isinstance(i, int) and i == 0 and slot < TABLES):
                            pool.wait_ge(summed_in[n], i * (16 * RING // TABLES) + 16 * (slot // TABLES))
                            pool.sem_inc(pool_steps, 1)
                        pool.indirect_dma_start(
                            out=sums[n], in_=ring[:, slot, 0:SW], in_offset=None,
                            out_offset=bass.IndirectOffsetOnAxis(ap=idx_stage[:, half, j:j + 1], axis=0),
                            compute_op=ALU.add).then_inc(summed_in[n], 16)
                        if j == TABLES - 1:
                            pool.sem_inc(group_in, 1)

            scatter(0)
            with pool.Fori(1, ITER) as i:
                scatter(i)

        @block.scalar
        def _(act):
            act.wait_ge(const_ready, 9)

            def blocks_out(first, dst):
                for g in range(NB):
                    act.wait_ge(block_turned, first + g + 1)
                    src = ps[:, (first + g) % 2, 0:P]
                    if len(dst(g).shape) == 3:
                        src = src.rearrange("p (w h) -> p w h", h=H)
                    nc.scalar.copy(dst(g), src).then_inc(block_out, 1)

            def root(n):
                act.wait_ge(var_ready, n)
                tiles = CHUNKS[n - 1][1] - CHUNKS[n - 1][0]
                nc.scalar.activation(sd[:, 0:tiles], mv[:, 0:tiles, 1], ACT.Sqrt,
                                     bias=eps_col[:, 0:1]).then_inc(rooted, 1)

            act.sem_inc(evacuated, 2)
            act.wait_ge(in_x, 32)

            def turned_out(proj):
                def step(p):
                    for a in range(2):
                        act.wait_ge(turned, p * 2 + (proj * NT + a + 1))
                        act.wait_ge(projected, p * 2 + (proj * NT + a + 1))
                        nc.scalar.copy(xT[:, a, :, :].rearrange("p k n -> p (k n)"),
                                       ps[:, a, 0:2 * P]).then_inc(xT_ready, 1)
                return step

            def to_stage(p):
                for a in range(2):
                    nc.scalar.copy(stage[:, a, :], one(feat, p * 2 + a)).then_inc(staged, 1)

            def xw_out(p):
                for a in range(2):
                    act.wait_ge(projected, p * 2 + (a + 3))
                    nc.scalar.copy(one(aux, p * 2 + a), ps[:, 2 + a, 0:D]).then_inc(evacuated, 1)

            pipeline(act, [(-2, xw_out), (-1, turned_out(XW)), (0, to_stage)])
            act.wait_ge(deg_ready, 1)
            nc.scalar.activation(dsq[:], deg[:], ACT.Sqrt, bias=ones[:, 0:1]).then_inc(deg_rooted, 1)
            act.wait_ge(dinv_ready, 1)
            act.wait_ge(evacuated, 2 + NT)
            for t in range(HALF, NT):
                nc.scalar.mul(aux[:, t, :], aux[:, t, :], dinv[:, t:t + 1]).then_inc(y0_ready, 1)
            blocks_out(0, lambda g: turnedT[:, g, :])
            act.wait_ge(y0_ready, HALF)
            act.wait_ge(y0_first, 1)
            act.wait_ge(rows_stored, 16)
            act.wait_ge(attn_used, 1)
            nc.scalar.copy(acc[0][:, :, 0:D], aux[:]).then_inc(loops_in, 1)

            def deviation(u, src):
                def step(p):
                    act.wait_ge(mean_made, p + (u * NPAIR + 1))
                    act.wait_ge(sd_made, p + u * NPAIR)
                    for a in range(2):
                        ins = nc.scalar.activation(squares[:, a, :], one(src, p * 2 + a), ACT.Square,
                                                   bias=less_mean[:, ds(p * 2 + a, 1)],
                                                   accum_out=square_sums[:, a:a + 1])
                    ins.then_inc(squared, 1)
                    act.wait_ge(squared, p + (u * NPAIR + 1))
                    nc.scalar.activation(sd[:, ds(p * 2, 2)], square_sums[:], ACT.Sqrt, scale=1.0 / D,
                                         bias=eps_col[:, 0:1]).then_inc(sd_made, 1)
                return step

            def normalise_to_stage(u, nth, proj, src):
                def step(p):
                    act.wait_ge(scale_made, p + (u * NPAIR + 1))
                    for a in range(2):
                        act.wait_ge(turned, p * 2 + (proj * NT + a - 1))
                        act.wait_ge(kept, p * 2 + (nth * NT + a + 1))
                        nc.scalar.activation(stage[:, a, :], one(src, p * 2 + a), ACT.Identity,
                                             scale=rstd[:, ds(p * 2 + a, 1)],
                                             bias=shift[:, ds(p * 2 + a, 1)]).then_inc(staged, 1)
                return step

            pipeline(act, [(-1, turned_out(Q)), (1, deviation(0, acc[0])), (0, normalise_to_stage(0, 0, Q, acc[0]))])
            act.wait_ge(kept, 2 + NT)
            pipeline(act, [(-1, turned_out(K)), (0, to_stage)])

            act.sem_inc(maskT_ready[SCORE], 2)
            with act.Fori(0, ITER) as i:
                for side in range(2):
                    for half in range(2):
                        act.wait_ge(maskT_full[SCORE], i * 4 + (side * 2 + half + 2))
                        act.wait_ge(k_ready, i * 8 + (side * 4 + 4))
                        nc.scalar.copy(maskT[:, half * 4:half * 4 + 4, :].rearrange("p a b -> p (a b)"),
                                       ps[:, half, :]).then_inc(maskT_ready[SCORE], 1)
                    if side == 0:
                        nc.scalar.copy(stage[:, 0, :], one(feat, i)).then_inc(staged, 1)
                    else:
                        act.wait_ge(turned, i + (V * NT + 1))
                        nc.scalar.copy(xT[:, 0, :, :].rearrange("p k n -> p (k n)"),
                                       ps[:, 6, 0:2 * P]).then_inc(xT_ready, 1)
                        act.wait_ge(projected, i + (V * NT + 3))
                        nc.scalar.copy(one(acc[1], i), ps[:, 7, 0:D]).then_inc(evacuated, 1)
            act.wait_ge(v_stored, 16 * NT)
            blocks_out(NB, lambda g: turnedT[:, g, :])
            act.wait_ge(less_m, 1)
            nc.scalar.activation(turnedT, turnedT, ACT.Exp, scale=HD ** -0.5).then_inc(exps_ready, 1)
            blocks_out(2 * NB, lambda g: score[:, g * 32:g * 32 + 32, :])
            with act.Fori(0, NT) as t:
                nc.scalar.copy(stage[:, 0, :], one(feat, t)).then_inc(staged, 1)
                act.wait_ge(turned, t + (SKIP * NT + 1))
                nc.scalar.copy(xT[:, 0, :, :].rearrange("p k n -> p (k n)"),
                               ps[:, 0, 0:2 * P]).then_inc(xT_ready, 1)
                act.wait_ge(projected, t + (SKIP * NT + 3))
                nc.scalar.copy(one(aux, t), ps[:, 1, 0:D])
                nc.scalar.copy(skip_logit[:, bass.ds(t, 1)], ps[:, 1, D:D + 1]).then_inc(evacuated, 1)

            act.wait_ge(gate_in_made, NPAIR)
            nc.scalar.activation(gate[:], gate[:], ACT.Sigmoid, bias=scal_bc[:, 1:2]).then_inc(gate_made, 1)

            def normalise(p):
                act.wait_ge(scale_made, p + (NPAIR + 1))
                for a in range(2):
                    ins = nc.scalar.activation(one(acc[0], p * 2 + a), one(acc[0], p * 2 + a), ACT.Identity,
                                               scale=rstd[:, ds(p * 2 + a, 1)], bias=shift[:, ds(p * 2 + a, 1)])
                ins.then_inc(normed, 1)

            def negative_part(p):
                act.wait_ge(biased, p + 1)
                nc.scalar.activation(two(aux, p), two(acc[0], p), ACT.Relu, scale=-1.0).then_inc(negated, 1)

            pipeline(act, [(1, deviation(1, acc[0])), (0, normalise)])
            pipeline(act, [(-1, turned_out(L2P)), (3, negative_part), (1, deviation(2, acc[0])),
                           (0, normalise_to_stage(2, 1, L2P, acc[0]))])
            act.wait_ge(l2_logits, 1)
            nc.scalar.activation(alpha[:], ral[:], ACT.Exp).then_inc(l2_exps, 1)

            def y3_evacuated(p):
                for a in range(2):
                    act.wait_ge(projected, p * 2 + (L3P * NT + a + 3))
                    nc.scalar.copy(one(acc[0], p * 2 + a), ps[:, 2 + a, 0:D]).then_inc(y3_out, 1)

            act.sem_inc(y3_out, 2)
            pipeline(act, [(-2, y3_evacuated), (-1, turned_out(L3P)), (1, deviation(3, aux)),
                           (0, normalise_to_stage(3, 2, L3P, aux))])
            act.sem_inc(maskT_ready[SPREAD], 2)
            act.sem_inc(row_out, 4)
            with act.Fori(0, ITER) as i:
                for side in range(2):
                    for half in range(2):
                        act.wait_ge(maskT_full[SPREAD], i * 4 + (side * 2 + half + 1))
                        act.wait_ge(row_full, i * RING + (side * GRP + 1))
                        nc.scalar.copy(maskT[:, half * 4:half * 4 + 4, :].rearrange("p a b -> p (a b)"),
                                       ps[:, half, :]).then_inc(maskT_ready[SPREAD], 1)
                    act.wait_ge(group_in, i * 2 + (side + 1))
                    for j in range(GRP):
                        act.wait_ge(row_full, i * RING + (side * GRP + j + 2))
                        nc.scalar.copy(ring[:, side * GRP + j, 0:SW], ps[:, 2 + j % 4, 0:SW]).then_inc(row_out, 1)
            for n in range(1, len(CHUNKS) + 1):
                root(n)

        @block.tensor
        def _(pe):
            pe.wait_ge(const_ready, 9)
            pe.wait_ge(ones_ready, 1)
            pe.sem_inc(projected, 2)

            def turn_blocks(first, src):
                for g in range(NB):
                    if first + g >= 2:
                        pe.wait_ge(block_out, first + g - 1)
                    pe.transpose(ps[:, (first + g) % 2, 0:P], src(g), ident[:]).then_inc(block_turned, 1)

            def spread_ends(n):
                pe.wait_ge(ends_ready, n)
                for side in range(2):
                    mm = pe.matmul(ps[:, 2 + side, 0:NW], same_head[:],
                                   ends[:, side, :, :].rearrange("p b n -> p (b n)"), start=True, stop=True)
                mm.then_inc(ends_spread, 1)

            def aggregate(loop, banks, width, beside=None):
                before = GATHERS.index(loop) * ITER * 16
                with pe.Fori(0, ITER) as i:
                    for half in range(2):
                        pe.wait_ge(mask_ready[loop], i * 2 + (half + 1))
                        for j in range(GRP):
                            slot = half * GRP + j
                            if loop == ATT:
                                pe.wait_ge(ev_ready, i * GRP + (half * 4 + j // 2 + 1))
                            else:
                                pe.wait_ge(got[slot], i * 16 + (before + 16))
                            pe.wait_ge(added[loop], i * RING + (slot + 1))
                            pe.matmul(ps[:, 8 - banks + j % banks, 0:width], mask[:, half, j, :],
                                      ring[:, slot, 0:width],
                                      start=True, stop=True).then_inc(summed[loop], 1)
                            if beside and j % 2 == 1:
                                beside(i, half * 4 + j // 2)

            def turn_masks(loop, i, half):
                pe.wait_ge(mask_ready[loop], i * 2 + (half + 1))
                pe.wait_ge(maskT_ready[loop], i * 4 + (2 * half + 2))
                for j in range(GRP):
                    tr = pe.transpose(ps[:, j // 4, (j % 4) * P:(j % 4 + 1) * P], mask[:, half, j, :], ident[:])
                    if j % 4 == 3:
                        tr.then_inc(maskT_full[loop], 1)
                pe.wait_ge(maskT_ready[loop], i * 4 + (2 * half + 4))

            pe.matmul(ps[:, 7, 0:NT], zero_b, zero_b[:, 0:NT], start=True, stop=False, skip_group_check=True)

            def count(i, group):
                pe.wait_ge(place_ready, i * 4 + (group + 1))
                for j in range(GRP):
                    mm = pe.matmul(ps[:, 7, 0:NT], at_place[:, group, j, :],
                                   in_tile[:, ds(i * (4 * GRP) + group * GRP + j, 1), :]
                                   .rearrange("p a b -> p (a b)"),
                                   start=False, stop=False, skip_group_check=True)
                mm.then_inc(counted, 1)

            pe.wait_ge(in_w0, 16)

            def turn(proj):
                def step(p):
                    for a in range(2):
                        pe.wait_ge(staged, p * 2 + (proj * NT + a + 1))
                        if not (isinstance(p, int) and proj * NT + p == 0):
                            pe.wait_ge(xT_ready, p * 2 + (proj * NT + a - 1))
                        pe.transpose(ps[:, a, 0:P], stage[:, a, 0:P], ident[:])
                        pe.transpose(ps[:, a, P:2 * P], stage[:, a, P:2 * P], ident[:]).then_inc(turned, 1)
                return step

            def product(proj, w, c0, n):
                def step(p):
                    for a in range(2):
                        pe.wait_ge(xT_ready, p * 2 + (proj * NT + a + 1))
                        pe.wait_ge(evacuated, p * 2 + (proj * NT + a + 1))
                        pe.matmul(ps[:, 2 + a, 0:n], xT[:, a, 0, :], w[:, 0, c0:c0 + n], start=True, stop=False)
                        pe.matmul(ps[:, 2 + a, 0:n], xT[:, a, 1, :], w[:, 1, c0:c0 + n],
                                  start=False, stop=True).then_inc(projected, 1)
                return step

            def counts(first, last):
                def step(p):
                    for group in range(first, last + 1):
                        count(p, group)
                return step

            pipeline(pe, [(0, turn(XW)), (0, counts(0, 1)), (-1, product(XW, w_sb, 0, D)), (0, counts(2, 3))])
            pe.matmul(ps[:, 7, 0:NT], zero_b, zero_b[:, 0:NT], start=False, stop=True,
                      skip_group_check=True).then_inc(deg_full, 1)
            pe.wait_ge(deg_ready, 1)
            pe.matmul(ps[:, 6, 0:NT], ones[:], deg[:], start=True, stop=True).then_inc(cum_ready, 1)
            pe.wait_ge(falls_ready, 1)
            pe.matmul(ps[:, 6, NT:NT + 1], ones[0:ROWS // 4, :], falls_of[0:ROWS // 4, :], start=True,
                      stop=True).then_inc(cum_ready, 1)
            pe.wait_ge(order_known, 1)
            unsorted = pe.alloc_register("pe_unsorted")
            pe.load(unsorted, unsorted_i[0:1, 0:1])
            with pe.If_ne(unsorted, 0):
                pe.wait_ge(tris_ready, 2)
                pe.matmul(ps[:, 4, 0:NT], is_after, deg[:], start=True, stop=True).then_inc(ranks_full, 1)
                pe.wait_ge(ranks_out, 1)

                def look_up(n):
                    pe.matmul(ps[0:n, 4, 0:NT], place_hotT[:, 0:n], next_rank, start=True, stop=True)
                    pe.matmul(ps[:, 5, 0:NT], place_hot[0:n, :], tile_hot[0:n, :], start=True,
                              stop=True).then_inc(looked_up, 1)

                with pe.Fori(0, FULL_ROWS) as j:
                    pe.wait_ge(hots_ready, j + 1)
                    look_up(P)
                pe.wait_ge(hots_ready, FULL_ROWS + 1)
                look_up(E - FULL_ROWS * P)
            pe.wait_ge(diag_ready, 1)
            for g in range(4):
                mm = pe.matmul(ps[:, 6, g * WG:(g + 1) * WG], ones[0:WG, :], tile_diag[:, g, :],
                               start=True, stop=True)
            mm.then_inc(tiles_full, 1)
            pe.wait_ge(rowsf_ready, 1)
            for g in range(4):
                pe.transpose(ps[:, 4, g * WG:(g + 1) * WG], rows_f[:, g, 0:P], ident[0:WG, 0:WG])
                tr = pe.transpose(ps[:, 5, g * WG:(g + 1) * WG], rows_f[:, g, P:2 * P], ident[0:WG, 0:WG])
            tr.then_inc(rowsT_ready, 1)
            pe.wait_ge(evacuated, 2 + NT)
            pe.wait_ge(keys_ready, 1)
            turn_blocks(0, lambda g: key4[:, g * 32:g * 32 + 32, :].rearrange("p a b -> p (a b)"))
            pe.sem_inc(summed[AGG0], RING)
            spread_ends(1)
            pe.wait_ge(starts_ready, 1)
            aggregate(AGG0, 8, D)
            pe.wait_ge(added[AGG0], 8 + NW)
            pe.wait_ge(in_w, 96)

            pipeline(pe, [(-1, product(Q, w_sb, D, D)), (0, turn(Q))])
            pipeline(pe, [(-1, product(K, w_sb, 3 * D, D)), (0, turn(K))])

            def beside(proj, c0, its_bias, t, half, bank):
                if half == 0:
                    pe.wait_ge(staged, t + (proj * NT + 1))
                    pe.wait_ge(xT_ready, t + proj * NT)
                    pe.transpose(ps[:, bank, 0:P], stage[:, 0, 0:P], ident[:])
                    pe.transpose(ps[:, bank, P:2 * P], stage[:, 0, P:2 * P], ident[:]).then_inc(turned, 1)
                else:
                    pe.wait_ge(xT_ready, t + (proj * NT + 1))
                    pe.wait_ge(evacuated, t + (proj * NT + 2))
                    if proj == SKIP:
                        logit = ps[:, bank + 1, D:D + 1]
                        pe.matmul(logit, xT[:, 0, 0, :], skip_gate[:, 0:1], start=True, stop=False)
                        pe.matmul(logit, xT[:, 0, 1, :], skip_gate[:, 1:2], start=False, stop=False)
                        pe.matmul(logit, ones[0:1, :], skip_gate[0:1, 2:3], start=False, stop=True)
                    to = ps[:, bank + 1, 0:D]
                    pe.matmul(to, xT[:, 0, 0, :], w_sb[:, 0, c0:c0 + D], start=True, stop=False)
                    pe.matmul(to, xT[:, 0, 1, :], w_sb[:, 1, c0:c0 + D], start=False, stop=False)
                    pe.matmul(to, ones[0:1, :], bias_bc[0:1, its_bias * D:(its_bias + 1) * D], start=False,
                              stop=True).then_inc(projected, 1)

            pe.wait_ge(evacuated, 2 + (K + 1) * NT)
            pe.sem_inc(k_ready, 4)
            pe.sem_inc(maskT_full[SCORE], 1)
            tile_regs = [pe.alloc_register(f"k_tile{j}") for j in range(GRP)]
            with pe.Fori(0, ITER) as i:
                for half in range(2):
                    pe.load(tile_regs, tile_i[0:1, bass.ds(i * RING + half * GRP, GRP)])
                    tiles = [pe.snap(r, min_val=0, max_val=NT - 1) for r in tile_regs]
                    turn_masks(SCORE, i, half)
                    for j in range(GRP):
                        if j % 2 == 0:
                            pe.wait_ge(scored, i * 8 + (half * 4 + j // 2 + 2))
                        mm = pe.matmul(ps[:, 2 + j // 2, (j % 2) * D:(j % 2 + 1) * D], maskT[:, j, :],
                                       aux[:, bass.ds(tiles[j], 1), :].rearrange("p a b -> p (a b)"),
                                       start=True, stop=True)
                        if j % 2 == 1:
                            mm.then_inc(k_ready, 1)
                    beside(V, 2 * D, 2, i, half, 6)

            pe.wait_ge(scored, 5 + NW // 2)
            pe.sem_inc(summed[ATT], RING)
            turn_blocks(NB, lambda g: score[:, g * 32:g * 32 + 32, :].rearrange("p a b -> p (a b)"))
            spread_ends(2)
            pe.wait_ge(block_out, 2 * NB)
            pe.wait_ge(exps_ready, 1)
            turn_blocks(2 * NB, lambda g: turnedT[:, g, :])

            def skip(t, step):
                if step % 4 == 0:
                    beside(SKIP, 4 * D, 4, t, step // 4, 0)

            pe.wait_ge(skip_gate_ready, 1)
            aggregate(ATT, 4, D + H, skip)
            pe.wait_ge(added[ATT], 4 + NW)
            pipeline(pe, [(-1, product(L2P, w2_sb, 0, AW)), (0, turn(L2P))])

            def l3_product(p):
                for a in range(2):
                    pe.wait_ge(xT_ready, p * 2 + (L3P * NT + a + 1))
                    pe.wait_ge(y3_out, p * 2 + (a + 1))
                    pe.wait_ge(evacuated, p * 2 + (L3P * NT + a + 1))
                    for bank, c0 in ((2 + a, 5 * D), (4 + a, 6 * D)):
                        pe.matmul(ps[:, bank, 0:D], xT[:, a, 0, :], w_sb[:, 0, c0:c0 + D], start=True, stop=False)
                        mm = pe.matmul(ps[:, bank, 0:D], xT[:, a, 1, :], w_sb[:, 1, c0:c0 + D],
                                       start=False, stop=True)
                    mm.then_inc(projected, 1)

            pipeline(pe, [(-1, l3_product), (0, turn(L3P))])
            pe.wait_ge(y3_ready, 1)
            pe.sem_inc(dup_full, 1)
            pe.sem_inc(row_full, 1)
            with pe.Fori(0, ITER) as i:
                for half in range(2):
                    pe.load(tile_regs, tile_i[0:1, bass.ds(i * RING + half * GRP, GRP)])
                    tiles = [pe.snap(r, min_val=0, max_val=NT - 1) for r in tile_regs]
                    pe.wait_ge(mask_ready[SPREAD], i * 2 + (half + 1))
                    pe.wait_ge(same_ready, i * 2 + (half + 1))
                    pe.wait_ge(maskT_ready[SPREAD], i * 4 + (2 * half + 2))
                    for j in range(GRP):
                        mm = pe.matmul(ps[:, j // 4, (j % 4) * P:(j % 4 + 1) * P], mask[:, half, j, :],
                                       same[:, j, :], start=True, stop=True)
                        if j % 4 == 3:
                            mm.then_inc(maskT_full[SPREAD], 1)
                    pe.wait_ge(idx_ready, i * 2 + (half + 1))
                    for j in range(GRP):
                        mm = pe.matmul(ps[:, 6, j:j + 1], earlier[:, j, :], ones[:, 0:1], start=True, stop=True)
                    mm.then_inc(dup_full, 1)
                    pe.wait_ge(maskT_ready[SPREAD], i * 4 + (2 * half + 4))
                    for j in range(GRP):
                        pe.wait_ge(row_out, i * RING + (half * GRP + j + 1))
                        pe.matmul(ps[:, 2 + j % 4, 0:SW], maskT[:, j, :],
                                  acc[0][:, bass.ds(tiles[j], 1), 0:SW].rearrange("p a b -> p (a b)"),
                                  start=True, stop=True).then_inc(row_full, 1)

        @block.vector
        def _(v):
            chain = [0]

            def link(ins):
                chain[0] += 1
                ins.then_inc(dve_seq, 1)
                v.wait_ge(dve_seq, chain[0])

            def bias(n, count=1):
                return bias_bc[:, n * D:(n + count) * D]

            def over_tiles(row, tiles=NT):
                return row.unsqueeze(1).to_broadcast([P, tiles, row.shape[-1]])

            v.memset(runs_i[:, 8 * P:], PAD_DST).then_inc(runs_cleared, 1)
            v.memset(feat[:, USED - 1:NT, :], 0.0).then_inc(x_tail, 1)
            v.wait_ge(const_ready, 9)
            v.wait_ge(in_edges, 16)
            dst_i = edge_cols[:, 1, :]
            v.tensor_copy(l2_idx[:], edge_cols[:, :, 0:USED])
            v.tensor_single_scalar(lane_of[:, 1:2], lane_of[:, 0:1], H - 1, ALU.bitwise_and)
            v.tensor_single_scalar(lane_of[:, 2:3], lane_of[:, 0:1], 2, ALU.arith_shift_right)
            link(v.tensor_copy(lane_of_f[:, 0:1], lane_of[:, 0:1]))
            link(v.tensor_copy(lane_of_f[:, 1:3], lane_of[:, 1:3]))
            v.tensor_scalar(same_head[:], lane_row, lane_of_f[:, 1:2], None, ALU.is_equal)
            link(v.tensor_scalar(lane[:], iota_d[:, 0:32], lane_of_f[:, 2:3], None, ALU.is_equal))
            v.tensor_single_scalar(dst_parts_i[:, 0, :], dst_i, P - 1, ALU.bitwise_and)
            link(v.tensor_single_scalar(dst_parts_i[:, 1, :], dst_i, 7, ALU.arith_shift_right))
            link(v.tensor_copy(dst_parts, dst_parts_i))
            link(v.tensor_tensor(in_tile, dst_parts[:, 1, :].unsqueeze(2).to_broadcast([P, NW, NT]),
                                 iota_d[:, 0:NT].unsqueeze(1).to_broadcast([P, NW, NT]), ALU.is_equal))
            v.sem_inc(counted, 4)
            with v.Fori(0, NPAIR) as i:
                for group in range(4):
                    v.wait_ge(counted, i * 4 + (group + 1))
                    make_places(v, i, group).then_inc(place_ready, 1)
            v.wait_ge(deg_full, 1)
            link(v.tensor_copy(deg[:], ps[:, 7, 0:NT]))
            v.sem_inc(deg_ready, 1)
            v.wait_ge(deg_rooted, 1)
            v.reciprocal(dinv[:], dsq[:]).then_inc(dinv_ready, 1)
            v.wait_ge(dinv_ready, 1)
            v.wait_ge(evacuated, 2 + NT)
            v.tensor_tensor(aux[:, 0:HALF, :], aux[:, 0:HALF, :],
                            dinv[:, 0:HALF].unsqueeze(2).to_broadcast([P, HALF, D]), ALU.mult).then_inc(y0_first, 1)
            v.wait_ge(in_runs, 32)
            link(v.tensor_copy(runs_f, runs_i.rearrange("p (e s) -> p e s", s=2)[:, :, 1]))
            link(v.tensor_tensor(falls, runs_f[:, 0:4 * P], runs_f[:, 1:], ALU.is_gt))
            v.tensor_reduce(falls_of[0:ROWS // 4, :], falls, X_AXIS, ALU.add).then_inc(falls_ready, 1)
            v.wait_ge(cum_ready, 2)
            link(v.memset(cum[:, 0:1], 0.0))
            link(v.tensor_tensor_scan(cum[:, 1:NT], ones[:, 0:NT - 1], ps[:, 6, 0:NT - 1], 0.0, ALU.mult, ALU.add))
            link(v.tensor_copy(cum_i[:, 0, :], cum[:]))
            v.tensor_copy(unsorted_i[:, 0:1], ps[0:1, 6, NT:NT + 1]).then_inc(order_known, 1)
            v.wait_ge(order_known, 1)
            unsorted = v.alloc_register("dve_unsorted")
            v.load(unsorted, unsorted_i[0:1, 0:1])
            with v.If_ne(unsorted, 0):
                sort_step = sem("sort_step")
                made = [0]

                def then(ins, j=None):
                    made[0] += 1
                    ins.then_inc(sort_step, 1)
                    v.wait_ge(sort_step, made[0] if j is None else j * STEPS + made[0])

                then(v.tensor_copy(dst_cols, edge_cols[:, 1, :]))
                v.wait_ge(ranks_full, 1)
                then(v.tensor_tensor(next_rank, ps[:, 4, 0:NT], cum[:], ALU.add))
                v.sem_inc(ranks_out, 1)
                STEPS = 9

                def rank_row(j, at, n, loaded, before):
                    v.wait_ge(row_loaded, loaded)
                    pairs_of = row_i.rearrange("p (e s) -> p e s", s=2)
                    v.tensor_copy(row_f, pairs_of[:, :, 1])
                    then(v.tensor_single_scalar(place_i, pairs_of[:, :, 1], P - 1, ALU.bitwise_and), j)
                    then(v.tensor_copy(place_f, place_i), j)
                    v.sem_inc(row_seen, 1)
                    v.tensor_scalar(place_hotT, place_f, lane_of_f[:, 0:1], None, ALU.is_equal)
                    v.tensor_scalar(place_hot, iota_d[:], dst_parts[:, 0, at], None, ALU.is_equal)
                    then(v.tensor_scalar(tile_hot, iota_d[:, 0:NT], dst_parts[:, 1, at], None, ALU.is_equal), j)
                    v.sem_inc(hots_ready, 1)
                    then(v.scalar_tensor_tensor(out=early_of, in0=row_f, scalar=dst_cols[:, at], in1=is_before,
                                                op0=ALU.is_equal, op1=ALU.mult, accum_out=rank_f[:, 0:1]), j)
                    v.wait_ge(looked_up, before + 1)
                    then(v.scalar_tensor_tensor(out=rank_of[0:n, :], in0=ps[0:n, 4, 0:NT], scalar=1.0,
                                                in1=tile_hot[0:n, :], op0=ALU.mult, op1=ALU.mult,
                                                accum_out=rank_f[0:n, 1:2]), j)
                    then(v.tensor_tensor(next_rank, next_rank, ps[:, 5, 0:NT], ALU.add), j)
                    then(v.tensor_tensor(rank_f[0:n, 1:2], rank_f[0:n, 1:2], rank_f[0:n, 0:1], ALU.add), j)
                    then(v.tensor_copy(rank_i[0:n, :], rank_f[0:n, 1:2]), j)
                    then(v.tensor_copy(pair_i, edge_cols[:, :, at].rearrange("p s a -> p (s a)")), j)
                    v.sem_inc(rank_ready, 1)
                    v.wait_ge(edge_put, before * 16 + 16)

                v.sem_inc(row_seen, 1)
                v.wait_ge(tris_ready, 2)
                with v.Fori(0, FULL_ROWS) as j:
                    rank_row(j, bass.ds(j, 1), P, j * 16 + 16, j)
                made[0] = 2 + FULL_ROWS * STEPS
                rank_row(None, slice(FULL_ROWS, FULL_ROWS + 1), E - FULL_ROWS * P, FULL_ROWS * 16 + 16, FULL_ROWS)
            link(v.tensor_scalar(cum_i[:, 1, :], cum[:], -1.0, None, ALU.add))
            link(v.tensor_single_scalar(cum_i[:], cum_i[:], 7, ALU.arith_shift_right))
            link(v.tensor_copy(first_row[:], cum_i[:, 0, :]))
            link(v.tensor_copy(last_row[:], cum_i[:, 1, :]))
            U1 = USED
            link(v.tensor_tensor(items[:, 0:U1], last_row[:, 1:U1 + 1], first_row[:, 0:U1], ALU.subtract))
            link(v.tensor_scalar(items[:, 0:U1], items[:, 0:U1], 1.0, None, ALU.add))
            link(v.tensor_tensor(off[:, 0:U1], cum[:, 1:U1 + 1], cum[:, 0:U1], ALU.is_gt))
            link(v.tensor_tensor(items[:, 0:U1], items[:, 0:U1], off[:, 0:U1], ALU.mult))
            link(v.memset(start[:, 0:1], 0.0))
            link(v.tensor_tensor_scan(start[:, 1:U1 + 1], ones[:, 0:U1], items[:, 0:U1], 0.0, ALU.mult, ALU.add))
            link(v.tensor_tensor(off[:, 0:U1], first_row[:, 0:U1], start[:, 0:U1], ALU.subtract))
            link(v.tensor_tensor(doff[:, 1:U1], off[:, 1:U1], off[:, 0:U1 - 1], ALU.subtract))
            shape = [WG, 4, U1 - 1]
            link(v.tensor_tensor(ge[:], wcol[:].unsqueeze(2).to_broadcast(shape),
                                 start[0:WG, 1:U1].unsqueeze(1).to_broadcast(shape), ALU.is_ge))
            link(v.tensor_tensor(geo[:], ge[:], doff[0:WG, 1:U1].unsqueeze(1).to_broadcast(shape), ALU.mult))
            link(v.tensor_reduce(tcol[:], ge[:], X_AXIS, ALU.add))
            link(v.tensor_reduce(jcol[:], geo[:], X_AXIS, ALU.add))
            link(v.tensor_scalar(t128[:], tcol[:], float(P), None, ALU.mult))
            link(v.tensor_tensor(jcol[:], jcol[:], wcol[:], ALU.add))
            link(v.tensor_scalar(jcol[:], jcol[:], off[0:WG, 0:1], -float(PAD_ROW), ALU.add, ALU.add))
            link(v.tensor_scalar(jcol2[:], wcol[:], start[0:WG, U1:U1 + 1], None, ALU.is_lt))
            link(v.tensor_tensor(jcol[:], jcol[:], jcol2[:], ALU.mult))
            v.tensor_scalar(jidx[:], jcol[:], float(PAD_ROW), None, ALU.add).then_inc(jidx_ready, 1)
            for g in range(4):
                ins = v.tensor_scalar(tile_diag[:, g, :], ident[0:WG, 0:WG], tcol[:, g:g + 1], None, ALU.mult)
            ins.then_inc(diag_ready, 1)
            v.wait_ge(tiles_full, 1)
            tw = tile_row
            link(v.tensor_copy(tw[:], ps[:, 6, 0:NW]))
            link(v.tensor_copy(tile_i[:], tw[0:1, :]))
            v.wait_ge(rows_got, 64)
            work_pairs = work_i.rearrange("p g (e s) -> p g e s", s=2)
            link(v.tensor_copy(rows_f[:, :, 0:P], work_pairs[:, :, :, 0]))
            link(v.tensor_tensor(rows_f[:, :, P:2 * P], work_pairs[:, :, :, 1],
                                 t128[:].unsqueeze(2).to_broadcast([WG, 4, P]), ALU.subtract))
            v.sem_inc(rowsf_ready, 1)

            def evacuate(proj, write):
                base = proj * NT
                with v.Fori(0, NPAIR) as i:
                    for a in range(2):
                        v.wait_ge(projected, i * 2 + (base + a + 3))
                        write(a, lambda t: t[:, bass.ds(i * 2 + a, 1), :].rearrange("p a b -> p (a b)")
                              ).then_inc(evacuated, 1)
                v.wait_ge(evacuated, 2 + base + NT)

            v.wait_ge(rowsT_ready, 1)
            link(v.memset(dstl[:, NW:], -1.0))
            link(v.tensor_copy(dstl[:, 0:NW], ps[:, 5, 0:NW]))
            link(v.tensor_copy(srcT[:], ps[:, 4, 0:NW]))
            v.sem_inc(meta_ready, 1)

            def make_mask(loop, slot, at):
                shape3 = [P, GRP, P]
                return v.tensor_tensor(mask[:, slot, :, :], iota_d[:].unsqueeze(1).to_broadcast(shape3),
                                       dstl[:, at].unsqueeze(2).to_broadcast(shape3),
                                       ALU.is_equal).then_inc(mask_ready[loop], 1)

            def mask_loop(loop, slot_free, per_group, later, group):
                make_mask(loop, 0, slice(0, GRP))
                with v.Fori(0, ITER) as i:
                    for half in range(2):
                        v.wait_ge(slot_free, i * (2 * per_group) + (half * per_group + later))
                        make_mask(loop, 1 - half, bass.ds(i * RING + (half + 1) * GRP, GRP))
                        if group:
                            group(i, half)

            def per_node(col, width=D):
                return col.unsqueeze(2).to_broadcast([P, NT, width])

            link(v.tensor_copy(key4,
                               dstl[:, 0:NW].unsqueeze(2).to_broadcast([P, NW, H])))
            v.sem_inc(keys_ready, 1)
            v.wait_ge(in_w, 96)
            for k in range(2):
                for side in range(2):
                    link(v.tensor_tensor(prod[:, 0, 0:D], w2_sb[:, k, 0:D], attn_bc[:, 1 - side, :], ALU.mult))
                    link(v.tensor_reduce(w2_sb[:, k, D + side * H:D + (side + 1) * H],
                                         prod[:, 0, 0:D].rearrange("p (h d) -> p h d", d=HD), X_AXIS, ALU.add))
            v.sem_inc(attn_used, 1)
            v.wait_ge(block_out, NB)
            by_row = starts[:, 0:NB * P].rearrange("p (b e) -> p b e", e=P)
            link(v.memset(starts[:], -BIG))
            link(v.tensor_tensor(by_row[:, :, 1:P], turnedT[:, :, 0:P - 1], turnedT[:, :, 1:P], ALU.not_equal))
            link(v.tensor_scalar(by_row[:, :, 1:P], by_row[:, :, 1:P], -BIG, None, ALU.mult))

            def spread_ends(rows, n):
                for side, e in enumerate((0, P - 1)):
                    ins = v.tensor_tensor(ends[:, side, :, :], lane[:].unsqueeze(1).to_broadcast([P, NB, 32]),
                                          rows[:, :, e].unsqueeze(2).to_broadcast([P, NB, 32]), ALU.mult)
                ins.then_inc(ends_ready, 1)
                v.wait_ge(ends_spread, n)

            first, last = ps[:, 2, 0:NW], ps[:, 3, 0:NW]
            spread_ends(turnedT, 1)
            link(v.memset(joined[:], 1.0))
            link(v.tensor_copy(one_seg[:], first))
            link(v.tensor_tensor(joined[:, 1:NW], one_seg[:, 1:NW], last[:, 0:NW - 1], ALU.not_equal))
            link(v.tensor_tensor(carry_w, tw[:, 1:NW], tw[:, 0:NW - 1], ALU.not_equal))
            link(v.tensor_tensor(joined[:, 1:NW], joined[:, 1:NW], carry_w, ALU.max))
            link(v.tensor_scalar(joined[:], joined[:], -BIG, None, ALU.mult))
            link(v.tensor_tensor(one_seg[:], one_seg[:], last, ALU.not_equal))
            link(v.tensor_scalar(one_seg[:], one_seg[:], -BIG, None, ALU.mult))
            v.sem_inc(starts_ready, 1)
            v.wait_ge(loops_in, 1)
            link(v.tensor_tensor(acc[1][:, :, 0:D], over_tiles(bias(0)), per_node(dsq[:]), ALU.mult))

            tile_regs = [v.alloc_register(f"add_tile{j}") for j in range(GRP)]

            def add_group(loop, i, half, width, full, free, bank):
                v.load(tile_regs, tile_i[0:1, bass.ds(i * RING + half * GRP, GRP)])
                for j in range(GRP):
                    t = v.snap(tile_regs[j], min_val=0, max_val=NT - 1)
                    n = half * GRP + j
                    v.wait_ge(summed[loop], i * RING + (full + n + 1))
                    v.wait_ge(added[loop], i * RING + (free + n - 1))
                    into = acc[j % 2][:, bass.ds(t, 1), 0:width].rearrange("p a b -> p (a b)")
                    v.tensor_tensor(into, into, ps[:, bank(j), 0:width], ALU.add).then_inc(added[loop], 1)

            def aggregate(loop):
                v.sem_inc(added[loop], 8)
                mask_loop(loop, summed[loop], GRP, 2 * GRP,
                          lambda i, half: add_group(loop, i, half, D, RING, 8, lambda j: j))
                v.wait_ge(added[loop], 8 + NW)

            norms = [0]

            def layernorm(src, dst, tiles=NT):
                norms[0] += 1
                for t in range(tiles):
                    ins = v.bn_stats(stats[:, t, :], src[:, t, :])
                link(ins)
                for t in range(tiles):
                    ins = v.bn_aggr(mv[:, t, :], stats[:, t, :])
                link(ins)
                v.sem_inc(var_ready, 1)
                v.wait_ge(rooted, norms[0])
                link(v.reciprocal(rstd[:, 0:tiles], sd[:, 0:tiles]))
                for t in range(tiles):
                    ins = v.tensor_scalar(dst[:, t, :], src[:, t, :], mv[:, t, 0:1], rstd[:, t:t + 1],
                                          ALU.subtract, ALU.mult)
                link(ins)

            a0, a1 = acc[0][:, :, 0:D], acc[1][:, :, 0:D]
            v.wait_ge(y0_stored, 32)
            aggregate(AGG0)
            v.sem_inc(scored, 5)

            def merge(p):
                v.tensor_tensor(two(acc[0], p), two(acc[0], p), two(acc[1], p), ALU.add).then_inc(merged, 1)

            def negated_mean(u):
                def step(p):
                    v.wait_ge(summed_up, p + (u * NPAIR + 1))
                    v.tensor_scalar(less_mean[:, ds(p * 2, 2)], feature_sums[:], -1.0 / D, None,
                                    ALU.mult).then_inc(mean_made, 1)
                return step

            def scale(u):
                def step(p):
                    v.wait_ge(sd_made, p + (u * NPAIR + 1))
                    v.reciprocal(rstd[:, ds(p * 2, 2)], sd[:, ds(p * 2, 2)]).then_inc(rstd_made, 1)
                    v.wait_ge(rstd_made, p + (u * NPAIR + 1))
                    v.scalar_tensor_tensor(out=shift[:, ds(p * 2, 2)], in0=less_mean[:, ds(p * 2, 2)], scalar=1.0,
                                           in1=rstd[:, ds(p * 2, 2)], op0=ALU.mult,
                                           op1=ALU.mult).then_inc(scale_made, 1)
                return step

            def residual(p):
                v.wait_ge(relued, p + 1)
                for a in range(2):
                    t = p * 2 + a
                    ins = v.scalar_tensor_tensor(out=one(acc[0], t), in0=one(acc[0], t), scalar=1.0,
                                                 in1=one(feat, t), op0=ALU.mult, op1=ALU.add,
                                                 accum_out=feature_sums[:, a:a + 1])
                ins.then_inc(summed_up, 1)

            def relu_scaled(p):
                v.wait_ge(merged, p + 1)
                for a in range(2):
                    ins = v.tensor_scalar(one(acc[0], p * 2 + a), one(acc[0], p * 2 + a),
                                          dinv[:, ds(p * 2 + a, 1)], 0.0, ALU.mult, ALU.max)
                ins.then_inc(relued, 1)

            def q_out(p):
                for a in range(2):
                    v.wait_ge(projected, p * 2 + (Q * NT + a + 3))
                    v.tensor_tensor(one(acc[0], p * 2 + a), ps[:, 2 + a, 0:D], bias(1),
                                    ALU.add).then_inc(evacuated, 1)

            pipeline(v, [(0, scale(0)), (3, merge), (-2, q_out), (3, relu_scaled), (2, residual), (2, negated_mean(0))])
            v.wait_ge(evacuated, 2 + (Q + 1) * NT)
            evacuate(K, lambda a, at: v.tensor_tensor(at(aux), ps[:, 2 + a, 0:D], bias(3), ALU.add))

            def scores(i, half):
                for q in range(4):
                    slot = half * GRP + 2 * q
                    for n in range(2):
                        v.wait_ge(got[slot + n], i * 16 + (ITER * 16 + 16))
                    v.wait_ge(k_ready, i * 8 + (4 + half * 4 + q + 1))
                    v.wait_ge(scored, i * 8 + (half * 4 + q + 4))
                    chain_at = i * 8 + (half * 4 + q + 1)
                    v.tensor_tensor(prod[:, q % 2, :].rearrange("p (a b) -> p a b", a=2),
                                    ps[:, 2 + q, :].rearrange("p (a b) -> p a b", a=2),
                                    ring[:, slot:slot + 2, 0:D],
                                    ALU.mult).then_inc(prod_ready, 1)
                    v.wait_ge(prod_ready, chain_at)
                    v.tensor_reduce(score[:, bass.ds(i * RING + slot, 2), :].rearrange("p a h -> p (a h)"),
                                    prod[:, q % 2, :].rearrange("p (g d) -> p g d", d=HD), X_AXIS,
                                    ALU.add).then_inc(scored, 1)

            mask_loop(SCORE, maskT_full[SCORE], 2, 1, scores)
            v.wait_ge(scored, 5 + NW // 2)
            v.wait_ge(v_stored, 16 * NT)
            v.wait_ge(block_out, 2 * NB)
            flat = lambda t: t.rearrange("p g e -> p (g e)")

            def row_maxima(values):
                link(v.tensor_tensor_scan(flat(runT), starts[:, 0:NB * P], flat(values), -BIG, ALU.add, ALU.max))
                link(v.tensor_tensor_scan(flat(runT)[:, ::-1], starts[:, 1:][:, ::-1], flat(runT)[:, ::-1], -BIG,
                                          ALU.add, ALU.max))

            row_maxima(turnedT)
            spread_ends(runT, 2)
            link(v.tensor_tensor(carry[:, 0, :], joined[:, 0:NW], one_seg[:], ALU.add))
            link(v.tensor_tensor(carry[:, 1, :], joined[:, 1:], one_seg[:], ALU.add))
            link(v.tensor_tensor_scan(carried[:, 0, :], carry[:, 0, :], last, -BIG, ALU.add, ALU.max))
            link(v.tensor_copy(carry[:, 0, :], first))
            link(v.tensor_tensor_scan(carried[:, 1, ::-1], carry[:, 1, ::-1], carry[:, 0, ::-1], -BIG,
                                      ALU.add, ALU.max))
            link(v.memset(carry, -BIG))
            link(v.tensor_tensor(carry[:, 0, 1:NW], carried[:, 0, 0:NW - 1], joined[:, 1:NW], ALU.add))
            link(v.tensor_tensor(carry[:, 1, 0:NW - 1], carried[:, 1, 1:NW], joined[:, 1:NW], ALU.add))
            for side in range(2):
                ins = v.tensor_tensor(placed[:, side, :, :], lane[:].unsqueeze(1).to_broadcast([P, NB, 32]),
                                      carry[:, side, :].rearrange("p (b n) -> p b n", n=32), ALU.mult)
            link(ins)
            link(v.tensor_reduce(carry_in.rearrange("p s b -> p (s b)"),
                                 placed.rearrange("p s b n -> p (s b) n"), X_AXIS, ALU.add))
            for side, e in enumerate((0, P - 1)):
                ins = v.tensor_tensor(runT[:, :, e], runT[:, :, e], carry_in[:, side, :], ALU.max)
            link(ins)
            row_maxima(runT)
            link(v.tensor_tensor(turnedT, turnedT, runT, ALU.subtract))
            v.sem_inc(less_m, 1)
            link(v.tensor_tensor(wgate_bc[:, 0:D], wgate_bc[:, 0:D], wgate_bc[:, 2 * D:3 * D], ALU.add))
            for n, row in enumerate((w_sb[:, 0, 4 * D:5 * D], w_sb[:, 1, 4 * D:5 * D], bias(4))):
                link(v.tensor_tensor(prod[:, 0, 0:D], row, wgate_bc[:, 0:D], ALU.mult))
                link(v.tensor_reduce(skip_gate[:, n:n + 1], prod[:, 0, 0:D], X_AXIS, ALU.add))
            v.sem_inc(skip_gate_ready, 1)
            link(v.memset(acc[0][:], 0.0))
            v.wait_ge(block_out, 3 * NB)
            link(v.memset(acc[1][:], 0.0))
            link(v.tensor_tensor(wgate_bc[:, D:2 * D], wgate_bc[:, D:2 * D], wgate_bc[:, 2 * D:3 * D],
                                 ALU.subtract))
            link(v.tensor_scalar(less_slope[:], scal_bc[:, 0:1], -1.0, None, ALU.mult))

            def attend(i, half):
                at = i * RING + half * GRP
                for n in range(GRP):
                    v.wait_ge(got[half * GRP + n], i * 16 + (2 * ITER * 16 + 16))
                    if n == 0:
                        v.tensor_copy(ring[:, half * GRP:(half + 1) * GRP, D:D + H],
                                      score[:, bass.ds(at, GRP), :])
                    if n % 2 == 1:
                        slot = half * GRP + n - 1
                        rows = ring[:, slot:slot + 2, 0:D].rearrange("p w (h d) -> p w h d", d=HD)
                        v.tensor_tensor(rows, rows,
                                        score[:, bass.ds(i * RING + slot, 2), :].unsqueeze(3)
                                        .to_broadcast([P, 2, H, HD]), ALU.mult).then_inc(ev_ready, 1)
                add_group(ATT, i, half, D + H, RING, 4, lambda j: 4 + j % 4)

            v.sem_inc(added[ATT], 4)
            mask_loop(ATT, summed[ATT], GRP, 2 * GRP, attend)
            v.wait_ge(added[ATT], 4 + NW)
            v.wait_ge(evacuated, 2 + (SKIP + 1) * NT)
            dens = [a[:, :, D:D + H] for a in acc]
            link(v.tensor_tensor(den4[:], dens[0], dens[1], ALU.add))
            v.sem_inc(dens_ready, 1)
            link(v.tensor_scalar(den4[:], den4[:], 1e-30, None, ALU.max))
            link(v.reciprocal(den4[:], den4[:]))

            def gate_logit(p):
                v.wait_ge(agg_merged, p + 1)
                rows = two(acc[0], p).rearrange("p t (h d) -> p t h d", d=HD)
                v.tensor_tensor(rows, rows, den4[:, ds(p * 2, 2), :].unsqueeze(3).to_broadcast([P, 2, H, HD]),
                                ALU.mult).then_inc(agg_made, 1)
                v.wait_ge(agg_made, p + 1)
                for a in range(2):
                    ins = v.scalar_tensor_tensor(out=prod[:, a, 0:D], in0=one(acc[0], p * 2 + a), scalar=1.0,
                                                 in1=wgate_bc[:, D:2 * D], op0=ALU.mult, op1=ALU.mult,
                                                 accum_out=agg_logit[:, a:a + 1])
                ins.then_inc(logits_made, 1)
                v.wait_ge(logits_made, p + 1)
                v.tensor_tensor(two(aux, p), two(aux, p), two(acc[0], p), ALU.subtract).then_inc(differed, 1)
                v.tensor_tensor(gate[:, ds(p * 2, 2)], agg_logit[:], skip_logit[:, ds(p * 2, 2)],
                                ALU.add).then_inc(gate_in_made, 1)

            def mix(p):
                v.wait_ge(mean_made, p + NPAIR)
                for a in range(2):
                    t = p * 2 + a
                    ins = v.scalar_tensor_tensor(out=one(acc[0], t), in0=one(aux, t), scalar=gate[:, ds(t, 1)],
                                                 in1=one(acc[0], t), op0=ALU.mult, op1=ALU.add,
                                                 accum_out=feature_sums[:, a:a + 1])
                ins.then_inc(summed_up, 1)

            with v.Fori(0, NPAIR) as p:
                gate_logit(p)
            v.wait_ge(gate_made, 1)
            v.wait_ge(differed, NPAIR)
            pipeline(v, [(0, scale(1)), (3, mix), (3, negated_mean(1))])

            def weight(p):
                v.wait_ge(normed, p + 1)
                v.tensor_tensor(two(acc[0], p), two(acc[0], p),
                                bias(5).unsqueeze(1).to_broadcast([P, 2, D]), ALU.mult).then_inc(weighted, 1)

            def rectify(p):
                v.wait_ge(negated, p + 1)
                v.wait_ge(mean_made, p + 2 * NPAIR)
                v.scalar_tensor_tensor(out=two(acc[0], p), in0=two(acc[0], p), scalar=0.0, in1=two(feat, p),
                                       op0=ALU.max, op1=ALU.add).then_inc(rectified, 1)
                v.wait_ge(rectified, p + 1)
                for a in range(2):
                    t = p * 2 + a
                    ins = v.scalar_tensor_tensor(out=one(acc[0], t), in0=one(aux, t), scalar=less_slope[:, 0:1],
                                                 in1=one(acc[0], t), op0=ALU.mult, op1=ALU.add,
                                                 accum_out=feature_sums[:, a:a + 1])
                ins.then_inc(summed_up, 1)

            def l2_out(p):
                for a in range(2):
                    v.wait_ge(projected, p * 2 + (L2P * NT + a + 3))
                    v.tensor_copy(acc[0][:, ds(p * 2 + a, 1), :].rearrange("p a b -> p (a b)"),
                                  ps[:, 2 + a, 0:AW]).then_inc(evacuated, 1)

            pipeline(v, [(0, scale(2)), (6, weight), (-2, l2_out), (2, rectify), (2, negated_mean(2))])
            v.wait_ge(kept, 2 + 2 * NT)
            v.wait_ge(l2_got, 2 * USED * 16)
            link(v.memset(acc[1][:, USED:, :], 0.0))
            link(v.memset(ral[:, USED:, :], 0.0))
            link(v.tensor_tensor(ral[:], ral[:], acc[1][:, :, D:D + H], ALU.add))
            link(v.tensor_scalar(alpha[:], ral[:], 0.0, 0.01, ALU.min, ALU.mult))
            link(v.scalar_tensor_tensor(out=ral[:], in0=ral[:], scalar=0.0, in1=alpha[:], op0=ALU.max, op1=ALU.add))
            link(v.tensor_reduce(small[:, 3, :], ral[:], X_AXIS, ALU.max))
            link(v.tensor_tensor(ral[:], ral[:], per_node(small[:, 3, :], H), ALU.subtract))
            v.sem_inc(l2_logits, 1)
            v.wait_ge(l2_exps, 1)
            link(v.tensor_reduce(small[:, 3, :], alpha[:], X_AXIS, ALU.add))
            link(v.reciprocal(small[:, 3, :], small[:, 3, :]))
            link(v.tensor_tensor(alpha[:], alpha[:], per_node(small[:, 3, :], H), ALU.mult))
            link(v.tensor_tensor(bias(7), bias(7), bias(8), ALU.add))
            v.wait_ge(l2_stored, 16 * (NPAIR + 1))
            link(v.memset(acc[0][:, :, D:SW], 1.0))

            def attend_heads(p):
                rows = two(acc[1], p).rearrange("p t (h d) -> p t h d", d=HD)
                v.tensor_tensor(rows, rows, alpha[:, ds(p * 2, 2), :].unsqueeze(3).to_broadcast([P, 2, H, HD]),
                                ALU.mult).then_inc(attended, 1)
                v.wait_ge(attended, p + 1)
                v.wait_ge(mean_made, p + 3 * NPAIR)
                v.tensor_tensor(two_heads, acc[1][:, ds(p * 2, 2), 0:D // 2], acc[1][:, ds(p * 2, 2), D // 2:D],
                                ALU.add).then_inc(heads_summed, 1)
                v.wait_ge(heads_summed, p * 2 + 1)
                v.tensor_tensor(head_sum, two_heads[:, :, 0:HD], two_heads[:, :, HD:2 * HD],
                                ALU.add).then_inc(heads_summed, 1)
                v.wait_ge(heads_summed, p * 2 + 2)
                for a in range(2):
                    t = p * 2 + a
                    heads = lambda x: one(x, t).rearrange("p (h d) -> p h d", d=HD)
                    ins = v.scalar_tensor_tensor(out=heads(aux), in0=heads(feat), scalar=1.0,
                                                 in1=head_sum[:, a, :].unsqueeze(1).to_broadcast([P, H, HD]),
                                                 op0=ALU.mult, op1=ALU.add, accum_out=feature_sums[:, a:a + 1])
                ins.then_inc(summed_up, 1)

            def root_out(p):
                for a in range(2):
                    v.wait_ge(projected, p * 2 + (L3P * NT + a + 3))
                    v.tensor_tensor(one(aux, p * 2 + a), ps[:, 4 + a, 0:D], bias(7),
                                    ALU.add).then_inc(evacuated, 1)

            pipeline(v, [(0, scale(3)), (-2, root_out), (3, attend_heads), (3, negated_mean(3))])
            v.wait_ge(kept, 2 + 3 * NT)
            v.wait_ge(y3_out, 2 + NT)
            link(v.memset(srcf[:, NW:], 0.0))
            link(v.tensor_copy(srcf[:, 0:NW], srcT[:]))
            v.sem_inc(y3_ready, 1)
            v.sem_inc(srcf_ready, 1)
            v.wait_ge(tri_ready, 1)
            shape3 = [P, GRP, P]

            def make_same(side, at):
                v.tensor_tensor(same, src_row[:, side, :, :], srcf[:, at].unsqueeze(2).to_broadcast(shape3),
                                ALU.is_equal).then_inc(same_made, 1)

            v.wait_ge(row_in[0], 16)
            make_same(0, slice(0, GRP))
            v.wait_ge(same_made, 1)
            v.tensor_tensor(earlier, same, before_tri.unsqueeze(1).to_broadcast(shape3),
                            ALU.mult).then_inc(same_ready, 1)

            def spread(i, half):
                v.wait_ge(dup_full, i * 2 + (half + 2))
                v.wait_ge(row_in[1 - half], i * 16 + 16 * (half + 1))
                make_same(1 - half, bass.ds(i * RING + (half + 1) * GRP, GRP))
                at = bass.ds(i * RING + half * GRP, GRP)
                v.tensor_scalar(to_spare, srcf[:, at], -1.0, spare_row[:, 0:1], ALU.mult,
                                ALU.add).then_inc(idx_steps, 1)
                v.wait_ge(idx_steps, i * 4 + (half * 2 + 1))
                v.scalar_tensor_tensor(out=to_spare2, in0=ps[:, 6, 0:GRP], scalar=0.5, in1=to_spare,
                                       op0=ALU.is_gt, op1=ALU.mult).then_inc(idx_steps, 1)
                v.wait_ge(same_made, i * 2 + (half + 2))
                v.tensor_tensor(earlier, same, before_tri.unsqueeze(1).to_broadcast(shape3),
                                ALU.mult).then_inc(same_ready, 1)
                v.wait_ge(idx_steps, i * 4 + (half * 2 + 2))
                v.wait_ge(group_in, i * 2 + (half + 1))
                v.tensor_tensor(idx_stage[:, half, :], srcf[:, at], to_spare2, ALU.add).then_inc(idx_ready, 1)

            v.sem_inc(idx_ready, 1)
            mask_loop(SPREAD, dup_full, 1, 1, spread)
            link(v.tensor_tensor(aux[:], aux[:], feat[:], ALU.add))
            for c, (first, last) in enumerate(CHUNKS):
                nodes = slice(first, last)
                v.wait_ge(read_back[c], 16 * TABLES)
                total = chunk_of(0, c)[:, :, 0:SW]
                for n in range(1, TABLES):
                    link(v.tensor_tensor(total, total, chunk_of(n, c)[:, :, 0:SW], ALU.add))
                v.sem_inc(chunk_used, 1)
                link(v.tensor_scalar(rcnt[:, nodes], total[:, :, D], 1.0, None, ALU.max))
                link(v.reciprocal(rcnt[:, nodes], rcnt[:, nodes]))
                mean = total[:, :, 0:D]
                for t in range(first, last):
                    ins = v.scalar_tensor_tensor(out=mean[:, t - first, :], in0=mean[:, t - first, :],
                                                 scalar=rcnt[:, t:t + 1], in1=aux[:, t, :], op0=ALU.mult,
                                                 op1=ALU.add)
                link(ins)
                layernorm(mean, feat[:, nodes, :], last - first)
                v.sem_inc(out_ready, 1)
                v.sem_inc(chunk_used, 1)


def kernel(**inputs):
    import numpy as np
    import concourse.bacc as bacc
    from concourse.bass_utils import run_bass_kernel_spmd

    f = {k: np.asarray(v) for k, v in inputs.items()}
    rows = np.zeros((ROWS * P, 2), np.int32)
    rows[:, 1] = PAD_DST
    rows[:E, 0], rows[:E, 1] = f["src"], f["dst"]
    cols = np.zeros((P, 2, NW), np.int32)
    cols[:, 1, :] = PAD_DST
    cols[:, :, :ROWS] = rows.reshape(ROWS, P, 2).transpose(1, 2, 0)
    w_all = np.concatenate([f["L0_gnn_W"], f["L1_gnn_Wq"].T, f["L1_gnn_Wv"].T, f["L1_gnn_Wk"].T,
                            f["L1_gnn_Wskip"].T, f["L3_gnn_W2"].T, f["L3_gnn_W1"].T], axis=1)
    bias = np.concatenate([f[n] for n in ("L0_gnn_b", "L1_gnn_bq", "L1_gnn_bv", "L1_gnn_bk", "L1_gnn_bskip",
                                          "L1_gnn_ln_w", "L1_gnn_ln_b", "L3_gnn_b1", "L3_gnn_b2")])
    arrays = {
        "x": f["x"], "edges": rows.reshape(ROWS, 2 * P), "edges_t": cols, "w_all": w_all, "w_l2": f["L2_gnn_weight"],
        "bias": bias,
        "attn": np.concatenate([f["L2_gnn_attn_l"].reshape(-1), f["L2_gnn_attn_r"].reshape(-1)]),
        "wgate": f["L1_gnn_Wgate"].reshape(-1),
        "scalars": np.concatenate([f["L1_gnn_prelu_a"].reshape(1), f["L1_gnn_bgate"].reshape(1)]),
    }
    arrays = {k: np.ascontiguousarray(a) for k, a in arrays.items()}
    nc = bacc.Bacc("TRN2", target_bir_lowering=False, num_devices=1)
    aps = [nc.dram_tensor(k, a.shape, mybir.dt.from_np(a.dtype), kind="ExternalInput").ap()
           for k, a in arrays.items()]
    out = nc.dram_tensor("out", (N, D), F32, kind="ExternalOutput").ap()
    gnn_kernel(nc, *aps, out)
    return run_bass_kernel_spmd(nc, [arrays], core_ids=[0]).results[0]["out"]
```
